# Optimizing a Trainium2 kernel written in Bass

```python
import numpy as np
import jax
import jax.numpy as jnp

def _softmax(x, axis=-1):
    return jax.nn.softmax(x, axis=axis)

def _gelu(x):
    return jax.nn.gelu(x, approximate=True)

def _silu(x):
    return jax.nn.silu(x)

def _sigmoid(x):
    return jax.nn.sigmoid(x)

def _layernorm(x, axis=-1, eps=1e-05):
    m = jnp.mean(x, axis=axis, keepdims=True)
    v = jnp.var(x, axis=axis, keepdims=True)
    return (x - m) / jnp.sqrt(v + eps)

def _scatter_add(tgt, idx, src, axis=0):
    return tgt.at[idx].add(src)

def _segment_sum(src, seg, n):
    return jax.ops.segment_sum(src, seg, n)
kernel_name = 'mk_adaln_d1_jaxref_r8_f5c877'

def setup_inputs(seed: int=0):
    np.random.seed(seed)
    _w = jnp.asarray

    def _L0_attn_setup():
        import jax, jax.numpy as jnp
        import numpy as np
        B, T, C = (4, 256, 128)
        H, D = (16, 64)
        MAX_REL = 16
        NUM_BUCKETS = 2 * MAX_REL + 1
        key = jax.random.key(seed)
        ks = jax.random.split(key, 7)
        x = jax.random.normal(ks[0], (B, T, C), dtype=jnp.float32)
        Wq = jax.random.normal(ks[1], (H, C, D), dtype=jnp.float32) * 0.02
        Wk = jax.random.normal(ks[2], (H, C, D), dtype=jnp.float32) * 0.02
        Wv = jax.random.normal(ks[3], (H, C, D), dtype=jnp.float32) * 0.02
        Wp = jax.random.normal(ks[4], (H * D, C), dtype=jnp.float32) * 0.02
        bp = jnp.zeros((C,), dtype=jnp.float32)
        rel_table = jax.random.normal(ks[5], (NUM_BUCKETS, H), dtype=jnp.float32) * 0.02
        return {'x': x, 'Wq': Wq, 'Wk': Wk, 'Wv': Wv, 'Wp': Wp, 'bp': bp, 'rel_table': rel_table}
    _L0_attn_in = _L0_attn_setup()

    def _L0_ffn_setup():
        import math
        import jax, jax.numpy as jnp
        import numpy as np
        E = 8
        TOPK = 2
        CF = 1.25
        EPS = 1e-05
        NEG = -1e+30

        def _layer_norm(x, gamma, beta):
            mu = jnp.mean(x, axis=-1, keepdims=True)
            var = jnp.mean((x - mu) ** 2, axis=-1, keepdims=True)
            return (x - mu) * jax.lax.rsqrt(var + EPS) * gamma + beta
        key = jax.random.key(seed)
        ks = jax.random.split(key, 8)
        B, S, H, F = (4, 256, 128, 512)
        hidden_states = jax.random.normal(ks[0], (B, S, H), jnp.float32)
        token_mask = jnp.ones((B, S), jnp.int32)
        Wr = jax.random.normal(ks[1], (H, E), jnp.float32) * 0.001
        br = jnp.zeros((E,), jnp.float32)
        W1 = jax.random.normal(ks[2], (E, H, F), jnp.float32) * (1.0 / np.sqrt(H))
        b1 = jax.random.normal(ks[3], (E, F), jnp.float32) * 0.01
        W2 = jax.random.normal(ks[4], (E, F, H), jnp.float32) * (1.0 / np.sqrt(F))
        b2 = jax.random.normal(ks[5], (E, H), jnp.float32) * 0.01
        gamma = jnp.ones((H,), jnp.float32)
        beta = jnp.zeros((H,), jnp.float32)
        return {'hidden_states': hidden_states, 'Wr': Wr, 'br': br, 'W1': W1, 'b1': b1, 'W2': W2, 'b2': b2, 'gamma': gamma, 'beta': beta, 'token_mask': token_mask}
    _L0_ffn_in = _L0_ffn_setup()
    _L0_c = _w((lambda *s: np.random.randn(*s).astype(np.float32) * 0.05)(8, 128))
    _L0_wmod = _w((lambda *s: np.random.randn(*s).astype(np.float32) * 0.05)(128, 6 * 128) * 128 ** (-0.5))
    _d = {'L0_attn_x': _L0_attn_in['x'], 'L0_attn_Wq': _L0_attn_in['Wq'], 'L0_attn_Wk': _L0_attn_in['Wk'], 'L0_attn_Wv': _L0_attn_in['Wv'], 'L0_attn_Wp': _L0_attn_in['Wp'], 'L0_attn_bp': _L0_attn_in['bp'], 'L0_attn_rel_table': _L0_attn_in['rel_table'], 'L0_ffn_Wr': _L0_ffn_in['Wr'], 'L0_ffn_br': _L0_ffn_in['br'], 'L0_ffn_W1': _L0_ffn_in['W1'], 'L0_ffn_b1': _L0_ffn_in['b1'], 'L0_ffn_W2': _L0_ffn_in['W2'], 'L0_ffn_b2': _L0_ffn_in['b2'], 'L0_ffn_gamma': _L0_ffn_in['gamma'], 'L0_ffn_beta': _L0_ffn_in['beta'], 'L0_ffn_token_mask': _L0_ffn_in['token_mask'], 'L0_c': _L0_c, 'L0_wmod': _L0_wmod}
    _x0 = _d['L0_attn_x']
    _d['L0_attn_x'] = jax.random.normal(jax.random.fold_in(jax.random.key(seed), 1), (8, 256, 128), dtype=_x0.dtype)
    del _x0
    return _d

def reference(L0_attn_x, L0_attn_Wq, L0_attn_Wk, L0_attn_Wv, L0_attn_Wp, L0_attn_bp, L0_attn_rel_table, L0_ffn_Wr, L0_ffn_br, L0_ffn_W1, L0_ffn_b1, L0_ffn_W2, L0_ffn_b2, L0_ffn_gamma, L0_ffn_beta, L0_ffn_token_mask, L0_c, L0_wmod):

    def _L0_attn_ref(x, Wq, Wk, Wv, Wp, bp, rel_table):
        import jax, jax.numpy as jnp
        import numpy as np
        B, T, C = (4, 256, 128)
        H, D = (16, 64)
        MAX_REL = 16
        NUM_BUCKETS = 2 * MAX_REL + 1
        Tq = x.shape[1]
        pos = jnp.arange(Tq)
        rel = pos[None, :] - pos[:, None]
        idx = jnp.clip(rel + MAX_REL, 0, NUM_BUCKETS - 1)
        bias = rel_table[idx]
        bias = jnp.transpose(bias, (2, 0, 1))
        q = jnp.einsum('btc,hcd->bhtd', x, Wq)
        k = jnp.einsum('btc,hcd->bhtd', x, Wk)
        v = jnp.einsum('btc,hcd->bhtd', x, Wv)
        scale = 1.0 / jnp.sqrt(jnp.float32(D))
        scores = jnp.einsum('bhtd,bhsd->bhts', q, k) * scale + bias[None]
        causal = jnp.tril(jnp.ones((Tq, Tq), dtype=bool))
        scores = jnp.where(causal[None, None], scores, jnp.float32(-jnp.inf))
        w = jax.nn.softmax(scores, axis=-1)
        out = jnp.einsum('bhts,bhsd->bhtd', w, v)
        out = jnp.transpose(out, (0, 2, 1, 3)).reshape(x.shape[0], Tq, H * D)
        return out @ Wp + bp

    def _L0_ffn_ref(hidden_states, Wr, br, W1, b1, W2, b2, gamma, beta, token_mask):
        import math
        import jax, jax.numpy as jnp
        import numpy as np
        E = 8
        TOPK = 2
        CF = 1.25
        EPS = 1e-05
        NEG = -1e+30

        def _layer_norm(x, gamma, beta):
            mu = jnp.mean(x, axis=-1, keepdims=True)
            var = jnp.mean((x - mu) ** 2, axis=-1, keepdims=True)
            return (x - mu) * jax.lax.rsqrt(var + EPS) * gamma + beta
        B, S, H = hidden_states.shape
        x = hidden_states.reshape(-1, H)
        N = x.shape[0]
        logits = x @ Wr + br
        top_vals, top_idx = jax.lax.top_k(logits, TOPK)
        w = jax.nn.softmax(top_vals, axis=-1)
        flat_idx = top_idx.reshape(-1)
        flat_tok = jnp.repeat(jnp.arange(N), TOPK)
        w_flat = w.reshape(-1)
        cap = max(int(math.ceil(N / E * CF)), 1)
        key_mat = jnp.where(flat_idx[None, :] == jnp.arange(E)[:, None], w_flat[None, :], NEG)
        kv, ki = jax.lax.top_k(key_mat, cap)
        valid = kv > NEG / 2
        tok = flat_tok[ki]
        gate = jnp.where(valid, w_flat[ki], 0.0)
        xe = x[tok]
        h1 = jnp.einsum('ech,ehf->ecf', xe, W1) + b1[:, None, :]
        h1 = jax.nn.gelu(h1, approximate=False)
        y = jnp.einsum('ecf,efh->ech', h1, W2) + b2[:, None, :]
        out = jnp.zeros_like(x).at[tok.reshape(-1)].add((y * gate[..., None]).reshape(-1, H))
        out = out.reshape(B, S, H) + hidden_states
        return _layer_norm(out, gamma, beta)
    x = L0_attn_x
    mod = (_silu(L0_c) @ L0_wmod).reshape(L0_c.shape[0], 6, 1, -1)
    sa, ca, ga, sb, cb, gb = (mod[:, 0], mod[:, 1], mod[:, 2], mod[:, 3], mod[:, 4], mod[:, 5])
    ga = (2 * (ga >= 0) - 1) * jnp.maximum(jnp.abs(ga), 0.25)
    gb = (2 * (gb >= 0) - 1) * jnp.maximum(jnp.abs(gb), 0.25)
    h = _layernorm(x, axis=-1) * (1 + ca) + sa
    x = x + ga * _L0_attn_ref(h, L0_attn_Wq, L0_attn_Wk, L0_attn_Wv, L0_attn_Wp, L0_attn_bp, L0_attn_rel_table)
    h = _layernorm(x, axis=-1) * (1 + cb) + sb
    x = x + gb * _L0_ffn_ref(h, L0_ffn_Wr, L0_ffn_br, L0_ffn_W1, L0_ffn_b1, L0_ffn_W2, L0_ffn_b2, L0_ffn_gamma, L0_ffn_beta, L0_ffn_token_mask)
    return x

_drawn_inputs = setup_inputs


def setup_inputs(seed=0):
    import zlib

    import numpy as np

    out = dict(_drawn_inputs(seed))
    spreads = {'L0_attn_bp': (0.0, 0.311),
     'L0_ffn_br': (0.0, 0.1),
     'L0_ffn_gamma': (1.0, 0.2),
     'L0_ffn_beta': (0.0, 0.31)}
    factors = {'L0_attn_Wq': 8.0,
     'L0_attn_Wk': 8.0,
     'L0_attn_Wv': 8.0,
     'L0_attn_Wp': 8.0,
     'L0_attn_rel_table': 8.0,
     'L0_ffn_b1': 64.0,
     'L0_ffn_b2': 64.0}
    for name, (base, spread) in spreads.items():
        noise = np.random.default_rng([zlib.crc32(name.encode()), seed]).standard_normal(out[name].shape)
        drawn = base * np.exp(spread * noise) if base else spread * noise
        out[name] = jnp.asarray(drawn.astype(out[name].dtype))
    for name, factor in factors.items():
        out[name] = (out[name] * factor).astype(out[name].dtype)
    return out
```

```python
import concourse.bass as bass
from concourse import mybir
from contextlib import ExitStack


def adaln_attention_moe_kernel(nc, x, Wq, Wk, Wv, Wp, bp, rel_table, Wr, br, W1, b1, W2, b2,
                               gamma, beta, c, wmod, out):
    f32 = mybir.dt.float32
    bf16 = mybir.dt.bfloat16
    i32 = mybir.dt.int32
    ALU = mybir.AluOpType
    ACT = mybir.ActivationFunctionType
    X = mybir.AxisListType.X

    B, T, C = x.shape
    H, _, D = Wq.shape
    E, _, F = W1.shape
    P = 128
    REL = 16
    NT = B * T // P
    TPB = T // P
    assert (T, C, D, H, TPB) == (256, P, 64, 16, 2)
    CAP = -(-B * T * 5 // (4 * E))
    SLOTS = E * CAP
    TRASH = SLOTS
    HG = 4
    NHG = H // HG
    GROUPS = B * NHG
    UNROLL = 2 * NHG
    FT = F // P
    EPS = 1e-5
    NEG = -1e30
    SCALE = float(D) ** -0.5
    BAND = P + T - 1
    BITS = 30
    ROUNDS = BITS // 2
    MODS = 6
    SA, CA, GA, SB, CB, GB = range(MODS)

    ctx = ExitStack()
    with ctx:
        def sb(name, shape, dt=f32):
            return ctx.enter_context(nc.sbuf_tensor(name, shape, dt))

        def sem(name):
            return ctx.enter_context(nc.semaphore(name))

        band_dram = nc.dram_tensor("band_dram", [H, P, BAND], f32, kind="Internal").ap()
        xe_dram = nc.dram_tensor("xe_dram", [SLOTS, C], f32, kind="Internal").ap()
        ye_dram = nc.dram_tensor("ye_dram", [SLOTS + 1, C], f32, kind="Internal").ap()

        ident = sb("ident", [P, P])
        xr = sb("xr", [P, NT, C])
        hn = sb("hn", [P, NT, C])
        wqkv = sb("wqkv", [P, 3, H, D])
        wp_sb = sb("wp_sb", [P, H // 2, C])
        wT = sb("wT", [P, 3, H // 2, C])
        A_sb = sb("A_sb", [P, H, C])
        G_sb = sb("G_sb", [P, H, C])
        bias_sb = sb("bias_sb", [P, H, T])
        mod = sb("mod", [P, B, MODS, C])
        h_cur = sb("h_cur", [P, 2, TPB, C])
        hT_cur = sb("hT_cur", [P, 2, T])
        kT = sb("kT", [P, 2, HG, T])
        S2 = sb("S2", [P, 2, HG, P + T])
        rowmin = sb("rowmin", [P, 2, 2 * HG])
        rowsum = sb("rowsum", [P, 2, 2 * HG])
        rowinv = sb("rowinv", [P, 2, 2 * HG])
        pT0 = sb("pT0", [P, 2, HG, T])
        pT1 = sb("pT1", [P, 2, HG, P])
        uT = sb("uT", [P, 2, HG, T])
        oT = sb("oT", [P, T])
        h2_cur = sb("h2_cur", [P, TPB, C])
        h2T = sb("h2T", [P, T])
        bp_bc = sb("bp_bc", [P, C])
        gamma_bc = sb("gamma_bc", [P, C])
        beta_bc = sb("beta_bc", [P, C])
        br_bc = sb("br_bc", [P, E])
        b2_bc = sb("b2_bc", [P, E, C])
        wr_sb = sb("wr_sb", [P, E])
        b1_sb = sb("b1_sb", [P, E, FT])
        band = sb("band", [H, BAND])
        tabT = sb("tabT", [H, 2 * REL + 1])
        cT = sb("cT", [P, B])
        silu = sb("silu", [P, 3, B])
        silu_bc = sb("silu_bc", [P, B, P])
        wmod_sb = sb("wmod_sb", [P, MODS * C])
        stats = sb("stats", [P, NT, 6])
        mv = sb("mv", [P, NT, 2])
        rstd = sb("rstd", [P, NT])
        stats2 = sb("stats2", [P, TPB, 6])
        mv2 = sb("mv2", [P, TPB, 2])
        rstd2 = sb("rstd2", [P, TPB])
        NEWTON = 3
        RSQRT_LINKS = 3 + 3 * NEWTON
        nwt = sb("nwt", [P, 3, NT])
        gtmp = sb("gtmp", [P, 2, TPB, C])
        lg = sb("lg", [P, NT, E])
        w1_sb = sb("w1_sb", [P, E, F])
        w2_sb = sb("w2_sb", [P, E, FT, C])

        rt = sb("rt", [P, 12, NT, E])
        LG2, OH1, OH2, SCORE, KEY, SEL, SLOT, MASKED, PREF, EQF, TMP, LOWFIRST = range(12)
        rv = sb("rv", [P, 12, NT])
        M1, M2, BEST, E1, W0, W1_, SL, SE, G1, G2, ONEP, SPARE = range(12)
        masks = sb("masks", [P, 2, NT, E], bf16)
        ones_bf = sb("ones_bf", [P, P], bf16)
        before_bf = sb("before_bf", [P, P], bf16)
        cand = sb("cand", [P, 4, E], i32)
        incs = sb("incs", [P, 3, E], i32)
        passing = sb("passing", [P, 3, E, NT], bf16)
        cnt_bf = sb("cnt_bf", [P, 3, E], bf16)
        best4 = sb("best4", [P, 4, E])
        slot_base = sb("slot_base", [P, NT, E])
        ngt = sb("ngt", [P, E])
        ngt_bf = sb("ngt_bf", [P, E], bf16)
        idx = sb("idx", [P, 2, NT], i32)

        y_got = [A_sb[:, :, :], G_sb[:, :, :]]
        xe_sb = bias_sb[:, :, :].rearrange("p h t -> p (h t)")[:, 0:SLOTS] \
            .rearrange("p (q t n) -> p q t n", q=E // 2, t=5)
        xeT = S2[:, :, :, :].rearrange("p r h t -> p (r h t)")[:, 0:SLOTS] \
            .rearrange("p (q n) -> p q n", q=E // 2)
        gT = wT[:, :, :, :].rearrange("p a h n -> p (a h n)")[:, 0:2 * FT * CAP] \
            .rearrange("p (r f n) -> p r f n", r=2, f=FT)
        y_sb = kT[:, :, :, :].rearrange("p a h n -> p (a h n)")[:, 0:2 * 3 * C] \
            .rearrange("p (r t n) -> p r t n", r=2, t=3)
        zeros = pT0[:, :, :, :].rearrange("p a h n -> p (a h n)")

        banks = ctx.enter_context(nc.psum_tensor("banks", [P, 8, 512], f32))
        KU, SP_, TP, OB, AUX = (0, 1), (2, 3), (4, 5), 6, 7

        ld_x, ld_w, ld_wp, ld_c, ld_mod, ld_tab, ld_small, ld_bias, st_band = (
            sem(n) for n in ("ld_x", "ld_w", "ld_wp", "ld_c", "ld_mod", "ld_tab", "ld_small",
                             "ld_bias", "st_band"))
        ld_w1, ld_w2 = sem("ld_w1"), sem("ld_w2")
        zero_set, zero_st = sem("zero_set"), sem("zero_st")
        id_set, id_made, band_made = sem("id_set"), sem("id_made"), sem("band_made")
        const_made = sem("const_made")
        silu_exp, silu_made = sem("silu_exp"), sem("silu_made")
        mod_ready, mod_copied = sem("mod_ready"), sem("mod_copied")
        wt_ready, wt_copied = sem("wt_ready"), sem("wt_copied")
        hn_made = sem("hn_made")
        hcur_made, hT_ready, hT_copied = sem("hcur_made"), sem("hT_ready"), sem("hT_copied")
        k_ready, k_copied = sem("k_ready"), sem("k_copied")
        s_ready, biased, expd, normed = sem("s_ready"), sem("biased"), sem("expd"), sem("normed")
        t_ready, t_copied = sem("t_ready"), sem("t_copied")
        u_ready, u_copied = sem("u_ready"), sem("u_copied")
        o_ready, oT_copied = sem("o_ready"), sem("oT_copied")
        oN_ready, h2_made = sem("oN_ready"), sem("h2_made")
        h2T_ready, h2T_copied = sem("h2T_ready"), sem("h2T_copied")
        lg_ready, lg_copied = sem("lg_ready"), sem("lg_copied")
        inv_made = sem("inv_made")
        dve_chain = sem("dve_chain")
        ln2_chain = sem("ln2_chain")
        pool_chain = sem("pool_chain")
        top_made, e1_made = sem("top_made"), sem("e1_made")
        search_chain, counted, count_ready = sem("search_chain"), sem("counted"), sem("count_ready")
        masks_made, prefix_ready = sem("masks_made"), sem("prefix_ready")
        sel_made, pos_ready = sem("sel_made"), sem("pos_ready")
        idx_made, scattered = sem("idx_made"), sem("scattered")
        ld_xe = [sem(f"ld_xe{q}") for q in range(E // 2)]
        x_ready, x_copied = sem("x_ready"), sem("x_copied")
        f_ready, gelu_done = sem("f_ready"), sem("gelu_done")
        y_ready, y_copied = sem("y_ready"), sem("y_copied")
        st_y = [sem(f"st_y{r}") for r in range(2)]
        gathered = sem("gathered")
        out_made, st_out = sem("out_made"), sem("st_out")

        block = ctx.enter_context(nc.Block())

        def both(ap):
            return ap.unsqueeze(1).to_broadcast([P, TPB, C])

        LAST = GROUPS + 4

        def heads_of(q):
            return slice(q % 2 + 8 * (q // 2 % 2), q % 2 + 8 * (q // 2 % 2) + 7, 2)

        wait_register = {}

        def reached(eng, value):
            if not isinstance(value, int):
                if eng not in wait_register:
                    wait_register[eng] = eng.alloc_register("reached")
                eng.reg_mov(wait_register[eng], value)
                value = wait_register[eng]
            eng.wait_ge(id_made, 1)
            return value

        def w_at(at):
            return at // NHG

        def has(at, lag):
            return 0 <= at - lag < GROUPS

        def attention(eng, step):
            for m in range(UNROLL):
                step(m, m, m // NHG)
            with eng.Fori(1, GROUPS // UNROLL) as i:
                for j in range(UNROLL):
                    step(UNROLL * i + j, UNROLL + j, 2 * i + j // NHG)
            for m in range(GROUPS, LAST + NHG):
                step(m, m, m // NHG)

        @block.sync
        def _(sp):
            sp.dma_start(cT[:, :], c.rearrange("b k -> k b"), allow_slow_non_contiguous=True).then_inc(ld_c, 16)
            sp.dma_start(wqkv[:, 0, :, :], Wq.rearrange("h c d -> c h d")).then_inc(ld_w, 16)
            sp.dma_start(wqkv[:, 1, :, :], Wk.rearrange("h c d -> c h d")).then_inc(ld_w, 16)
            sp.dma_start(wqkv[:, 2, :, :], Wv.rearrange("h c d -> c h d")).then_inc(ld_w, 16)
            sp.dma_start(wp_sb[:, :, :], Wp.rearrange("(g p) n -> p g n", p=P)).then_inc(ld_wp, 16)
            sp.wait_ge(band_made, 1)
            sp.dma_start(band_dram, band[:, :].unsqueeze(1).to_broadcast([H, P, BAND])).then_inc(st_band, 16)
            sp.wait_ge(st_band, 16)
            for h in range(H):
                sp.dma_start(bias_sb[:, h, :],
                             bass.AP(band_dram.tensor, h * P * BAND + P - 1, [[BAND - 1, P], [1, T]])
                             ).then_inc(ld_bias, 16)
            for dst, src in ((gamma_bc, gamma), (beta_bc, beta), (br_bc, br)):
                sp.dma_start(dst[:, :], src.partition_broadcast(P)).then_inc(ld_small, 16)
            sp.dma_start(b2_bc[:, :, :], b2.partition_broadcast(P)).then_inc(ld_small, 16)
            sp.dma_start(wr_sb[:, :], Wr).then_inc(ld_small, 16)
            sp.dma_start(b1_sb[:, :, :], b1.rearrange("e (f p) -> p e f", p=P), allow_slow_non_contiguous=True).then_inc(ld_small, 16)
            sp.wait_ge(zero_set, 1)
            sp.dma_start(xe_dram.rearrange("(p a) n -> p (a n)", p=P)[:, 0:2048], zeros
                         ).then_inc(zero_st, 16)
            sp.dma_start(xe_dram.rearrange("(p a) n -> p (a n)", p=P)[:, 2048:], zeros[:, 0:512]
                         ).then_inc(zero_st, 16)
            sp.dma_start(ye_dram[TRASH:TRASH + 1, :], zeros[0:1, 0:C]).then_inc(zero_st, 16)

            sp.dma_start(w1_sb[:, :, :], W1.rearrange("e c f -> c e f")).then_inc(ld_w1, 16)
            sp.dma_start(w2_sb[:, :, :, :], W2.rearrange("e (f p) c -> p e f c", p=P)).then_inc(ld_w2, 16)
            sp.wait_ge(scattered, 2 * NT * 16)
            for q in range(E // 2):
                sp.dma_start(xe_sb[:, q, :, :],
                             xe_dram[q * 5 * P:(q + 1) * 5 * P, :].rearrange("(t p) n -> p t n", p=P)
                             ).then_inc(ld_xe[q], 16)
            for e in range(E):
                sp.wait_ge(y_copied, 2 * e + 2)
                sp.dma_start(ye_dram[e * CAP:e * CAP + 2 * P, :].rearrange("(t p) n -> p t n", p=P),
                             y_sb[:, e % 2, 0:2, :]).then_inc(st_y[e % 2], 16)
                sp.dma_start(ye_dram[e * CAP + 2 * P:(e + 1) * CAP, :],
                             y_sb[0:CAP - 2 * P, e % 2, 2, :]).then_inc(st_y[e % 2], 16)
            for s in range(4):
                sp.wait_ge(out_made, s + 1)
                sp.dma_start(out.rearrange("b (t p) n -> p (b t) n", p=P)[:, 4 * s:4 * s + 4, :],
                             y_got[1][:, 4 * s:4 * s + 4, :]).then_inc(st_out, 16)
            sp.wait_ge(st_out, 64)

        @block.gpsimd
        def _(pool):
            nc.gpsimd.memset(ident[:, :], 0.0).then_inc(id_set, 1)
            nc.gpsimd.memset(ones_bf[:, :], 1.0).then_inc(const_made, 1)
            pool.wait_ge(id_set, 1)
            nc.gpsimd.affine_select(out=ident[:, :], in_=ident[:, :], compare_op=ALU.not_equal,
                                    fill=1.0, base=0, pattern=[[-1, P]], channel_multiplier=1
                                    ).then_inc(id_made, 1)
            nc.gpsimd.memset(zeros, 0.0).then_inc(zero_set, 1)
            pool.wait_ge(const_made, 1)
            nc.gpsimd.affine_select(out=before_bf[:, :], in_=ones_bf[:, :], compare_op=ALU.is_gt,
                                    fill=0.0, base=0, pattern=[[1, P]], channel_multiplier=-1
                                    ).then_inc(const_made, 1)
            nc.gpsimd.iota(slot_base[:, :, :], [[0, NT], [CAP, E]], base=-TRASH, channel_multiplier=0,
                           allow_small_or_imprecise_dtypes=True).then_inc(const_made, 1)
            nc.gpsimd.iota(rt[:, LOWFIRST, :, :], [[0, NT], [-1, E]], base=E, channel_multiplier=0,
                           allow_small_or_imprecise_dtypes=True).then_inc(const_made, 1)
            for j in range(3):
                nc.gpsimd.memset(incs[:, j, :], (j + 1) << (BITS - 2)).then_inc(const_made, 1)
            nc.gpsimd.memset(cand[:, 0, :], 0).then_inc(const_made, 1)

            def step(m, at, w):
                if has(at, 1):
                    n, r = m - 1, (at - 1) % 2
                    pool.wait_ge(inv_made, reached(pool, n + 1))
                    for k in range(2 * HG):
                        h, second = k % HG, k // HG
                        part = S2[:, r, h, P:P + T] if second else S2[:, r, h, 0:P]
                        nc.gpsimd.tensor_scalar(part, part, rowinv[:, r, k:k + 1], None,
                                                op0=ALU.mult).then_inc(normed, 1)
            attention(pool, step)

            pool.wait_ge(idx_made, 1)
            pool.wait_ge(zero_st, 48)
            for t in range(NT):
                for k in range(2):
                    nc.gpsimd.indirect_dma_start(
                        out=xe_dram, out_offset=bass.IndirectOffsetOnAxis(ap=idx[:, k, t:t + 1], axis=0),
                        in_=hn[:, t, :], in_offset=None, bounds_check=SLOTS - 1, oob_is_err=False
                    ).then_inc(scattered, 16)
            for r in range(2):
                pool.wait_ge(st_y[r], 16 * E)
            for t in range(NT):
                for k in range(2):
                    nc.gpsimd.indirect_dma_start(
                        out=y_got[k][:, t, :], out_offset=None, in_=ye_dram,
                        in_offset=bass.IndirectOffsetOnAxis(ap=idx[:, k, t:t + 1], axis=0),
                        bounds_check=SLOTS, oob_is_err=False
                    ).then_inc(gathered, 16)

        @block.scalar
        def _(act):
            act.dma_start(xr[:, :, :], x.rearrange("b (t p) n -> p (b t) n", p=P)).then_inc(ld_x, 16)
            act.dma_start(wmod_sb[:, :], wmod).then_inc(ld_mod, 16)
            act.dma_start(tabT[:, :], rel_table.rearrange("r h -> h r"), allow_slow_non_contiguous=True).then_inc(ld_tab, 16)
            act.dma_start(bp_bc[:, :], bp.partition_broadcast(P)).then_inc(ld_tab, 16)
            act.wait_ge(ld_c, 16)
            nc.scalar.activation(silu[:, 0, :], cT[:, :], ACT.Exp, scale=-1.0).then_inc(silu_exp, 1)
            for q in range(6 + 8):
                act.wait_ge(wt_ready, q + 1)
                src = banks[:, 4 + q % 4, :]
                if q < 6:
                    dst = wT[:, q // 2, 4 * (q % 2):4 * (q % 2) + 4, :].rearrange("p g n -> p (g n)")
                    nc.scalar.activation(dst, src, ACT.Copy).then_inc(wt_copied, 1)
                else:
                    dst = (A_sb, G_sb)[(q - 6) // 4][:, heads_of(q - 6), :]
                    nc.scalar.activation(dst, src.rearrange("p (g n) -> p g n", g=4), ACT.Copy,
                                         scale=SCALE if q < 10 else 1.0).then_inc(wt_copied, 1)

            def step(m, at, w):
                if has(at, 1):
                    n, r = m - 1, (at - 1) % 2
                    for k in range(2 * HG):
                        h, second = k % HG, k // HG
                        part = S2[:, r, h, P:P + T] if second else S2[:, r, h, 0:P]
                        act.wait_ge(biased, 2 * HG * n + k + 1)
                        nc.scalar.activation(part, part, ACT.Exp, scale=-1.0,
                                             bias=rowmin[:, r, k:k + 1],
                                             accum_out=rowsum[:, r, k:k + 1]).then_inc(expd, 1)
                if has(at, 0):
                    for k in range(2):
                        act.wait_ge(k_ready, 2 * m + k + 1)
                        if at >= 2:
                            act.wait_ge(s_ready, 3 * (m - 2) + 3)
                        nc.scalar.activation(
                            kT[:, at % 2, 2 * k:2 * k + 2, :].rearrange("p h t -> p (h t)"),
                            banks[:, KU[k], :], ACT.Copy).then_inc(k_copied, 1)
                if has(at, 4) and at % NHG == NHG - 1:
                    act.wait_ge(o_ready, m - 3)
                    if w_at(at) >= 2:
                        act.wait_ge(oN_ready, w - 1)
                    nc.scalar.activation(oT[:, :], banks[:, OB, 0:T], ACT.Copy).then_inc(oT_copied, 1)
            attention(act, step)

            act.wait_ge(top_made, 1)
            nc.scalar.activation(rv[:, E1, :], rv[:, SPARE, :], ACT.Exp).then_inc(e1_made, 1)
            for e in range(E):
                for f in range(FT):
                    act.wait_ge(f_ready, FT * e + f + 1)
                    if e >= 2:
                        act.wait_ge(y_ready, 2 * (e - 2) + 2)
                    nc.scalar.activation(gT[:, e % 2, f, :], banks[:, 2 + f, 0:CAP], ACT.Gelu,
                                         bias=b1_sb[:, e, f:f + 1]).then_inc(gelu_done, 1)

        @block.tensor
        def _(pe):
            mm, tr = nc.tensor.matmul, nc.tensor.transpose
            pe.wait_ge(id_made, 1)
            for q in range(6):
                if q % 2 == 0:
                    pe.wait_ge(ld_w, 16 * 3)
                if q >= 4:
                    pe.wait_ge(wt_copied, q - 3)
                for g in range(4):
                    gg = 4 * (q % 2) + g
                    last = tr(banks[:, 4 + q % 4, g * P:(g + 1) * P],
                              wqkv[:, q // 2, 2 * gg:2 * gg + 2, :].rearrange("p h d -> p (h d)"),
                              ident[:, :])
                last.then_inc(wt_ready, 1)
            pe.wait_ge(silu_made, 1)
            pe.wait_ge(ld_mod, 16)
            for b in range(B):
                for k, (lo, hi) in enumerate(((0, 512), (512, MODS * C))):
                    q = 2 * b + k
                    if q >= 4:
                        pe.wait_ge(mod_copied, q - 3)
                    mm(banks[:, q % 4, 0:hi - lo], silu_bc[:, b, :], wmod_sb[:, lo:hi],
                       start=True, stop=True).then_inc(mod_ready, 1)
            pe.wait_ge(ld_wp, 16)
            for q in range(6, 14):
                pe.wait_ge(wt_copied, q - 3 if q > 8 else 6)
                for g in range(4):
                    h = range(H)[heads_of(q - 6)][g]
                    lo = D * (h % 2)
                    if q < 10:
                        l, r = wT[lo:lo + D, 1, h // 2, :], wT[lo:lo + D, 0, h // 2, :]
                    else:
                        l, r = wT[lo:lo + D, 2, h // 2, :], wp_sb[lo:lo + D, h // 2, :]
                    last = mm(banks[:, 4 + q % 4, g * P:(g + 1) * P], l, r, start=True, stop=True)
                last.then_inc(wt_ready, 1)
            pe.wait_ge(wt_copied, 14)
            pe.wait_ge(mod_copied, 16)

            def step(m, at, w):
                if has(at, 1):
                    n, r, par = m - 1, (at - 1) % 2, (at - 1) // NHG % 2
                    pe.wait_ge(k_copied, 2 * n + 2)
                    for k in range(3):
                        bank = SP_[(3 * (at - 1) + k) % 2]
                        if at - 1 > 0 or k == 2:
                            pe.wait_ge(biased, 8 * n + (-2, 0, 4)[k])
                        if k == 0:
                            mm(banks[:, bank, :], hT_cur[:, par, 0:P], kT[:, r, :, 0:P],
                               start=True, stop=True).then_inc(s_ready, 1)
                        else:
                            mm(banks[:, bank, :], hT_cur[:, par, P:T], kT[:, r, 2 * k - 2:2 * k, :],
                               start=True, stop=True).then_inc(s_ready, 1)
                if at % NHG == 0 and has(at, 0):
                    pe.wait_ge(hcur_made, w + 1)
                    if w_at(at) >= 2:
                        pe.wait_ge(lg_copied, w - 1)
                    for t in range(TPB):
                        last = tr(banks[:, AUX, t * P:(t + 1) * P], h_cur[:, w_at(at) % 2, t, :], ident[:, :])
                    last.then_inc(hT_ready, 1)
                if has(at, 3):
                    n, r, par = m - 3, (at - 3) % 2, (at - 3) // NHG % 2
                    pe.wait_ge(t_copied, 3 * n + 3)
                    for k in range(2):
                        if has(at, 1):
                            pe.wait_ge(k_copied, 2 * (m - 1) + k + 1)
                        else:
                            pe.wait_ge(u_copied, 2 * (m - 4) + k + 1)
                        mm(banks[:, KU[k], :], h_cur[:, par, 0, :], pT0[:, r, 2 * k:2 * k + 2, :],
                           start=True, stop=False)
                        u2 = banks[:, KU[k], :].rearrange("p (h t) -> p h t", h=2)[:, :, P:T]
                        mm(u2, h_cur[:, par, 1, :], pT1[:, r, 2 * k:2 * k + 2, :],
                           start=False, stop=True).then_inc(u_ready, 1)
                if at % NHG == 0 and w_at(at) >= 2:
                    pe.wait_ge(oT_copied, w - 1)
                    if w_at(at) < B:
                        pe.wait_ge(hT_copied, w + 1)
                    pe.wait_ge(lg_copied, w - 1)
                    for t in range(TPB):
                        last = tr(banks[:, AUX, T + t * P:T + (t + 1) * P], oT[:, t * P:(t + 1) * P],
                                  ident[:, :])
                    last.then_inc(oN_ready, 1)
                if at % NHG == 2 and w_at(at) >= 2:
                    pe.wait_ge(h2_made, w - 1)
                    if w_at(at) < B:
                        pe.wait_ge(hT_copied, w + 1)
                    for t in range(TPB):
                        last = tr(banks[:, AUX, t * P:(t + 1) * P], h2_cur[:, t, :], ident[:, :])
                    last.then_inc(h2T_ready, 1)
                if has(at, 2):
                    n, r2 = m - 2, (at - 2) % 2
                    pe.wait_ge(normed, 8 * n + 8)
                    for k in range(3):
                        bank = TP[(3 * (at - 2) + k) % 2]
                        if at - 2 > 0 or k == 2:
                            pe.wait_ge(t_copied, 3 * n + k - 1)
                        for q in range(4):
                            if k < 2:
                                h, t = 2 * k + q // 2, q % 2
                                src = S2[:, r2, h, 0:P] if t == 0 else S2[:, r2, h, P:2 * P]
                            else:
                                src = S2[:, r2, q, 2 * P:3 * P]
                            last = tr(banks[:, bank, q * P:(q + 1) * P], src, ident[:, :])
                        last.then_inc(t_ready, 1)
                if has(at, 0):
                    if at % NHG == 0:
                        pe.wait_ge(hT_copied, w + 1)
                    for k in range(2):
                        if has(at, 3):
                            pe.wait_ge(u_copied, 2 * (m - 3) + k + 1)
                        elif at >= 1:
                            pe.wait_ge(k_copied, 2 * (m - 1) + k + 1)
                        for j in range(2):
                            last = mm(banks[:, KU[k], j * T:(j + 1) * T],
                                      A_sb[:, HG * (at % NHG) + 2 * k + j, :],
                                      hT_cur[:, w_at(at) % 2, :], start=True, stop=True)
                        last.then_inc(k_ready, 1)
                if has(at, 4):
                    n, r, g = m - 4, (at - 4) % 2, (at - 4) % NHG
                    pe.wait_ge(u_copied, 2 * n + 2)
                    if g == 0 and w_at(at) >= 2:
                        pe.wait_ge(oT_copied, w - 1)
                    for j in range(HG):
                        last = mm(banks[:, OB, 0:T], G_sb[:, HG * g + j, :], uT[:, r, j, :],
                                  start=(g == 0 and j == 0), stop=(g == NHG - 1 and j == HG - 1))
                    last.then_inc(o_ready, 1)
                if at % NHG == 3 and w_at(at) >= 2:
                    pe.wait_ge(h2T_copied, w - 1)
                    for t in range(TPB):
                        last = mm(banks[:, AUX, T + t * E:T + (t + 1) * E], h2T[:, t * P:(t + 1) * P],
                                  wr_sb[:, :], start=True, stop=True)
                    last.then_inc(lg_ready, 1)
            pe.wait_ge(ld_small, 16 * 6)
            attention(pe, step)

            with pe.Fori(0, ROUNDS) as i:
                pe.wait_ge(counted, i + 1)
                mm(banks[:, 0, 0:3 * E], ones_bf[:, :], cnt_bf[:, :, :].rearrange("p a e -> p (a e)"),
                   start=True, stop=True).then_inc(count_ready, 1)

            def prefix(bank, mask):
                out_ = banks[:, bank, 0:NT * E].rearrange("p (t e) -> p t e", e=E)
                last = mm(out_, before_bf[:, :], mask, start=True, stop=False)
                for t in range(NT - 1):
                    last = mm(out_[:, t + 1:, :], ones_bf[:, :],
                              mask[:, t:t + 1, :].to_broadcast([P, NT - 1 - t, E]),
                              start=False, stop=t == NT - 2)
                return last

            pe.wait_ge(masks_made, 1)
            prefix(1, masks[:, 1, :, :])
            mm(banks[:, 2, 0:E], ones_bf[:, :], ngt_bf[:, :], start=True, stop=True
               ).then_inc(prefix_ready, 1)
            pe.wait_ge(sel_made, 1)
            prefix(3, masks[:, 0, :, :]).then_inc(pos_ready, 1)

            def expert_in(q):
                pe.wait_ge(ld_xe[q], 16)
                for k in range(2):
                    if q >= 1:
                        pe.wait_ge(x_copied, 2 * (q - 1) + k + 1)
                    for t in range(4 * k, min(4 * k + 4, 5)):
                        last = tr(banks[:, k, (t % 4) * P:(t % 4 + 1) * P], xe_sb[:, q, t, :], ident[:, :])
                    last.then_inc(x_ready, 1)

            def first(e):
                pe.wait_ge(x_copied, 2 * (e // 2) + 2)
                pe.wait_ge(ld_w1, 16)
                for f in range(FT):
                    if e >= 1:
                        pe.wait_ge(gelu_done, FT * (e - 1) + f + 1)
                    mm(banks[:, 2 + f, 0:CAP], w1_sb[:, e, f * P:(f + 1) * P],
                       xeT[:, e // 2, CAP * (e % 2):CAP * (e % 2 + 1)],
                       start=True, stop=True).then_inc(f_ready, 1)

            def second(e):
                pe.wait_ge(gelu_done, FT * (e + 1))
                pe.wait_ge(ld_w2, 16)
                if e >= 2:
                    pe.wait_ge(y_copied, 2 * (e - 2) + 2)
                for t in range(3):
                    rows = min(P, CAP - t * P)
                    for f in range(FT):
                        last = mm(banks[0:rows, 6 + e % 2, t * C:(t + 1) * C],
                                  gT[:, e % 2, f, t * P:t * P + rows], w2_sb[:, e, f, :],
                                  start=f == 0, stop=f == FT - 1)
                    if t >= 1:
                        last.then_inc(y_ready, 1)
            for e in range(E + 1):
                if e < E:
                    if e % 2 == 0:
                        expert_in(e // 2)
                    first(e)
                if e >= 1:
                    second(e - 1)

        @block.vector
        def _(dve):
            v = nc.vector
            count = [0]

            def link(ins):
                count[0] += 1
                ins.then_inc(dve_chain, 1)
                dve.wait_ge(dve_chain, count[0])

            def rsqrt(linked, out_, var, n):
                y, a = nwt[:, 1, 0:n], nwt[:, 2, 0:n]
                linked(v.tensor_scalar(nwt[:, 0, 0:n], var, EPS, None, op0=ALU.add))
                linked(v.tensor_scalar(a.bitcast(i32), nwt[:, 0, 0:n].bitcast(i32), 1, None,
                                       op0=ALU.logical_shift_right))
                linked(v.tensor_scalar(y.bitcast(i32), a.bitcast(i32), -1.0, float(0x5f3759df),
                                       op0=ALU.mult, op1=ALU.add))
                for k in range(NEWTON):
                    linked(v.tensor_tensor(a, y, y, op=ALU.mult))
                    linked(v.scalar_tensor_tensor(a, a, -0.5, nwt[:, 0, 0:n], op0=ALU.mult, op1=ALU.mult))
                    linked(v.scalar_tensor_tensor(out_ if k == NEWTON - 1 else y, a, 1.5, y,
                                                  op0=ALU.add, op1=ALU.mult))

            v.memset(nwt[:, 0, 0:1], 0.0).then_inc(lg_copied, 1)
            dve.wait_ge(silu_exp, 1)
            link(v.tensor_scalar(silu[:, 1, :], silu[:, 0, :], 1.0, None, op0=ALU.add))
            link(v.reciprocal(silu[:, 2, :], silu[:, 1, :]))
            link(v.tensor_tensor(silu[:, 1, :], cT[:, :], silu[:, 2, :], op=ALU.mult))
            v.tensor_copy(silu_bc[:, :, :], silu[:, 1, :].unsqueeze(2).to_broadcast([P, B, P])
                          ).then_inc(silu_made, 1)
            dve.wait_ge(ld_tab, 32)
            far = T - REL - 1
            link(v.memset(band[:, far:], NEG))
            link(v.tensor_copy(band[:, 0:far], tabT[:, 0:1].to_broadcast([H, far])))
            v.tensor_copy(band[:, far:far + REL + 1], tabT[:, 0:REL + 1]).then_inc(band_made, 1)
            dve.wait_ge(ld_x, 16)
            for t in range(NT):
                last = v.bn_stats(stats[:, t, :], xr[:, t, :])
            link(last)
            for t in range(NT):
                last = v.bn_aggr(mv[:, t, :], stats[:, t, :])
            link(last)
            rsqrt(link, rstd[:, :], mv[:, :, 1], NT)
            for q in range(2 * B):
                dve.wait_ge(mod_ready, q + 1)
                b, k = q // 2, q % 2
                lo, hi = (0, 512) if k == 0 else (512, MODS * C)
                v.tensor_copy(mod[:, b, :, :].rearrange("p a n -> p (a n)")[:, lo:hi],
                              banks[:, q % 4, 0:hi - lo]).then_inc(mod_copied, 1)
            dve.wait_ge(mod_copied, 2 * B)
            for k in (CA, CB):
                last = v.tensor_scalar(mod[:, :, k, :], mod[:, :, k, :], 1.0, None, op0=ALU.add)
            link(last)
            for t in range(NT):
                last = v.tensor_scalar(hn[:, t, :], xr[:, t, :], mv[:, t, 0:1], rstd[:, t:t + 1],
                                       op0=ALU.subtract, op1=ALU.mult)
            link(last)
            hn4 = hn[:, :, :].rearrange("p (b t) n -> p b t n", b=B)
            for k, op in ((CA, ALU.mult), (SA, ALU.add)):
                for t in range(TPB):
                    last = v.tensor_tensor(hn4[:, :, t, :], hn4[:, :, t, :], mod[:, :, k, :], op=op)
                link(last)
            for k in (GA, GB):
                sgn, mag = (uT[:, n, :, :].rearrange("p h t -> p (h t)").rearrange("p (b n) -> p b n", b=B)
                            for n in range(2))
                link(v.tensor_scalar(sgn, mod[:, :, k, :], 0.0, 2.0, op0=ALU.is_ge, op1=ALU.mult))
                link(v.scalar_tensor_tensor(mag, mod[:, :, k, :], -1.0, mod[:, :, k, :],
                                            op0=ALU.mult, op1=ALU.max))
                link(v.tensor_scalar(mag, mag, 0.25, None, op0=ALU.max))
                link(v.scalar_tensor_tensor(mod[:, :, k, :], sgn, -1.0, mag, op0=ALU.add, op1=ALU.mult))

            def ln2(m, at, w):
                b = w - 2
                n_links = 8 + RSQRT_LINKS
                base = [n_links * b]

                def chain(ins, stand=False):
                    base[0] = base[0] + 1
                    ins.then_inc(ln2_chain, 1)
                    dve.wait_ge(ln2_chain, reached(dve, base[0]) if stand else base[0])
                xb = xr[:, bass.ds(2 * b, TPB), :]
                o = banks[:, AUX, T:2 * T].rearrange("p (t n) -> p t n", t=TPB)

                def mods(k):
                    return mod[:, bass.ds(b, 1), k, :].to_broadcast([P, TPB, C])
                dve.wait_ge(oN_ready, b + 1)
                chain(v.tensor_tensor(gtmp[:, 0, :, :], o, both(bp_bc[:, :]), op=ALU.add))
                chain(v.tensor_tensor(gtmp[:, 1, :, :], gtmp[:, 0, :, :], mods(GA), op=ALU.mult))
                chain(v.tensor_tensor(xb, xb, gtmp[:, 1, :, :], op=ALU.add), stand=True)
                for t in range(TPB):
                    last = v.bn_stats(stats2[:, t, :], xr[:, bass.ds(2 * b + t, 1), :])
                chain(last, stand=True)
                for t in range(TPB):
                    last = v.bn_aggr(mv2[:, t, :], stats2[:, t, :])
                chain(last)
                rsqrt(chain, rstd2[:, :], mv2[:, :, 1], TPB)
                for t in range(TPB):
                    last = v.tensor_scalar(gtmp[:, 0, t, :], xr[:, bass.ds(2 * b + t, 1), :].rearrange("p a n -> p (a n)"),
                                           mv2[:, t, 0:1], rstd2[:, t:t + 1],
                                           op0=ALU.subtract, op1=ALU.mult)
                chain(last)
                chain(v.tensor_tensor(gtmp[:, 1, :, :], gtmp[:, 0, :, :], mods(CB), op=ALU.mult))
                chain(v.tensor_tensor(h2_cur[:, :, :], gtmp[:, 1, :, :], mods(SB), op=ALU.add))
                v.tensor_copy(hn[:, bass.ds(2 * b, TPB), :], h2_cur[:, :, :]).then_inc(h2_made, 1)

            def step(m, at, w):
                if at % NHG == 0 and has(at, 0):
                    if w_at(at) >= 2:
                        dve.wait_ge(u_ready, 2 * (m - 5) + 2)
                    v.tensor_copy(h_cur[:, w_at(at) % 2, :, :], hn[:, bass.ds(2 * w, TPB), :]
                                  ).then_inc(hcur_made, 1)
                if has(at, 1):
                    n, r, g = m - 1, (at - 1) % 2, (at - 1) % NHG
                    if at - 1 >= 2:
                        dve.wait_ge(t_ready, 3 * (m - 3) + 3)
                    for k in range(3):
                        bank = SP_[(3 * (at - 1) + k) % 2]
                        dve.wait_ge(s_ready, reached(dve, 3 * n + k + 1))
                        if k == 0:
                            parts = [(h, banks[:, bank, h * P:(h + 1) * P], S2[:, r, h, 0:P],
                                      bias_sb[:, HG * g + h, P:T], h) for h in range(HG)]
                        else:
                            parts = [(h, banks[:, bank, (h % 2) * T:(h % 2 + 1) * T], S2[:, r, h, P:P + T],
                                      bias_sb[:, HG * g + h, :], HG + h) for h in (2 * k - 2, 2 * k - 1)]
                        for h, src, dst, bias, col in parts:
                            v.tensor_tensor_reduce(out=dst, in0=src, in1=bias, scale=-1.0, scalar=3e38,
                                                   op0=ALU.add, op1=ALU.min,
                                                   accum_out=rowmin[:, r, col:col + 1]).then_inc(biased, 1)
                if at % NHG == 0 and has(at, 0):
                    dve.wait_ge(hT_ready, w + 1)
                    if w_at(at) >= 2:
                        dve.wait_ge(s_ready, 3 * (m - 5) + 3)
                    v.tensor_copy(hT_cur[:, w_at(at) % 2, :], banks[:, AUX, 0:T]).then_inc(hT_copied, 1)
                if has(at, 3):
                    n = m - 3
                    for k in range(2):
                        dve.wait_ge(u_ready, 2 * n + k + 1)
                        if at - 3 >= 2:
                            dve.wait_ge(o_ready, m - 4)
                        v.tensor_copy(uT[:, (at - 3) % 2, 2 * k:2 * k + 2, :].rearrange("p h t -> p (h t)"),
                                      banks[:, KU[k], :]).then_inc(u_copied, 1)
                if at % NHG == 0 and w_at(at) >= 2:
                    ln2(m, at, w)
                if has(at, 2):
                    n, r = m - 2, (at - 2) % 2
                    for k in range(3):
                        dve.wait_ge(t_ready, 3 * n + k + 1)
                        if at - 2 >= 2:
                            dve.wait_ge(u_ready, 2 * (m - 4) + 2)
                        src = banks[:, TP[(3 * (at - 2) + k) % 2], :]
                        dst = pT1[:, r, :, :] if k == 2 else pT0[:, r, 2 * k:2 * k + 2, :]
                        v.tensor_copy(dst.rearrange("p h t -> p (h t)"), src).then_inc(t_copied, 1)
                if has(at, 1):
                    dve.wait_ge(expd, 2 * HG * m)
                    v.reciprocal(rowinv[:, (at - 1) % 2, :], rowsum[:, (at - 1) % 2, :]).then_inc(inv_made, 1)
                if at % NHG == 2 and w_at(at) >= 2:
                    dve.wait_ge(h2T_ready, w - 1)
                    v.tensor_copy(h2T[:, :], banks[:, AUX, 0:T]).then_inc(h2T_copied, 1)
                if at % NHG == 3 and w_at(at) >= 2:
                    dve.wait_ge(lg_ready, w - 1)
                    v.tensor_tensor(lg[:, bass.ds(2 * (w - 2), TPB), :],
                                    banks[:, AUX, T:T + TPB * E].rearrange("p (t e) -> p t e", t=TPB),
                                    br_bc[:, :].unsqueeze(1).to_broadcast([P, TPB, E]),
                                    op=ALU.add).then_inc(lg_copied, 1)
            dve.wait_ge(zero_st, 48)
            dve.wait_ge(ld_bias, 16 * H)
            dve.wait_ge(ld_small, 16 * 6)
            attention(dve, step)

            dve.wait_ge(lg_copied, B + 1)
            dve.wait_ge(const_made, 8)

            def r(k):
                return rt[:, k, :, :]

            def tok(k):
                return rv[:, k, :]

            def tok_e(k):
                return rv[:, k, :].unsqueeze(2).to_broadcast([P, NT, E])

            def best(src, m_, oh):
                link(v.tensor_reduce(tok(m_), src, axis=X, op=ALU.max))
                link(v.tensor_tensor(r(SCORE), src, tok_e(m_), op=ALU.is_equal))
                link(v.tensor_tensor(r(TMP), r(SCORE), r(LOWFIRST), op=ALU.mult))
                link(v.tensor_reduce(tok(BEST), r(TMP), axis=X, op=ALU.max))
                link(v.tensor_tensor(r(oh), r(TMP), tok_e(BEST), op=ALU.is_equal))
            best(lg[:, :, :], M1, OH1)
            link(v.scalar_tensor_tensor(r(LG2), r(OH1), -3e38, lg[:, :, :], op0=ALU.mult, op1=ALU.add))
            best(r(LG2), M2, OH2)
            v.tensor_tensor(tok(SPARE), tok(M2), tok(M1), op=ALU.subtract).then_inc(top_made, 1)
            dve.wait_ge(e1_made, 1)
            link(v.tensor_scalar(tok(ONEP), tok(E1), 1.0, None, op0=ALU.add))
            link(v.reciprocal(tok(W0), tok(ONEP)))
            link(v.tensor_tensor(tok(W1_), tok(E1), tok(W0), op=ALU.mult))
            link(v.tensor_tensor(r(TMP), r(OH1), tok_e(W0), op=ALU.mult))
            link(v.tensor_tensor(r(SCORE), r(OH2), tok_e(W1_), op=ALU.mult))
            link(v.tensor_tensor(r(TMP), r(TMP), r(SCORE), op=ALU.add))
            link(v.tensor_tensor(r(SCORE), r(OH1), r(OH2), op=ALU.add))
            link(v.scalar_tensor_tensor(r(KEY), r(SCORE), -1.0, r(TMP), op0=ALU.add, op1=ALU.add))
            key_te = r(KEY).rearrange("p t e -> p e t").unsqueeze(1).to_broadcast([P, 3, E, NT])
            with dve.Fori(0, ROUNDS) as i:
                chain = [0]

                def linked(ins):
                    chain[0] += 1
                    ins.then_inc(search_chain, 1)
                    dve.wait_ge(search_chain, 6 * i + chain[0])
                linked(v.tensor_tensor(cand[:, 1:4, :], cand[:, 0:1, :].to_broadcast([P, 3, E]), incs[:, :, :],
                                       op=ALU.bitwise_or))
                candf = cand[:, :, :].bitcast(f32)
                linked(v.tensor_tensor(passing[:, :, :, :], key_te,
                                       candf[:, 1:4, :].unsqueeze(3).to_broadcast([P, 3, E, NT]), op=ALU.is_ge))
                with nc.allow_low_precision(reason="counts up to 16 are exact"):
                    v.tensor_reduce(cnt_bf[:, :, :], passing[:, :, :, :], axis=X, op=ALU.add).then_inc(counted, 1)
                linked(v.tensor_scalar(incs[:, :, :], incs[:, :, :], 2, None, op0=ALU.logical_shift_right))
                dve.wait_ge(count_ready, i + 1)
                cnt = banks[:, 0, 0:3 * E].rearrange("p (a e) -> p a e", a=3)
                linked(v.scalar_tensor_tensor(best4[:, 1:4, :], cnt, CAP - 0.5, candf[:, 1:4, :],
                                              op0=ALU.is_ge, op1=ALU.mult))
                linked(v.tensor_reduce(best4[:, 0, :], best4[:, 1:4, :].rearrange("p a e -> p e a"),
                                       axis=X, op=ALU.max))
                linked(v.tensor_tensor(candf[:, 0, :], best4[:, 0, :], candf[:, 0, :], op=ALU.max))
            thr = cand[:, 0, :].bitcast(f32).unsqueeze(1).to_broadcast([P, NT, E])
            link(v.tensor_tensor(r(MASKED), r(KEY), thr, op=ALU.is_gt))
            link(v.tensor_tensor(r(EQF), r(KEY), thr, op=ALU.is_equal))
            link(v.tensor_reduce(ngt[:, :], r(MASKED).rearrange("p t e -> p e t"), axis=X, op=ALU.add))
            link(v.tensor_copy(ngt_bf[:, :], ngt[:, :]))
            v.tensor_copy(masks[:, 1, :, :], r(EQF)).then_inc(masks_made, 1)
            dve.wait_ge(prefix_ready, 1)
            link(v.tensor_copy(ngt[:, :], banks[:, 2, 0:E]))
            pref = banks[:, 1, 0:NT * E].rearrange("p (t e) -> p t e", e=E)
            link(v.tensor_tensor(r(PREF), pref, ngt[:, :].unsqueeze(1).to_broadcast([P, NT, E]), op=ALU.add))
            link(v.scalar_tensor_tensor(r(TMP), r(PREF), CAP - 0.5, r(EQF), op0=ALU.is_lt, op1=ALU.mult))
            link(v.tensor_tensor(r(SEL), r(TMP), r(MASKED), op=ALU.add))
            v.tensor_copy(masks[:, 0, :, :], r(SEL)).then_inc(sel_made, 1)
            dve.wait_ge(pos_ready, 1)
            pos = banks[:, 3, 0:NT * E].rearrange("p (t e) -> p t e", e=E)
            link(v.tensor_tensor(r(SLOT), pos, slot_base[:, :, :], op=ALU.add))
            link(v.tensor_tensor(r(SLOT), r(SLOT), r(SEL), op=ALU.mult))
            for oh, k, gate, w_ in ((OH1, 0, G1, W0), (OH2, 1, G2, W1_)):
                link(v.tensor_tensor(r(TMP), r(oh), r(SLOT), op=ALU.mult))
                link(v.tensor_reduce(tok(SL), r(TMP), axis=X, op=ALU.add))
                link(v.tensor_scalar(idx[:, k, :], tok(SL), float(TRASH), None, op0=ALU.add))
                link(v.tensor_tensor(r(TMP), r(oh), r(SEL), op=ALU.mult))
                link(v.tensor_reduce(tok(SE), r(TMP), axis=X, op=ALU.add))
                last = v.tensor_tensor(tok(gate), tok(w_), tok(SE), op=ALU.mult)
                if k == 0:
                    link(last)
            last.then_inc(idx_made, 1)
            dve.wait_ge(idx_made, 1)

            for e in range(E + 1):
                if e < E and e % 2 == 0:
                    q = e // 2
                    for k in range(2):
                        dve.wait_ge(x_ready, 2 * q + k + 1)
                        n = 4 * P if k == 0 else P
                        v.tensor_copy(xeT[:, q, 4 * P * k:4 * P * k + n], banks[:, k, 0:n]).then_inc(x_copied, 1)
                if e >= 1:
                    d = e - 1
                    if d >= 2:
                        dve.wait_ge(st_y[d % 2], 32 * (d // 2))
                    dve.wait_ge(y_ready, 2 * d + 2)
                    bank = banks[:, 6 + d % 2, 0:3 * C].rearrange("p (t n) -> p t n", t=3)
                    v.tensor_tensor(y_sb[:, d % 2, 0:2, :], bank[:, 0:2, :],
                                    b2_bc[:, d, :].unsqueeze(1).to_broadcast([P, 2, C]), op=ALU.add
                                    ).then_inc(y_copied, 1)
                    v.tensor_tensor(y_sb[0:CAP - 2 * P, d % 2, 2, :], bank[0:CAP - 2 * P, 2, :],
                                    b2_bc[0:CAP - 2 * P, d, :], op=ALU.add).then_inc(y_copied, 1)

            dve.wait_ge(gathered, 2 * NT * 16)
            for s in range(4):
                ts = range(4 * s, 4 * s + 4)
                for t in ts:
                    last = v.scalar_tensor_tensor(hn[:, t, :], y_got[0][:, t, :], rv[:, G1, t:t + 1], hn[:, t, :],
                                                  op0=ALU.mult, op1=ALU.add)
                link(last)
                for t in ts:
                    last = v.scalar_tensor_tensor(hn[:, t, :], y_got[1][:, t, :], rv[:, G2, t:t + 1], hn[:, t, :],
                                                  op0=ALU.mult, op1=ALU.add)
                link(last)
                for t in ts:
                    last = v.bn_stats(stats[:, t, :], hn[:, t, :])
                link(last)
                for t in ts:
                    last = v.bn_aggr(mv[:, t, :], stats[:, t, :])
                link(last)
                rsqrt(link, rstd[:, 4 * s:4 * s + 4], mv[:, 4 * s:4 * s + 4, 1], 4)
                for t in ts:
                    last = v.tensor_scalar(hn[:, t, :], hn[:, t, :], mv[:, t, 0:1], rstd[:, t:t + 1],
                                           op0=ALU.subtract, op1=ALU.mult)
                link(last)
                part = hn[:, 4 * s:4 * s + 4, :]
                link(v.tensor_tensor(part, part, gamma_bc[:, :].unsqueeze(1).to_broadcast([P, 4, C]), op=ALU.mult))
                link(v.tensor_tensor(part, part, beta_bc[:, :].unsqueeze(1).to_broadcast([P, 4, C]), op=ALU.add))
                part4 = part.rearrange("p (b t) n -> p b t n", b=2)
                link(v.tensor_tensor(part4, part4, mod[:, 2 * s:2 * s + 2, GB, :].unsqueeze(2)
                                     .to_broadcast([P, 2, TPB, C]), op=ALU.mult))
                v.tensor_tensor(y_got[1][:, 4 * s:4 * s + 4, :], part, xr[:, 4 * s:4 * s + 4, :], op=ALU.add
                                ).then_inc(out_made, 1)


_INS = ['L0_attn_x', 'L0_attn_Wq', 'L0_attn_Wk', 'L0_attn_Wv', 'L0_attn_Wp', 'L0_attn_bp',
        'L0_attn_rel_table', 'L0_ffn_Wr', 'L0_ffn_br', 'L0_ffn_W1', 'L0_ffn_b1', 'L0_ffn_W2',
        'L0_ffn_b2', 'L0_ffn_gamma', 'L0_ffn_beta', 'L0_c', 'L0_wmod']
_OUTS = [((8, 256, 128), 'float32')]


def kernel(**inputs):
    import numpy as _np
    import concourse.bacc as _bacc
    from concourse import mybir as _mybir
    from concourse.bass_utils import run_bass_kernel_spmd as _run

    nc = _bacc.Bacc("TRN2", target_bir_lowering=False, num_devices=1)
    arrays, args = {}, []
    for name in _INS:
        a = _np.ascontiguousarray(inputs[name])
        arrays[f"in_{name}_dram"] = a
        args.append(nc.dram_tensor(f"in_{name}_dram", a.shape, _mybir.dt.from_np(a.dtype), kind="ExternalInput").ap())
    for i, (shape, dtype) in enumerate(_OUTS):
        dt = _mybir.dt.from_np(_np.dtype(dtype))
        args.append(nc.dram_tensor(f"out_{i}_dram", shape, dt, kind="ExternalOutput").ap())
    adaln_attention_moe_kernel(nc, *args)
    r = _run(nc, [arrays], core_ids=[0])
    got = tuple(r.results[0][f"out_{i}_dram"] for i in range(len(_OUTS)))
    return got[0]
```

```python
import concourse.bass as bass
from concourse import mybir
from contextlib import ExitStack


def adaln_attention_moe_kernel(nc, x, Wq, Wk, Wv, Wp, bp, rel_table, Wr, br, W1, b1, W2, b2,
                               gamma, beta, c, wmod, out):
    f32 = mybir.dt.float32
    f32r = mybir.dt.float32r
    bf16 = mybir.dt.bfloat16
    i32 = mybir.dt.int32
    ALU = mybir.AluOpType
    ACT = mybir.ActivationFunctionType
    X = mybir.AxisListType.X

    B, T, C = x.shape
    H, _, D = Wq.shape
    E, _, F = W1.shape
    P = 128
    REL = 16
    NT = B * T // P
    TPB = T // P
    assert (T, C, D, H, TPB) == (256, P, 64, 16, 2)
    CAP = -(-B * T * 5 // (4 * E))
    SLOTS = E * CAP
    TRASH = SLOTS
    ROW = C + 1
    NOWHERE = 2 * B * T
    PAIR = 2 * CAP // P
    HALF = CAP % P
    assert 2 * CAP == PAIR * P and 2 * HALF == P
    HG = 4
    NHG = H // HG
    GROUPS = B * NHG
    UNROLL = 2 * NHG
    FT = F // P
    EPS = 1e-5
    NEG = -1e30
    SCALE = float(D) ** -0.5
    BAND = P + T - 1
    BITS = 30
    DIGIT = 3
    ROUNDS = BITS // DIGIT
    CANDS = 2 ** DIGIT - 1
    MODS = 6
    OUT_CHUNKS = 4
    SA, CA, GA, SB, CB, GB = range(MODS)

    ctx = ExitStack()
    with ctx:
        def sb(name, shape, dt=f32, within=ctx):
            return within.enter_context(nc.sbuf_tensor(name, shape, dt))

        def sem(name):
            return ctx.enter_context(nc.semaphore(name))

        mod_dram = nc.dram_tensor("mod_dram", [B, MODS * C], f32, kind="Internal").ap()
        band_dram = nc.dram_tensor("band_dram", [H, BAND], f32, kind="Internal").ap()
        xe_dram = nc.dram_tensor("xe_dram", [SLOTS, ROW], f32, kind="Internal").ap()
        ye_dram = nc.dram_tensor("ye_dram", [B * T * 2, C], f32, kind="Internal").ap()

        ident = sb("ident", [P, P])
        xr = sb("xr", [P, NT, C])
        hn = sb("hn", [P, NT + TPB, C])
        mod = sb("mod", [P, B, MODS, C])
        bp_bc = sb("bp_bc", [P, C])
        gamma_bc = sb("gamma_bc", [P, C])
        beta_bc = sb("beta_bc", [P, C])
        br_bc = sb("br_bc", [P, E])
        b2_bc = sb("b2_bc", [P, E, C])
        wr_sb = sb("wr_sb", [P, E])
        b1_sb = sb("b1_sb", [P, E, FT])
        stats = sb("stats", [P, NT, 6])
        mv = sb("mv", [P, NT, 2])
        rstd = sb("rstd", [P, NT])
        rstd_all = sb("rstd_all", [P, NT])
        NEWTON = 3
        LN2_POOL_LINKS = 2
        nwt = sb("nwt", [P, 3, NT])
        lg = sb("lg", [P, TPB + NT, E])
        zeros = sb("zeros", [P, C])
        no_rows = sb("no_rows", [P, 5, ROW])

        rt = sb("rt", [P, 13, NT, E])
        LG2, OH1, OH2, SCORE, KEY, SEL, SLOT, MASKED, PREF, EQF, TMP, TMP2, LOWFIRST = range(13)
        rv = sb("rv", [P, 14, NT])
        M1, M2, BEST, E1, W0, W1_, SL, SL2, SE, SE2, G1, G2, ONEP, SPARE = range(14)
        masks = sb("masks", [P, 2, NT, E], bf16)
        ones_bf = sb("ones_bf", [P, P], bf16)
        before_bf = sb("before_bf", [P, P], bf16)
        cand = sb("cand", [P, 1 + CANDS, E], i32)
        incs = sb("incs", [P, CANDS, E], i32)
        passing = sb("passing", [P, NT, CANDS, E], bf16)
        best = sb("best", [P, 1 + CANDS, E])
        slot_base = sb("slot_base", [P, NT, E])
        ngt = sb("ngt", [P, E])
        ngt_bf = sb("ngt_bf", [P, E], bf16)
        idx = sb("idx", [P, 2, NT], i32)

        HI, LO = 0, 1
        attn = ExitStack()
        A_r = sb("A_r", [P, 2, H, C], f32r, attn)
        G_r = sb("G_r", [P, 2, H, C], f32r, attn)
        bias_sb = sb("bias_sb", [P, H, T], f32, attn)
        S2 = sb("S2", [P, 2, HG, P + T], f32, attn)
        rowmin = sb("rowmin", [P, 2, 2 * HG], f32, attn)
        rowsum = sb("rowsum", [P, 2, 2 * HG], f32, attn)
        rowinv = sb("rowinv", [P, 2, 2 * HG], f32, attn)
        oT = sb("oT", [P, T], f32, attn)
        h2_cur = sb("h2_cur", [P, TPB, C], f32, attn)
        h2T = sb("h2T", [P, T], f32, attn)
        stats2 = sb("stats2", [P, TPB, 6], f32, attn)
        mv2 = sb("mv2", [P, TPB, 2], f32, attn)
        nw2 = sb("nw2", [P, 4, TPB], f32, attn)
        gtmp = sb("gtmp", [P, 2, TPB, C], f32, attn)
        h_cur = sb("h_cur", [P, TPB, C], f32, attn)
        hTk = sb("hTk", [P, 2, 2, T], f32r, attn)
        start = ExitStack()
        wqk = sb("wqk", [P, 2, H, D], f32, start)
        wqT = sb("wqT", [P, H // 2, C], f32, start)
        wkT = sb("wkT", [P, H // 2, C], f32, start)
        wmod_sb = sb("wmod_sb", [P, MODS * C], f32, start)
        modrow = sb("modrow", [B, MODS, C], f32, start)
        gsign = sb("gsign", [B, 2, C], f32, start)
        band = sb("band", [H, BAND], f32, start)
        wv = sb("wv", [P, H, D], f32, start)
        wvT = sb("wvT", [P, H // 2, C], f32, start)
        wp_sb = sb("wp_sb", [P, H // 2, C], f32, start)
        start.close()
        h_r = sb("h_r", [P, 2, 2, TPB, C], f32r, attn)
        hTq = sb("hTq", [P, 2, 2, T], f32r, attn)
        kT = sb("kT", [P, 2, 2, HG, T], f32r, attn)
        uT = sb("uT", [P, 2, 2, HG, T], f32r, attn)
        pT0 = sb("pT0", [P, 2, 2, HG, T], f32r, attn)
        pT1 = sb("pT1", [P, 2, 2, HG, P], f32r, attn)
        tabT = sb("tabT", [H, 2 * REL + 1], f32, attn)
        cT = sb("cT", [P, B], f32, attn)
        silu = sb("silu", [P, 3, B], f32, attn)
        attn.close()

        w1_sb = sb("w1_sb", [P, E, F])
        w2_sb = sb("w2_sb", [P, E, FT, C])
        y_got = sb("y_got", [P, NT, 2, C])
        rows = sb("rows", [P, 2, NT, ROW])
        xe_sb = sb("xe_sb", [P, E // 2, PAIR, ROW])
        xeT = sb("xeT", [P, E // 2, 2 * CAP])
        gT = sb("gT", [P, 2, FT, CAP])
        y_sb = sb("y_sb", [P, E // 2, PAIR, C])
        ggb = sb("ggb", [P, B, C])
        xgb = sb("xgb", [P, NT, C])
        out_sb = sb("out_sb", [P, NT, C])
        banks = ctx.enter_context(nc.psum_tensor("banks", [P, 8, 512], f32))
        KU, SP_, TP, OB, AUX, HT0 = (0, 1), (2, 3), (4, 5), 6, 7, 2

        ld_x0 = sem("ld_x0")
        ld_x, ld_w, ld_wp, ld_c, ld_mod, ld_tab, ld_small, ld_bias, st_band = (
            sem(n) for n in ("ld_x", "ld_w", "ld_wp", "ld_c", "ld_mod", "ld_tab", "ld_small",
                             "ld_bias", "st_band"))
        ld_w1, ld_w2 = sem("ld_w1"), sem("ld_w2")
        zero_set, zero_st = sem("zero_set"), sem("zero_st")
        id_set, id_made, band_made = sem("id_set"), sem("id_made"), sem("band_made")
        const_made = sem("const_made")
        silu_exp, silu_made = sem("silu_exp"), sem("silu_made")
        mod_ready, modrow_made, st_mod, ld_mod0, ld_modr = (
            sem(n) for n in ("mod_ready", "modrow_made", "st_mod", "ld_mod0", "ld_modr"))
        wt_ready, wt_high = sem("wt_ready"), sem("wt_high")
        wT_copied, wt_low = sem("wT_copied"), sem("wt_low")
        stats_made, hn_chain = sem("stats_made"), sem("hn_chain")
        hr_high, hr_low, hTk_high, hTq_made = sem("hr_high"), sem("hr_low"), sem("hTk_high"), sem("hTq_made")
        k_high, t_high, u_high = sem("k_high"), sem("t_high"), sem("u_high")
        hn_made = sem("hn_made")
        hcur_made, hT_ready, hT_copied = sem("hcur_made"), sem("hT_ready"), sem("hT_copied")
        k_ready, k_copied = sem("k_ready"), sem("k_copied")
        s_ready, biased, expd, normed = sem("s_ready"), sem("biased"), sem("expd"), sem("normed")
        t_ready, t_copied = sem("t_ready"), sem("t_copied")
        u_ready, u_copied = sem("u_ready"), sem("u_copied")
        o_ready, oT_copied = sem("o_ready"), sem("oT_copied")
        oN_ready, h2_made = sem("oN_ready"), sem("h2_made")
        h2T_ready, h2T_copied = sem("h2T_ready"), sem("h2T_copied")
        lg_ready, lg_copied = sem("lg_ready"), sem("lg_copied")
        inv_made = sem("inv_made")
        dve_chain = sem("dve_chain")
        ln2_pool, ln2_dve = sem("ln2_pool"), sem("ln2_dve")
        attn_made, x2_made, norm2_made, h2_kept = (
            sem("attn_made"), sem("x2_made"), sem("norm2_made"), sem("h2_kept"))
        pool_chain = sem("pool_chain")
        top_made, e1_made = sem("top_made"), sem("e1_made")
        search_chain, compared, count_ready = sem("search_chain"), sem("compared"), sem("count_ready")
        masks_made, prefix_ready = sem("masks_made"), sem("prefix_ready")
        sel_made, pos_ready = sem("sel_made"), sem("pos_ready")
        idx_made, scattered = sem("idx_made"), sem("scattered")
        ld_xe = [sem(f"ld_xe{q}") for q in range(E // 2)]
        ids_made, rows_made, y_sent = sem("ids_made"), sem("rows_made"), sem("y_sent")
        ld_y = [sem(f"ld_y{s}") for s in range(OUT_CHUNKS)]
        ggb_made, fin_stats, fin_norm, fin_scaled = (
            sem("ggb_made"), sem("fin_stats"), sem("fin_norm"), sem("fin_scaled"))
        x_ready, x_copied = sem("x_ready"), sem("x_copied")
        f_ready, gelu_done = sem("f_ready"), sem("gelu_done")
        y_ready, y_copied = sem("y_ready"), sem("y_copied")
        out_made, st_out = sem("out_made"), sem("st_out")

        block = ctx.enter_context(nc.Block())

        def both(ap):
            return ap.unsqueeze(1).to_broadcast([P, TPB, C])

        LAG_S, LAG_T, LAG_U, LAG_O = 2, 3, 4, 5
        TRANSPOSES, G_IN_STEP = (0, 1, 2, 3, 8, 9), ((), (8, 9), (10, 11, 12), (13,))
        CONSTS = 5 + CANDS
        W_BANK = (4, 5, 6, 7, 4, 5, 6, 7, 4, 5, 6, 4, 5, 6)
        STEPS = GROUPS + 2 * NHG + 1

        def y_tiles(e):
            whole, mid = PAIR // 2, PAIR // 2
            if e % 2 == 0:
                return [(t, 0, P) for t in range(whole)] + [(mid, 0, HALF)]
            return [(mid, HALF, P)] + [(t, 0, P) for t in range(mid + 1, PAIR)]

        def flip(ap):
            return ap.rearrange("p (t n) -> p t n", n=P)[:, :, ::-1]

        def heads_of(q):
            k = (q - 4) if q < 8 else (q - 10)
            return slice(k % 2 + 8 * (k // 2), k % 2 + 8 * (k // 2) + 7, 2)

        class Links:

            def __init__(self, eng, chain, base=0, alone=False):
                self.eng, self.chain, self.count, self.alone = eng, chain, base, alone

            def __call__(self, ins):
                self.count = self.count + 1
                ins.then_inc(self.chain, 1)
                self.eng.wait_ge(self.chain, reached(self.eng, self.count) if self.alone else self.count)

        wait_register = {}

        def reached(eng, value):
            if not isinstance(value, int):
                if eng not in wait_register:
                    wait_register[eng] = eng.alloc_register("reached")
                eng.reg_mov(wait_register[eng], value)
                value = wait_register[eng]
            eng.wait_ge(id_made, 1)
            return value

        def pT_part(r, a, k):
            part = pT1[:, r, a, :, :] if k == 2 else pT0[:, r, a, 2 * k:2 * k + 2, :]
            return part.rearrange("p h t -> p (h t)")

        def w_at(at):
            return at // NHG

        def has(at, lag):
            return 0 <= at - lag < GROUPS

        def attention(eng, step):
            for m in range(UNROLL):
                step(m, m, m // NHG)
            with eng.Fori(1, GROUPS // UNROLL) as i:
                for j in range(UNROLL):
                    step(UNROLL * i + j, UNROLL + j, 2 * i + j // NHG)
            for m in range(GROUPS, STEPS):
                step(m, m, m // NHG)

        @block.sync
        def _(sp):
            sp.dma_start(cT[:, :], c.rearrange("b k -> k b"), allow_slow_non_contiguous=True).then_inc(ld_c, 16)
            sp.dma_start(wmod_sb[:, :], wmod).then_inc(ld_mod, 16)
            sp.dma_start(wqk[:, 0, :, :], Wq.rearrange("h c d -> c h d")).then_inc(ld_w, 16)
            sp.dma_start(wqk[:, 1, :, :], Wk.rearrange("h c d -> c h d")).then_inc(ld_w, 16)
            x_tiles = x.rearrange("b (t p) n -> p (b t) n", p=P)
            sp.dma_start(xr[:, TPB:, :], x_tiles[:, TPB:, :]).then_inc(ld_x, 16)
            sp.wait_ge(modrow_made, 1)
            sp.dma_start(mod_dram, modrow[:, :, :].rearrange("b a n -> b (a n)")).then_inc(st_mod, 16)
            sp.wait_ge(band_made, 1)
            sp.dma_start(band_dram, band[:, :]).then_inc(st_band, 16)
            sp.wait_ge(st_mod, 16)
            sp.dma_start(mod[:, 0:2, :, :].rearrange("p b a n -> p b (a n)"), mod_dram[0:2, :].partition_broadcast(P)
                         ).then_inc(ld_mod0, 16)
            sp.wait_ge(st_band, 16)
            sp.dma_start(bias_sb[:, :, :], bass.AP(band_dram.tensor, 0, [[1, P], [BAND, H], [1, T]])
                         ).then_inc(ld_bias, 16)
            sp.dma_start(wv[:, :, :], Wv.rearrange("h c d -> c h d")).then_inc(ld_wp, 16)
            sp.dma_start(wp_sb[:, :, :], Wp.rearrange("(g p) n -> p g n", p=P)).then_inc(ld_wp, 16)
            sp.dma_start(mod[:, 2:, :, :].rearrange("p b a n -> p b (a n)"), mod_dram[2:, :].partition_broadcast(P)
                         ).then_inc(ld_modr, 16)
            for dst, src in ((gamma_bc, gamma), (beta_bc, beta), (br_bc, br)):
                sp.dma_start(dst[:, :], src.partition_broadcast(P)).then_inc(ld_small, 16)
            sp.dma_start(b2_bc[:, :, :], b2.partition_broadcast(P)).then_inc(ld_small, 16)
            sp.dma_start(wr_sb[:, :], Wr).then_inc(ld_small, 16)
            sp.dma_start(b1_sb[:, :, :], b1.rearrange("e (f p) -> p e f", p=P), allow_slow_non_contiguous=True).then_inc(ld_small, 16)
            sp.wait_ge(zero_set, 3)
            for q in range(4):
                sp.dma_start(xe_dram.rearrange("(p a) n -> p (a n)", p=P)[:, 5 * ROW * q:5 * ROW * (q + 1)],
                             no_rows[:, :, :].rearrange("p a n -> p (a n)")).then_inc(zero_st, 16)
            sp.dma_start(ye_dram.rearrange("(p a) n -> p a n", p=P),
                         zeros[:, :].unsqueeze(1).to_broadcast([P, 2 * NT, C])).then_inc(zero_st, 16)

            sp.wait_ge(lg_copied, B + 1)
            sp.dma_start(w1_sb[:, :, :], W1.rearrange("e c f -> c e f")).then_inc(ld_w1, 16)
            sp.dma_start(w2_sb[:, :, :, :], W2.rearrange("e (f p) c -> p e f c", p=P)).then_inc(ld_w2, 16)
            sp.wait_ge(scattered, 2 * NT * 16)
            for q in range(E // 2):
                sp.dma_start(xe_sb[:, q, :, :],
                             xe_dram[q * PAIR * P:(q + 1) * PAIR * P, :].rearrange("(t p) n -> p t n", p=P)
                             ).then_inc(ld_xe[q], 16)
            sp.wait_ge(y_sent, 16 * PAIR * E // 2)
            n = NT // OUT_CHUNKS
            by_token = ye_dram.rearrange("(t p k) n -> p t k n", p=P, k=2)
            for s in range(OUT_CHUNKS):
                sp.dma_start(y_got[:, n * s:n * (s + 1), :, :], by_token[:, n * s:n * (s + 1), :, :]
                             ).then_inc(ld_y[s], 16)
            for s in range(OUT_CHUNKS):
                sp.wait_ge(out_made, s + 1)
                sp.dma_start(out.rearrange("b (t p) n -> p (b t) n", p=P)[:, n * s:n * (s + 1), :],
                             out_sb[:, n * s:n * (s + 1), :]).then_inc(st_out, 16)
            sp.wait_ge(st_out, 16 * OUT_CHUNKS)

        @block.gpsimd
        def _(pool):
            nc.gpsimd.memset(ident[:, :], 0.0).then_inc(id_set, 1)
            nc.gpsimd.memset(ones_bf[:, :], 1.0).then_inc(const_made, 1)
            pool.wait_ge(id_set, 1)
            nc.gpsimd.affine_select(out=ident[:, :], in_=ident[:, :], compare_op=ALU.not_equal,
                                    fill=1.0, base=0, pattern=[[-1, P]], channel_multiplier=1
                                    ).then_inc(id_made, 1)
            nc.gpsimd.memset(zeros[:, :], 0.0).then_inc(zero_set, 1)
            nc.gpsimd.memset(no_rows[:, :, 0:C], 0.0).then_inc(zero_set, 1)
            nc.gpsimd.memset(no_rows[:, :, C:ROW].bitcast(i32), NOWHERE).then_inc(zero_set, 1)
            nc.gpsimd.memset(h2_cur[:, :, :], 0.0).then_inc(h2_made, 1)
            pool.wait_ge(const_made, 1)
            nc.gpsimd.affine_select(out=before_bf[:, :], in_=ones_bf[:, :], compare_op=ALU.is_gt,
                                    fill=0.0, base=0, pattern=[[1, P]], channel_multiplier=-1
                                    ).then_inc(const_made, 1)
            nc.gpsimd.iota(slot_base[:, :, :], [[0, NT], [CAP, E]], base=-TRASH, channel_multiplier=0,
                           allow_small_or_imprecise_dtypes=True).then_inc(const_made, 1)
            nc.gpsimd.iota(rt[:, LOWFIRST, :, :], [[0, NT], [-1, E]], base=E, channel_multiplier=0,
                           allow_small_or_imprecise_dtypes=True).then_inc(const_made, 1)
            for j in range(CANDS):
                nc.gpsimd.memset(incs[:, j, :], (j + 1) << (BITS - DIGIT)).then_inc(const_made, 1)
            nc.gpsimd.memset(cand[:, 0, :], 0).then_inc(const_made, 1)

            t_, s_ = nc.gpsimd.tensor_tensor, nc.gpsimd.tensor_scalar

            def input_of(b):
                links = Links(pool, hn_chain, 4 * (b - 1))
                hb, xb = hn[:, 2 * b:2 * b + TPB, :], xr[:, 2 * b:2 * b + TPB, :]

                def each(ap):
                    return ap[:, 2 * b:2 * b + TPB].unsqueeze(2).to_broadcast([P, TPB, C])
                links(t_(hb, xb, each(mv[:, :, 0]), op=ALU.subtract))
                links(t_(hb, hb, each(rstd[:, :]), op=ALU.mult))
                links(t_(hb, hb, both(mod[:, b, CA, :]), op=ALU.mult))
                links(t_(hb, hb, both(mod[:, b, SA, :]), op=ALU.add))

            def step(m, at, w):
                if at == 0:
                    pool.wait_ge(stats_made, 1)
                    pool.wait_ge(ld_mod0, 16)
                if at == 1:
                    pool.wait_ge(ld_modr, 16)
                b = w - 2
                late = w_at(at) >= 2
                links = Links(pool, ln2_pool, LN2_POOL_LINKS * b, alone=True)

                def mods(k):
                    return mod[:, bass.ds(b, 1), k, :].to_broadcast([P, TPB, C])
                if at % NHG == 2 and late:
                    xb = xr[:, bass.ds(2 * b, TPB), :]
                    pool.wait_ge(attn_made, reached(pool, b + 1))
                    links(t_(gtmp[:, 1, :, :], gtmp[:, 0, :, :], mods(GA), op=ALU.mult))
                    t_(xb, xb, gtmp[:, 1, :, :], op=ALU.add).then_inc(x2_made, 1)
                if has(at, LAG_S):
                    n, r = m - LAG_S, at % 2
                    for k, (lo, hi) in enumerate(((0, P), (P, P + T))):
                        pool.wait_ge(inv_made, reached(pool, 2 * n + k + 1))
                        part = S2[:, r, :, lo:hi]
                        t_(part, part, rowinv[:, r, HG * k:HG * k + HG].unsqueeze(2)
                           .to_broadcast([P, HG, hi - lo]), op=ALU.mult).then_inc(normed, 1)
                if at % NHG == 0 and has(at, 0):
                    pool.wait_ge(hT_copied, reached(pool, w + 1))
                    if w_at(at) >= 2:
                        pool.wait_ge(s_ready, reached(pool, 3 * (m - 5) + 3))
                    for k in (HI, LO):
                        nc.gpsimd.tensor_copy(hTq[:, w_at(at) % 2, k, :].rearrange("p (t n) -> p t n", n=P),
                                              flip(hTk[:, w_at(at) % 2, k, :].bitcast(f32))).then_inc(hTq_made, 1)
                if at < B - 1:
                    input_of(at + 1)
                if at == B - 1:
                    nc.gpsimd.memset(hn[:, NT:, :], 0.0).then_inc(hn_chain, 4)
                if at % NHG == 3 and late:
                    links.count = LN2_POOL_LINKS * b + 1
                    pool.wait_ge(h2T_ready, reached(pool, w - 1))
                    pool.wait_ge(norm2_made, reached(pool, b + 1))
                    links(t_(gtmp[:, 1, :, :], gtmp[:, 0, :, :], mods(CB), op=ALU.mult))
                    t_(h2_cur[:, :, :], gtmp[:, 1, :, :], mods(SB), op=ALU.add).then_inc(h2_made, 1)
                    pool.wait_ge(h2_made, reached(pool, b + 2))
                    nc.gpsimd.tensor_copy(hn[:, bass.ds(2 * b, TPB), :], h2_cur[:, :, :]).then_inc(h2_kept, 1)
            attention(pool, step)

            pool.wait_ge(lg_copied, B + 1)
            pool.wait_ge(h2_kept, B)
            for k in range(2):
                nc.gpsimd.iota(rows[:, k, :, C:ROW].bitcast(i32), [[2 * P, NT], [0, 1]], base=k,
                               channel_multiplier=2).then_inc(ids_made, 1)
            nc.gpsimd.tensor_copy(rows[:, 1, :, 0:C], hn[:, 0:NT, :]).then_inc(rows_made, 1)
            pool.wait_ge(ld_small, 16 * 6)

            def per_batch(ap):
                return ap.unsqueeze(1).to_broadcast([P, B, C])
            t_(ggb[:, :, :], mod[:, :, GB, :], per_batch(gamma_bc[:, :]), op=ALU.mult).then_inc(ggb_made, 1)
            t_(out_sb[:, 0:B, :], mod[:, :, GB, :], per_batch(beta_bc[:, :]), op=ALU.mult).then_inc(ggb_made, 1)
            pool.wait_ge(ggb_made, 2)
            t_(xgb[:, :, :].rearrange("p (b t) n -> p b t n", t=TPB),
               xr[:, :, :].rearrange("p (b t) n -> p b t n", t=TPB),
               out_sb[:, 0:B, :].unsqueeze(2).to_broadcast([P, B, TPB, C]), op=ALU.add).then_inc(ggb_made, 1)
            pool.wait_ge(idx_made, 1)
            pool.wait_ge(ids_made, 2)
            pool.wait_ge(rows_made, 2)
            pool.wait_ge(zero_st, 80)
            for t in range(NT):
                for k in range(2):
                    nc.gpsimd.indirect_dma_start(
                        out=xe_dram, out_offset=bass.IndirectOffsetOnAxis(ap=idx[:, k, t:t + 1], axis=0),
                        in_=rows[:, k, t, :], in_offset=None, bounds_check=SLOTS - 1, oob_is_err=False
                    ).then_inc(scattered, 16)
            for q in range(E // 2):
                pool.wait_ge(ld_xe[q], 16)
                for t in range(PAIR):
                    pool.wait_ge(y_copied, 4 * q + (1, 1, 3, 4, 4)[t])
                    nc.gpsimd.indirect_dma_start(
                        out=ye_dram, out_offset=bass.IndirectOffsetOnAxis(
                            ap=xe_sb[:, q, t, C:ROW].bitcast(i32), axis=0),
                        in_=y_sb[:, q, t, :], in_offset=None, bounds_check=NOWHERE - 1, oob_is_err=False
                    ).then_inc(y_sent, 16)
            n = NT // OUT_CHUNKS
            for s in range(OUT_CHUNKS):
                part = hn[:, n * s:n * (s + 1), :].rearrange("p (b t) n -> p b t n", t=TPB)
                bs = slice(n * s // TPB, n * (s + 1) // TPB)
                pool.wait_ge(fin_norm, n * (s + 1))
                t_(part, part, ggb[:, bs, :].unsqueeze(2).to_broadcast([P, n // TPB, TPB, C]), op=ALU.mult
                   ).then_inc(fin_scaled, 1)

        @block.scalar
        def _(act):
            act.dma_start(xr[:, 0:TPB, :], x[0].rearrange("(t p) n -> p t n", p=P)).then_inc(ld_x0, 16)
            act.dma_start(tabT[:, :], rel_table.rearrange("r h -> h r"), allow_slow_non_contiguous=True).then_inc(ld_tab, 16)
            act.dma_start(bp_bc[:, :], bp.partition_broadcast(P)).then_inc(ld_tab, 16)
            act.wait_ge(ld_c, 16)
            nc.scalar.activation(silu[:, 0, :], cT[:, :], ACT.Exp, scale=-1.0).then_inc(silu_exp, 1)
            def weights_out(q):
                act.wait_ge(wt_ready, q + 1)
                src = banks[:, W_BANK[q], :]
                if q in TRANSPOSES:
                    dst = {0: wqT, 1: wkT, 4: wvT}[q // 2][:, 4 * (q % 2):4 * (q % 2) + 4, :]
                    nc.scalar.activation(dst.rearrange("p g n -> p (g n)"), src, ACT.Copy).then_inc(wT_copied, 1)
                else:
                    dst = (A_r if q < 8 else G_r)[:, HI, heads_of(q), :]
                    nc.scalar.activation(dst, src.rearrange("p (g n) -> p g n", g=4), ACT.Copy,
                                         scale=SCALE if q < 8 else 1.0).then_inc(wt_high, 1)
            for q in range(8):
                weights_out(q)

            def step(m, at, w):
                def exps(ks):
                    if not has(at, LAG_S):
                        return
                    n, r = m - LAG_S, at % 2
                    for k in ks:
                        h = k % HG
                        part = S2[:, r, h, P:P + T] if k // HG else S2[:, r, h, 0:P]
                        act.wait_ge(biased, 2 * HG * n + k + 1)
                        nc.scalar.activation(part, part, ACT.Exp, scale=-1.0,
                                             bias=rowmin[:, r, k:k + 1],
                                             accum_out=rowsum[:, r, k:k + 1]).then_inc(expd, 1)

                def t_part(k):
                    if not has(at, LAG_T):
                        return
                    n, r = m - LAG_T, (at - LAG_T) % 2
                    act.wait_ge(t_ready, 3 * n + k + 1)
                    if at - LAG_T >= 2:
                        act.wait_ge(u_ready, 2 * (m - 5) + 2)
                    nc.scalar.activation(pT_part(r, HI, k), banks[:, TP[(3 * (at - LAG_T) + k) % 2], :],
                                         ACT.Copy).then_inc(t_high, 1)

                def u_part(k):
                    if not has(at, LAG_U):
                        return
                    n = m - LAG_U
                    act.wait_ge(u_ready, 2 * n + k + 1)
                    if at - LAG_U >= 2:
                        act.wait_ge(o_ready, m - 5)
                    nc.scalar.activation(uT[:, at % 2, HI, 2 * k:2 * k + 2, :].rearrange("p h t -> p (h t)"),
                                         banks[:, KU[k], :], ACT.Copy).then_inc(u_high, 1)

                exps((0, 1, 2, 3))
                u_part(0)
                exps((4, 5))
                t_part(0)
                u_part(1)
                exps((6, 7))
                t_part(1)
                t_part(2)
                if has(at, 0):
                    for k in range(2):
                        act.wait_ge(k_ready, 2 * m + k + 1)
                        if at >= 2:
                            act.wait_ge(s_ready, 3 * (m - 2) + 3)
                        nc.scalar.activation(
                            kT[:, at % 2, HI, 2 * k:2 * k + 2, :].rearrange("p h t -> p (h t)"),
                            banks[:, KU[k], :], ACT.Copy).then_inc(k_high, 1)
                if at < len(G_IN_STEP):
                    for q in G_IN_STEP[at]:
                        weights_out(q)
                if at % NHG == 0 and 2 <= w_at(at) < B + 2:
                    act.wait_ge(o_ready, m - 4)
                    nc.scalar.activation(oT[:, :].rearrange("p (t n) -> p t n", n=P),
                                         flip(banks[:, OB, 0:T]), ACT.Copy).then_inc(oT_copied, 1)
            attention(act, step)

            act.wait_ge(top_made, 1)
            nc.scalar.activation(rv[:, E1, :], rv[:, SPARE, :], ACT.Exp).then_inc(e1_made, 1)
            act.wait_ge(lg_copied, B + 1)
            act.wait_ge(h2_kept, B)
            nc.scalar.activation(rows[:, 0, :, 0:C], hn[:, 0:NT, :], ACT.Copy).then_inc(rows_made, 1)
            for e in range(E):
                for f in range(FT):
                    act.wait_ge(f_ready, FT * e + f + 1)
                    if e >= 2:
                        act.wait_ge(y_ready, e - 1)
                    nc.scalar.activation(gT[:, e % 2, f, :], banks[:, 2 + f, 0:CAP], ACT.Gelu,
                                         bias=b1_sb[:, e, f:f + 1]).then_inc(gelu_done, 1)
            n = NT // OUT_CHUNKS
            for s in range(OUT_CHUNKS):
                act.wait_ge(fin_stats, s + 1)
                for t in range(n * s, n * (s + 1)):
                    nc.scalar.activation(hn[:, t, :], hn[:, t, :], ACT.Identity, scale=rstd[:, t:t + 1],
                                         bias=rv[:, SPARE, t:t + 1]).then_inc(fin_norm, 1)

        @block.tensor
        def _(pe):
            mm, tr = nc.tensor.matmul, nc.tensor.transpose
            pe.wait_ge(const_made, CONSTS)
            pe.wait_ge(id_made, 1)
            def weights(q):
                if q in TRANSPOSES:
                    pe.wait_ge(ld_w if q < 4 else ld_wp, 32)
                    if q >= 8:
                        pe.wait_ge(wt_low, 2)
                    w_ = wqk[:, q // 2, :, :] if q < 4 else wv[:, :, :]
                elif q < 8:
                    pe.wait_ge(wT_copied, 4)
                else:
                    pe.wait_ge(wT_copied, 6)
                    pe.wait_ge(wt_low, 5 if q == 13 else 4)
                for g in range(4):
                    out_ = banks[:, W_BANK[q], g * P:(g + 1) * P]
                    if q in TRANSPOSES:
                        gg = 4 * (q % 2) + g
                        last = tr(out_, w_[:, 2 * gg:2 * gg + 2, :].rearrange("p h d -> p (h d)"), ident[:, :])
                        continue
                    h = range(H)[heads_of(q)][g]
                    lo = D * (h % 2)
                    l, r = (wkT, wqT) if q < 8 else (wvT, wp_sb)
                    last = mm(out_, l[lo:lo + D, h // 2, :], r[lo:lo + D, h // 2, :], start=True, stop=True)
                last.then_inc(wt_ready, 1)
            pe.wait_ge(silu_made, 1)
            pe.wait_ge(ld_mod, 16)
            for k, (lo, hi) in enumerate(((0, 512), (512, MODS * C))):
                mm(banks[0:B, k, 0:hi - lo], silu[:, 1, :], wmod_sb[:, lo:hi],
                   start=True, stop=True).then_inc(mod_ready, 1)
            for q in range(8):
                weights(q)
            pe.wait_ge(hcur_made, 1)
            for t in range(TPB):
                last = tr(banks[:, HT0, t * P:(t + 1) * P], h_cur[:, t, :], ident[:, :])
            last.then_inc(hT_ready, 1)

            def mm3(out_, l, r, start, stop):
                mm(out_, l(HI), r(HI), start=start, stop=False)
                mm(out_, l(HI), r(LO), start=False, stop=False)
                return mm(out_, l(LO), r(HI), start=False, stop=stop)

            def step(m, at, w):
                def scores(k):
                    if not has(at, LAG_S):
                        return
                    n, r, par = m - LAG_S, at % 2, (at - LAG_S) // NHG % 2
                    if k == 0:
                        pe.wait_ge(k_copied, 2 * n + 2)
                        if (at - LAG_S) % NHG == 0:
                            pe.wait_ge(hTq_made, 2 * w + 2)
                    if at - LAG_S > 0 or k == 2:
                        pe.wait_ge(biased, 8 * n + (-2, 0, 4)[k])
                    tile = 0 if k == 0 else 1
                    mm3(banks[:, SP_[(3 * at + k) % 2], :],
                        lambda a: hTq[:, par, a, tile * P:(tile + 1) * P],
                        lambda a: kT[:, r, a, :, 0:P] if k == 0 else kT[:, r, a, 2 * k - 2:2 * k, :],
                        True, True).then_inc(s_ready, 1)

                def transposed(k):
                    if not has(at, LAG_T):
                        return
                    n, r = m - LAG_T, (at - LAG_T) % 2
                    if k == 0:
                        pe.wait_ge(normed, 2 * n + 2)
                    if at == LAG_T and k < 2:
                        pe.wait_ge(wt_low, 6 + k)
                    if at - LAG_T > 0 or k == 2:
                        pe.wait_ge(t_copied, 3 * n + k - 1)
                    for q in range(4):
                        if k < 2:
                            h, t = 2 * k + q // 2, q % 2
                            src = S2[:, r, h, 0:P] if t == 0 else S2[:, r, h, P:2 * P]
                        else:
                            src = S2[:, r, q, 2 * P:3 * P]
                        last = tr(banks[:, TP[(3 * (at - LAG_T) + k) % 2], q * P:(q + 1) * P], src, ident[:, :])
                    last.then_inc(t_ready, 1)

                def weighted(k):
                    if not has(at, LAG_U):
                        return
                    n, r, par = m - LAG_U, at % 2, (at - LAG_U) // NHG % 2
                    if k == 0:
                        if (at - LAG_U) % NHG == 0:
                            pe.wait_ge(hr_low, w)
                        pe.wait_ge(t_copied, 3 * n + 3)
                    if has(at, 1):
                        pe.wait_ge(k_copied, 2 * (m - 1) + k + 1)
                    else:
                        pe.wait_ge(u_copied, 2 * (m - 5) + k + 1)
                    mm3(banks[:, KU[k], :], lambda a: h_r[:, par, a, 0, :],
                        lambda a: pT0[:, r, a, 2 * k:2 * k + 2, :], True, False)
                    mm3(banks[:, KU[k], :].rearrange("p (h t) -> p h t", h=2)[:, :, P:T],
                        lambda a: h_r[:, par, a, 1, :],
                        lambda a: pT1[:, r, a, 2 * k:2 * k + 2, :], False, True).then_inc(u_ready, 1)

                if at == 2 * NHG - 1:
                    pe.wait_ge(ld_small, 16 * 6)
                scores(0)
                scores(1)
                weighted(0)
                transposed(0)
                scores(2)
                weighted(1)
                transposed(1)
                if at % NHG == 0 and w_at(at) >= 2:
                    pe.wait_ge(h2_made, w - 1)
                    if w_at(at) < B:
                        pe.wait_ge(hT_copied, w + 1)
                    for t in range(TPB):
                        last = tr(banks[:, AUX, t * P:(t + 1) * P], h2_cur[:, t, :], ident[:, :])
                    last.then_inc(h2T_ready, 1)
                if at % NHG == 1 and w_at(at) >= 2:
                    pe.wait_ge(oT_copied, w - 1)
                    pe.wait_ge(lg_copied, w - 1)
                    for t in range(TPB):
                        last = tr(banks[:, AUX, T + t * P:T + (t + 1) * P], oT[:, t * P:(t + 1) * P],
                                  ident[:, :])
                    last.then_inc(oN_ready, 1)
                if has(at, LAG_O):
                    n, r, g = m - LAG_O, (at - LAG_O) % 2, (at - LAG_O) % NHG
                    if at == LAG_O:
                        pe.wait_ge(wt_low, 8)
                    pe.wait_ge(u_copied, 2 * n + 2)
                    if g == 0 and w_at(at) >= 2:
                        pe.wait_ge(oT_copied, w - 1)
                    for j in range(HG):
                        last = mm3(banks[:, OB, 0:T], lambda a: G_r[:, a, HG * g + j, :],
                                   lambda a: uT[:, r, a, j, :], g == 0 and j == 0, g == NHG - 1 and j == HG - 1)
                    last.then_inc(o_ready, 1)
                transposed(2)
                if at % NHG == 2 and w_at(at) < B:
                    pe.wait_ge(hcur_made, w + 2)
                    pe.wait_ge(hT_copied, w + 1)
                    if w_at(at) >= 2:
                        pe.wait_ge(attn_made, w - 1)
                    for t in range(TPB):
                        last = tr(banks[:, AUX, t * P:(t + 1) * P], h_cur[:, t, :], ident[:, :])
                    last.then_inc(hT_ready, 1)
                if has(at, 0):
                    if at % NHG == 0:
                        pe.wait_ge(hT_copied, w + 1)
                    if at == 0:
                        pe.wait_ge(wt_low, 4)
                    for k in range(2):
                        if has(at, LAG_U):
                            pe.wait_ge(u_copied, 2 * (m - LAG_U) + k + 1)
                        elif at >= 1:
                            pe.wait_ge(k_copied, 2 * (m - 1) + k + 1)
                        for j in range(2):
                            last = mm3(banks[:, KU[k], j * T:(j + 1) * T],
                                       lambda a: A_r[:, a, HG * (at % NHG) + 2 * k + j, :],
                                       lambda a: hTk[:, w_at(at) % 2, a, :], True, True)
                        last.then_inc(k_ready, 1)
                if at < len(G_IN_STEP):
                    for q in G_IN_STEP[at]:
                        weights(q)
                if at % NHG == 0 and w_at(at) >= 2:
                    pe.wait_ge(h2T_copied, w - 1)
                    for t in range(TPB):
                        last = mm(banks[:, AUX, T + t * E:T + (t + 1) * E], h2T[:, t * P:(t + 1) * P],
                                  wr_sb[:, :], start=True, stop=True)
                    last.then_inc(lg_ready, 1)
            attention(pe, step)

            with pe.Fori(0, ROUNDS) as i:
                for t in range(NT):
                    if t % (NT // 2) == 0:
                        pe.wait_ge(compared, 2 * i + 1 + t // (NT // 2))
                    last = mm(banks[:, 0, 0:CANDS * E], ones_bf[:, :], passing[:, t, :, :].rearrange("p a e -> p (a e)"),
                              start=t == 0, stop=t == NT - 1)
                last.then_inc(count_ready, 1)

            def prefix(bank, mask):
                out_ = banks[:, bank, 0:NT * E].rearrange("p (t e) -> p t e", e=E)
                last = mm(out_, before_bf[:, :], mask, start=True, stop=False)
                for t in range(NT - 1):
                    last = mm(out_[:, t + 1:, :], ones_bf[:, :],
                              mask[:, t:t + 1, :].to_broadcast([P, NT - 1 - t, E]),
                              start=False, stop=t == NT - 2)
                return last

            pe.wait_ge(masks_made, 1)
            prefix(1, masks[:, 1, :, :])
            mm(banks[:, 2, 0:E], ones_bf[:, :], ngt_bf[:, :], start=True, stop=True
               ).then_inc(prefix_ready, 1)
            pe.wait_ge(sel_made, 1)
            prefix(3, masks[:, 0, :, :]).then_inc(pos_ready, 1)

            def expert_in(q):
                pe.wait_ge(ld_xe[q], 16)
                for k in range(2):
                    if q >= 1:
                        pe.wait_ge(x_copied, 2 * (q - 1) + k + 1)
                    for t in range(4 * k, min(4 * k + 4, PAIR)):
                        last = tr(banks[:, k, (t % 4) * P:(t % 4 + 1) * P], xe_sb[:, q, t, 0:C], ident[:, :])
                    last.then_inc(x_ready, 1)

            def first(e):
                pe.wait_ge(x_copied, 2 * (e // 2) + 2)
                pe.wait_ge(ld_w1, 16)
                for f in range(FT):
                    if e >= 1:
                        pe.wait_ge(gelu_done, FT * (e - 1) + f + 1)
                    mm(banks[:, 2 + f, 0:CAP], w1_sb[:, e, f * P:(f + 1) * P],
                       xeT[:, e // 2, CAP * (e % 2):CAP * (e % 2 + 1)],
                       start=True, stop=True).then_inc(f_ready, 1)

            def second(e):
                pe.wait_ge(gelu_done, FT * (e + 1))
                pe.wait_ge(ld_w2, 16)
                if e >= 2:
                    pe.wait_ge(y_copied, 2 * (e - 2) + 2)
                for k, (tile, first_row, end_row) in enumerate(y_tiles(e)):
                    lo = tile * P + first_row - CAP * (e % 2)
                    for f in range(FT):
                        last = mm(banks[first_row:end_row, 6 + e % 2, k * C:(k + 1) * C],
                                  gT[:, e % 2, f, lo:lo + end_row - first_row], w2_sb[:, e, f, :],
                                  start=f == 0, stop=f == FT - 1)
                last.then_inc(y_ready, 1)
            for e in range(E + 1):
                if e < E:
                    if e % 2 == 0:
                        expert_in(e // 2)
                    first(e)
                if e >= 1:
                    second(e - 1)

        @block.vector
        def _(dve):
            v = nc.vector
            link = Links(dve, dve_chain)

            def rsqrt_ops(out_, z, a, var, variance):
                stt, ts = v.scalar_tensor_tensor, v.tensor_scalar
                yield lambda: ts(var, variance, EPS, None, op0=ALU.add)
                yield lambda: ts(a.bitcast(i32), var.bitcast(i32), 1, None, op0=ALU.logical_shift_right)
                yield lambda: ts(z.bitcast(i32), a.bitcast(i32), -1.0, float(0x5f3759df),
                                 op0=ALU.mult, op1=ALU.add)
                for k in range(NEWTON):
                    yield lambda k=k: stt(a, z, 0.25 ** k, z, op0=ALU.mult, op1=ALU.mult)
                    yield lambda: v.tensor_tensor(a, a, var, op=ALU.mult)
                    yield lambda: stt(z, a, -3.0, z, op0=ALU.add, op1=ALU.mult)
                yield lambda: ts(out_, z, (-0.5) ** NEWTON, None, op0=ALU.mult)

            def rsqrt(linked, out_, var, n):
                for op in rsqrt_ops(out_, nwt[:, 1, 0:n], nwt[:, 2, 0:n], nwt[:, 0, 0:n], var):
                    linked(op())

            dve.wait_ge(silu_exp, 1)
            link(v.tensor_scalar(silu[:, 1, :], silu[:, 0, :], 1.0, None, op0=ALU.add))
            link(v.reciprocal(silu[:, 2, :], silu[:, 1, :]))
            v.tensor_tensor(silu[:, 1, :], cT[:, :], silu[:, 2, :], op=ALU.mult).then_inc(silu_made, 1)
            dve.wait_ge(mod_ready, 2)
            rows = modrow[:, :, :].rearrange("b a n -> b (a n)")
            v.tensor_copy(rows[:, 0:512], banks[0:B, 0, :])
            link(v.tensor_copy(rows[:, 512:MODS * C], banks[0:B, 1, 0:MODS * C - 512]))
            gates, scales = modrow[:, GA:MODS:GB - GA, :], modrow[:, CA:MODS:CB - CA, :]
            link(v.tensor_scalar(scales, scales, 1.0, None, op0=ALU.add))
            link(v.tensor_scalar(gsign[:, :, :], gates, 0.0, 2.0, op0=ALU.is_ge, op1=ALU.mult))
            link(v.scalar_tensor_tensor(gates, gates, -1.0, gates, op0=ALU.mult, op1=ALU.max))
            link(v.tensor_scalar(gates, gates, 0.25, None, op0=ALU.max))
            v.scalar_tensor_tensor(gates, gsign[:, :, :], -1.0, gates, op0=ALU.add, op1=ALU.mult
                                   ).then_inc(modrow_made, 1)
            dve.wait_ge(ld_tab, 32)
            far = T - REL - 1
            link(v.memset(band[:, far:], NEG))
            link(v.tensor_copy(band[:, 0:far], tabT[:, 0:1].to_broadcast([H, far])))
            v.tensor_copy(band[:, far:far + REL + 1], tabT[:, 0:REL + 1]).then_inc(band_made, 1)
            def statistics(lo, hi, out_):
                for t in range(lo, hi):
                    last = v.bn_stats(stats[:, t, :], xr[:, t, :])
                link(last)
                for t in range(lo, hi):
                    last = v.bn_aggr(mv[:, t, :], stats[:, t, :])
                link(last)
                rsqrt(link, out_, mv[:, lo:hi, 1], hi - lo)
            dve.wait_ge(ld_x0, 16)
            dve.wait_ge(ld_x, 16)
            statistics(0, NT, rstd_all[:, :])
            v.tensor_copy(rstd[:, :], rstd_all[:, :]).then_inc(stats_made, 1)

            def weight_low(q):
                dve.wait_ge(wt_high, q - 3 if q < 8 else q - 5)
                half = A_r if q < 8 else G_r
                v.scalar_tensor_tensor(half[:, LO, heads_of(q), :],
                                       banks[:, W_BANK[q], :].rearrange("p (g n) -> p g n", g=4),
                                       SCALE if q < 8 else 1.0, half[:, HI, heads_of(q), :].bitcast(f32),
                                       op0=ALU.mult, op1=ALU.subtract).then_inc(wt_low, 1)
            dve.wait_ge(ld_mod0, 16)
            for t in range(TPB):
                last = v.tensor_scalar(hn[:, t, :], xr[:, t, :], mv[:, t, 0:1], rstd_all[:, t:t + 1],
                                       op0=ALU.subtract, op1=ALU.mult)
            link(last)
            link(v.tensor_tensor(hn[:, 0:TPB, :], hn[:, 0:TPB, :], both(mod[:, 0, CA, :]), op=ALU.mult))
            v.tensor_tensor(h_cur[:, :, :], hn[:, 0:TPB, :], both(mod[:, 0, SA, :]), op=ALU.add
                            ).then_inc(hcur_made, 1)
            for q in range(4, 8):
                weight_low(q)
            dve.wait_ge(hT_ready, 1)
            v.tensor_copy(hTk[:, 0, HI, :], banks[:, HT0, 0:T]).then_inc(hTk_high, 1)
            dve.wait_ge(hTk_high, 1)
            v.tensor_tensor(hTk[:, 0, LO, :], banks[:, HT0, 0:T], hTk[:, 0, HI, :].bitcast(f32),
                            op=ALU.subtract).then_inc(hT_copied, 1)

            def ln2_ops(b):
                yield lambda: [v.bn_stats(stats2[:, t, :], xr[:, bass.ds(2 * b + t, 1), :]) for t in range(TPB)][-1]
                yield lambda: [v.bn_aggr(mv2[:, t, :], stats2[:, t, :]) for t in range(TPB)][-1]
                yield from rsqrt_ops(nw2[:, 1, :], nw2[:, 1, :], nw2[:, 2, :], nw2[:, 3, :], mv2[:, :, 1])
                yield lambda: [v.tensor_scalar(gtmp[:, 0, t, :], xr[:, bass.ds(2 * b + t, 1), :],
                                               mv2[:, t, 0:1], nw2[:, 1, t:t + 1],
                                               op0=ALU.subtract, op1=ALU.mult) for t in range(TPB)][-1]
            LN2_OPS = 7 + 3 * NEWTON
            ln2_left = {}

            def ln2(at, w, count=1):
                if at % NHG < 2 or w_at(at) < 2:
                    return
                b, key = w - 2, at // NHG
                if key not in ln2_left:
                    ln2_left[key] = list(ln2_ops(b))
                for _ in range(count):
                    done = LN2_OPS - len(ln2_left[key])
                    if done == LN2_OPS:
                        return
                    if done == 0:
                        dve.wait_ge(x2_made, reached(dve, b + 1))
                    else:
                        dve.wait_ge(ln2_dve, reached(dve, (LN2_OPS - 1) * b + done))
                    last = ln2_left[key].pop(0)()
                    last.then_inc(norm2_made if done == LN2_OPS - 1 else ln2_dve, 1)

            def step(m, at, w):
                def bias(k):
                    if not has(at, LAG_S):
                        return
                    n, r, g = m - LAG_S, at % 2, (at - LAG_S) % NHG
                    if at - LAG_S >= 2 and k == 0:
                        dve.wait_ge(t_ready, 3 * (m - 4) + 3)
                    bank = SP_[(3 * at + k) % 2]
                    dve.wait_ge(s_ready, reached(dve, 3 * n + k + 1))
                    if k == 0:
                        parts = [(banks[:, bank, h * P:(h + 1) * P], S2[:, r, h, 0:P],
                                  bias_sb[:, HG * g + h, P:T], h) for h in range(HG)]
                    else:
                        parts = [(banks[:, bank, (h % 2) * T:(h % 2 + 1) * T], S2[:, r, h, P:P + T],
                                  bias_sb[:, HG * g + h, :], HG + h) for h in (2 * k - 2, 2 * k - 1)]
                    for src, dst, row, col in parts:
                        v.tensor_tensor_reduce(out=dst, in0=src, in1=row, scale=-1.0, scalar=3e38,
                                               op0=ALU.add, op1=ALU.min,
                                               accum_out=rowmin[:, r, col:col + 1]).then_inc(biased, 1)

                def low(dst, src, high):
                    return v.tensor_tensor(dst, src, high.bitcast(f32), op=ALU.subtract)

                def t_low(k):
                    if not has(at, LAG_T):
                        return
                    n, r = m - LAG_T, (at - LAG_T) % 2
                    dve.wait_ge(t_high, 3 * n + k + 1)
                    low(pT_part(r, LO, k), banks[:, TP[(3 * (at - LAG_T) + k) % 2], :], pT_part(r, HI, k)
                        ).then_inc(t_copied, 1)

                def u_low(k):
                    if not has(at, LAG_U):
                        return
                    dve.wait_ge(u_high, 2 * (m - LAG_U) + k + 1)
                    part = [uT[:, at % 2, a, 2 * k:2 * k + 2, :].rearrange("p h t -> p (h t)") for a in (HI, LO)]
                    low(part[LO], banks[:, KU[k], :], part[HI]).then_inc(u_copied, 1)

                def inverse(k):
                    if not has(at, LAG_S):
                        return
                    n, r, part = m - LAG_S, at % 2, slice(HG * k, HG * k + HG)
                    dve.wait_ge(expd, 2 * HG * n + HG * (k + 1))
                    v.reciprocal(rowinv[:, r, part], rowsum[:, r, part]).then_inc(inv_made, 1)

                new = at % NHG == 2 and w_at(at) < B
                par = (w_at(at) + 1) % 2
                if new:
                    dve.wait_ge(hn_chain, 4 * (w + 1))
                    dve.wait_ge(hT_ready, w + 1)
                    dve.wait_ge(hr_low, w + 1)
                    v.tensor_copy(h_cur[:, :, :], hn[:, bass.ds(2 * (w + 1), TPB), :]).then_inc(hcur_made, 1)
                if at == LAG_S:
                    dve.wait_ge(ld_bias, 16)
                if at == 2 * NHG - 1:
                    dve.wait_ge(ld_small, 16 * 6)
                bias(0)
                bias(1)
                ln2(at, w)
                if at % NHG == 1 and has(at, 0):
                    if w_at(at) >= 2:
                        dve.wait_ge(u_ready, 2 * (m - 6) + 2)
                    v.tensor_copy(h_r[:, w_at(at) % 2, HI, :, :], h_cur[:, :, :]).then_inc(hr_high, 1)
                bias(2)
                ln2(at, w)
                if at % NHG == 1 and has(at, 0):
                    dve.wait_ge(hr_high, w + 1)
                    low(h_r[:, w_at(at) % 2, LO, :, :], h_cur[:, :, :], h_r[:, w_at(at) % 2, HI, :, :]
                        ).then_inc(hr_low, 1)
                u_low(0)
                ln2(at, w)
                t_low(0)
                ln2(at, w)
                inverse(0)
                u_low(1)
                ln2(at, w)
                t_low(1)
                if at % NHG == 0 and w_at(at) >= 2:
                    dve.wait_ge(h2T_ready, w - 1)
                    v.tensor_copy(h2T[:, :], banks[:, AUX, 0:T]).then_inc(h2T_copied, 1)
                ln2(at, w)
                inverse(1)
                if at % NHG == 1 and w_at(at) >= 2:
                    dve.wait_ge(oN_ready, w - 1)
                    v.tensor_tensor(gtmp[:, 0, :, :],
                                    banks[:, AUX, T:2 * T].rearrange("p (t n) -> p t n", t=TPB),
                                    both(bp_bc[:, :]), op=ALU.add).then_inc(attn_made, 1)
                t_low(2)
                ln2(at, w)
                if new:
                    dve.wait_ge(hT_ready, w + 2)
                    if w_at(at) >= 1:
                        dve.wait_ge(hTq_made, 2 * w)
                        dve.wait_ge(k_ready, 2 * (m - 3) + 2)
                    v.tensor_copy(hTk[:, par, HI, :], banks[:, AUX, 0:T]).then_inc(hTk_high, 1)
                if has(at, 0):
                    for k in range(2):
                        dve.wait_ge(k_high, 2 * m + k + 1)
                        part = [kT[:, at % 2, a, 2 * k:2 * k + 2, :].rearrange("p h t -> p (h t)")
                                for a in (HI, LO)]
                        low(part[LO], banks[:, KU[k], :], part[HI]).then_inc(k_copied, 1)
                        ln2(at, w)
                ln2(at, w, LN2_OPS if at % NHG == 3 else 1)
                if new:
                    dve.wait_ge(hTk_high, w + 2)
                    low(hTk[:, par, LO, :], banks[:, AUX, 0:T], hTk[:, par, HI, :]).then_inc(hT_copied, 1)
                if at < len(G_IN_STEP):
                    for q in G_IN_STEP[at]:
                        if q not in TRANSPOSES:
                            weight_low(q)
                if at % NHG == 0 and w_at(at) >= 2:
                    dve.wait_ge(lg_ready, w - 1)
                    v.tensor_tensor(lg[:, bass.ds(2 * (w - 2), TPB), :],
                                    banks[:, AUX, T:T + TPB * E].rearrange("p (t e) -> p t e", t=TPB),
                                    br_bc[:, :].unsqueeze(1).to_broadcast([P, TPB, E]),
                                    op=ALU.add).then_inc(lg_copied, 1)
            attention(dve, step)

            dve.wait_ge(lg_copied, B + 1)
            dve.wait_ge(h2_kept, B)
            dve.wait_ge(const_made, CONSTS)

            def r(k):
                return rt[:, k, :, :]

            def tok(k):
                return rv[:, k, :]

            def tok_e(k):
                return rv[:, k, :].unsqueeze(2).to_broadcast([P, NT, E])

            def best_expert(src, m_, oh):
                link(v.tensor_reduce(tok(m_), src, axis=X, op=ALU.max))
                link(v.tensor_tensor(r(SCORE), src, tok_e(m_), op=ALU.is_equal))
                link(v.tensor_tensor(r(TMP), r(SCORE), r(LOWFIRST), op=ALU.mult))
                link(v.tensor_reduce(tok(BEST), r(TMP), axis=X, op=ALU.max))
                link(v.tensor_tensor(r(oh), r(TMP), tok_e(BEST), op=ALU.is_equal))
            best_expert(lg[:, TPB:, :], M1, OH1)
            link(v.scalar_tensor_tensor(r(LG2), r(OH1), -3e38, lg[:, TPB:, :], op0=ALU.mult, op1=ALU.add))
            best_expert(r(LG2), M2, OH2)
            v.tensor_tensor(tok(SPARE), tok(M2), tok(M1), op=ALU.subtract).then_inc(top_made, 1)
            dve.wait_ge(e1_made, 1)
            link(v.tensor_scalar(tok(ONEP), tok(E1), 1.0, None, op0=ALU.add))
            link(v.reciprocal(tok(W0), tok(ONEP)))
            link(v.tensor_tensor(tok(W1_), tok(E1), tok(W0), op=ALU.mult))
            link(v.tensor_tensor(r(TMP), r(OH1), tok_e(W0), op=ALU.mult))
            link(v.tensor_tensor(r(SCORE), r(OH2), tok_e(W1_), op=ALU.mult))
            link(v.tensor_tensor(r(TMP), r(TMP), r(SCORE), op=ALU.add))
            link(v.tensor_tensor(r(SCORE), r(OH1), r(OH2), op=ALU.add))
            link(v.scalar_tensor_tensor(r(KEY), r(SCORE), -1.0, r(TMP), op0=ALU.add, op1=ALU.add))
            SEARCH_LINKS = 5
            with dve.Fori(0, ROUNDS) as i:
                chain = [0]

                def linked(ins):
                    chain[0] += 1
                    ins.then_inc(search_chain, 1)
                    dve.wait_ge(search_chain, SEARCH_LINKS * i + chain[0])
                linked(v.tensor_tensor(cand[:, 1:, :], cand[:, 0:1, :].to_broadcast([P, CANDS, E]), incs[:, :, :],
                                       op=ALU.bitwise_or))
                candf = cand[:, :, :].bitcast(f32)
                for k in range(2):
                    part = slice(k * NT // 2, (k + 1) * NT // 2)
                    v.tensor_tensor(passing[:, part, :, :],
                                    r(KEY)[:, part, :].unsqueeze(2).to_broadcast([P, NT // 2, CANDS, E]),
                                    candf[:, 1:, :].unsqueeze(1).to_broadcast([P, NT // 2, CANDS, E]), op=ALU.is_ge
                                    ).then_inc(compared, 1)
                linked(v.tensor_scalar(incs[:, :, :], incs[:, :, :], DIGIT, None, op0=ALU.logical_shift_right))
                dve.wait_ge(count_ready, i + 1)
                cnt = banks[:, 0, 0:CANDS * E].rearrange("p (a e) -> p a e", a=CANDS)
                linked(v.scalar_tensor_tensor(best[:, 1:, :], cnt, CAP - 0.5, candf[:, 1:, :],
                                              op0=ALU.is_ge, op1=ALU.mult))
                linked(v.tensor_reduce(best[:, 0, :], best[:, 1:, :].rearrange("p a e -> p e a"),
                                       axis=X, op=ALU.max))
                linked(v.tensor_tensor(candf[:, 0, :], best[:, 0, :], candf[:, 0, :], op=ALU.max))
            thr = cand[:, 0, :].bitcast(f32).unsqueeze(1).to_broadcast([P, NT, E])
            link(v.tensor_tensor(r(MASKED), r(KEY), thr, op=ALU.is_gt))
            link(v.tensor_tensor(r(EQF), r(KEY), thr, op=ALU.is_equal))
            link(v.tensor_reduce(ngt[:, :], r(MASKED).rearrange("p t e -> p e t"), axis=X, op=ALU.add))
            link(v.tensor_copy(ngt_bf[:, :], ngt[:, :]))
            v.tensor_copy(masks[:, 1, :, :], r(EQF)).then_inc(masks_made, 1)
            dve.wait_ge(prefix_ready, 1)
            link(v.tensor_copy(ngt[:, :], banks[:, 2, 0:E]))
            pref = banks[:, 1, 0:NT * E].rearrange("p (t e) -> p t e", e=E)
            link(v.tensor_tensor(r(PREF), pref, ngt[:, :].unsqueeze(1).to_broadcast([P, NT, E]), op=ALU.add))
            link(v.scalar_tensor_tensor(r(TMP), r(PREF), CAP - 0.5, r(EQF), op0=ALU.is_lt, op1=ALU.mult))
            link(v.tensor_tensor(r(SEL), r(TMP), r(MASKED), op=ALU.add))
            v.tensor_copy(masks[:, 0, :, :], r(SEL)).then_inc(sel_made, 1)
            dve.wait_ge(pos_ready, 1)
            pos = banks[:, 3, 0:NT * E].rearrange("p (t e) -> p t e", e=E)
            link(v.tensor_tensor(r(SLOT), pos, slot_base[:, :, :], op=ALU.add))
            link(v.tensor_tensor(r(SLOT), r(SLOT), r(SEL), op=ALU.mult))
            both_oh = rt[:, OH1:OH2 + 1, :, :]

            def twice(k):
                return rt[:, k:k + 1, :, :].to_broadcast([P, 2, NT, E])
            tmps = rt[:, TMP:TMP2 + 1, :, :]
            link(v.tensor_tensor(tmps, both_oh, twice(SLOT), op=ALU.mult))
            link(v.tensor_reduce(rv[:, SL:SL2 + 1, :], tmps, axis=X, op=ALU.add))
            v.tensor_scalar(idx[:, :, :], rv[:, SL:SL2 + 1, :], float(TRASH), None, op0=ALU.add
                            ).then_inc(idx_made, 1)
            link(v.tensor_tensor(tmps, both_oh, twice(SEL), op=ALU.mult))
            link(v.tensor_reduce(rv[:, SE:SE2 + 1, :], tmps, axis=X, op=ALU.add))
            link(v.tensor_tensor(rv[:, G1:G2 + 1, :], rv[:, W0:W1_ + 1, :], rv[:, SE:SE2 + 1, :], op=ALU.mult))
            dve.wait_ge(idx_made, 1)

            for e in range(E + 1):
                if e < E and e % 2 == 0:
                    q = e // 2
                    for k in range(2):
                        dve.wait_ge(x_ready, 2 * q + k + 1)
                        n = 4 * P if k == 0 else P
                        v.tensor_copy(xeT[:, q, 4 * P * k:4 * P * k + n], banks[:, k, 0:n]).then_inc(x_copied, 1)
                if e >= 1:
                    d = e - 1
                    dve.wait_ge(y_ready, d + 1)
                    bank = banks[:, 6 + d % 2, 0:3 * C].rearrange("p (t n) -> p t n", t=3)
                    tiles = y_tiles(d)
                    for ks in ((0, 1), (2,)) if d % 2 == 0 else ((0,), (1, 2)):
                        tile, first_row, end_row = tiles[ks[0]]
                        v.tensor_tensor(y_sb[first_row:end_row, d // 2, tile:tile + len(ks), :],
                                        bank[first_row:end_row, ks[0]:ks[-1] + 1, :],
                                        b2_bc[first_row:end_row, d, :].unsqueeze(1)
                                        .to_broadcast([end_row - first_row, len(ks), C]), op=ALU.add
                                        ).then_inc(y_copied, 1)

            n = NT // OUT_CHUNKS

            def last_sum(s):
                dve.wait_ge(fin_scaled, s + 1)
                if s == 0:
                    dve.wait_ge(ggb_made, 3)
                part = slice(n * s, n * (s + 1))
                v.tensor_tensor(out_sb[:, part, :], hn[:, part, :], xgb[:, part, :], op=ALU.add
                                ).then_inc(out_made, 1)
            for s in range(OUT_CHUNKS):
                ts = range(n * s, n * (s + 1))
                dve.wait_ge(ld_y[s], 16)
                for k in range(2):
                    for t in ts:
                        last = v.scalar_tensor_tensor(hn[:, t, :], y_got[:, t, k, :], rv[:, G1 + k, t:t + 1],
                                                      hn[:, t, :], op0=ALU.mult, op1=ALU.add)
                    link(last)
                for t in ts:
                    last = v.bn_stats(stats[:, t, :], hn[:, t, :])
                link(last)
                for t in ts:
                    last = v.bn_aggr(mv[:, t, :], stats[:, t, :])
                link(last)
                part = slice(n * s, n * (s + 1))
                rsqrt(link, rstd[:, part], mv[:, part, 1], n)
                v.scalar_tensor_tensor(rv[:, SPARE, part], mv[:, part, 0], -1.0, rstd[:, part],
                                       op0=ALU.mult, op1=ALU.mult).then_inc(fin_stats, 1)
                if s >= 1:
                    last_sum(s - 1)
            last_sum(OUT_CHUNKS - 1)


_INS = ['L0_attn_x', 'L0_attn_Wq', 'L0_attn_Wk', 'L0_attn_Wv', 'L0_attn_Wp', 'L0_attn_bp',
        'L0_attn_rel_table', 'L0_ffn_Wr', 'L0_ffn_br', 'L0_ffn_W1', 'L0_ffn_b1', 'L0_ffn_W2',
        'L0_ffn_b2', 'L0_ffn_gamma', 'L0_ffn_beta', 'L0_c', 'L0_wmod']
_OUTS = [((8, 256, 128), 'float32')]


def kernel(**inputs):
    import numpy as _np
    import concourse.bacc as _bacc
    from concourse import mybir as _mybir
    from concourse.bass_utils import run_bass_kernel_spmd as _run

    nc = _bacc.Bacc("TRN2", target_bir_lowering=False, num_devices=1)
    arrays, args = {}, []
    for name in _INS:
        a = _np.ascontiguousarray(inputs[name])
        arrays[f"in_{name}_dram"] = a
        args.append(nc.dram_tensor(f"in_{name}_dram", a.shape, _mybir.dt.from_np(a.dtype), kind="ExternalInput").ap())
    for i, (shape, dtype) in enumerate(_OUTS):
        dt = _mybir.dt.from_np(_np.dtype(dtype))
        args.append(nc.dram_tensor(f"out_{i}_dram", shape, dt, kind="ExternalOutput").ap())
    adaln_attention_moe_kernel(nc, *args)
    r = _run(nc, [arrays], core_ids=[0])
    got = tuple(r.results[0][f"out_{i}_dram"] for i in range(len(_OUTS)))
    return got[0]
```

```python
import concourse.bass as bass
from concourse import mybir
from contextlib import ExitStack


def adaln_attention_moe_kernel(nc, x, Wq, Wk, Wv, Wp, bp, rel_table, Wr, br, W1, b1, W2, b2,
                               gamma, beta, c, wmod, out):
    f32 = mybir.dt.float32
    f32r = mybir.dt.float32r
    bf16 = mybir.dt.bfloat16
    i32 = mybir.dt.int32
    ALU = mybir.AluOpType
    ACT = mybir.ActivationFunctionType
    X = mybir.AxisListType.X

    B, T, C = x.shape
    H, _, D = Wq.shape
    E, _, F = W1.shape
    P = 128
    REL = 16
    NT = B * T // P
    TPB = T // P
    assert (T, C, D, H, TPB) == (256, P, 64, 16, 2)
    CAP = -(-B * T * 5 // (4 * E))
    SLOTS = E * CAP
    TRASH = SLOTS
    NOWHERE = 2 * B * T
    SLOT_TILES = SLOTS // P
    PAIR = 2 * CAP // P
    HALF = CAP % P
    assert 2 * CAP == PAIR * P and 2 * HALF == P
    HG = 4
    NHG = H // HG
    GROUPS = B * NHG
    UNROLL = 2 * NHG
    FT = F // P
    EPS = 1e-5
    NEWTON = 3
    LN2_POOL_LINKS = 2
    NEG = -1e30
    SCALE = float(D) ** -0.5
    BAND = P + T - 1
    BITS = 30
    DIGIT = 3
    ROUNDS = BITS // DIGIT
    CANDS = 2 ** DIGIT - 1
    SEARCH_SPLIT = 10
    ROUND_UNROLL = 5
    MODS = 6
    CHUNKS = ((0, 4), (4, 8), (8, 12), (12, 16))
    LAST = len(CHUNKS) - 1
    SA, CA, GA, SB, CB, GB = range(MODS)

    ctx = ExitStack()
    with ctx:
        def sb(name, shape, dt=f32, within=ctx):
            return within.enter_context(nc.sbuf_tensor(name, shape, dt))

        def sem(name):
            return ctx.enter_context(nc.semaphore(name))

        mod_dram = nc.dram_tensor("mod_dram", [B, MODS * C], f32, kind="Internal").ap()
        band_dram = nc.dram_tensor("band_dram", [H, BAND], f32, kind="Internal").ap()
        h2_dram = nc.dram_tensor("h2_dram", [B * T, C], f32, kind="Internal").ap()
        ye_dram = nc.dram_tensor("ye_dram", [B * T * 2, C], f32, kind="Internal").ap()

        ident = sb("ident", [P, P])
        xr = sb("xr", [P, NT, C])
        hn = sb("hn", [P, NT + TPB, C])
        mod = sb("mod", [P, B, MODS, C])
        bp_bc = sb("bp_bc", [P, C])
        gamma_bc = sb("gamma_bc", [P, C])
        beta_bc = sb("beta_bc", [P, C])
        br_bc = sb("br_bc", [P, E])
        b2_bc = sb("b2_bc", [P, E, C])
        wr_sb = sb("wr_sb", [P, E])
        b1_sb = sb("b1_sb", [P, E, FT])
        stats = sb("stats", [P, NT, 6])
        mv = sb("mv", [P, NT, 2])
        rstd = sb("rstd", [P, NT])
        nwt = sb("nwt", [P, 3, NT])
        lg = sb("lg", [P, TPB + NT, E])
        zeros = sb("zeros", [P, C])

        rt = sb("rt", [P, 13, NT, E])
        LG2, OH1, OH2, SCORE, KEY, SEL, SLOT, MASKED, PREF, EQF, TMP, TMP2, LOWFIRST = range(13)
        rv = sb("rv", [P, 14, NT])
        M1, M2, BEST, E1, W0, W1_, SL, SL2, SE, SE2, G1, G2, ONEP, SPARE = range(14)
        masks = sb("masks", [P, 2, NT, E], bf16)
        ones_bf = sb("ones_bf", [P, P], bf16)
        before_bf = sb("before_bf", [P, P], bf16)
        cand = sb("cand", [P, 1 + CANDS, E], i32)
        incs = sb("incs", [P, CANDS, E], i32)
        passing = sb("passing", [P, NT, CANDS, E], bf16)
        best = sb("best", [P, 1 + CANDS, E])
        slot_base = sb("slot_base", [P, NT, E])
        ngt = sb("ngt", [P, E])
        ngt_bf = sb("ngt_bf", [P, E], bf16)
        slot_i = sb("slot_i", [P, 3, 2, NT], i32)
        slot_f = sb("slot_f", [P, 2, 2, NT])
        lane_iota = sb("lane_iota", [P, P])
        tile_iota = sb("tile_iota", [P, SLOT_TILES])
        digit = sb("digit", [P, 2, 2, NT])
        held = sb("held", [P, 2, SLOT_TILES])
        token_of = sb("token_of", [P, 2, SLOT_TILES], i32)
        row_of = sb("row_of", [P, SLOT_TILES], i32)

        HI, LO = 0, 1
        attn = ExitStack()
        A_r = sb("A_r", [P, 2, H, C], f32r, attn)
        G = sb("G", [P, H, C], f32, attn)
        bias_sb = sb("bias_sb", [P, H, T], f32, attn)
        S2 = sb("S2", [P, 2, HG, P + T], f32, attn)
        rowmin = sb("rowmin", [P, 2, 2 * HG], f32, attn)
        rowsum = sb("rowsum", [P, 2, 2 * HG], f32, attn)
        rowinv = sb("rowinv", [P, 2, 2 * HG], f32, attn)
        oT = sb("oT", [P, T], f32, attn)
        h2_cur = sb("h2_cur", [P, TPB, C], f32, attn)
        h2T = sb("h2T", [P, T], f32, attn)
        stats2 = sb("stats2", [P, TPB, 6], f32, attn)
        mv2 = sb("mv2", [P, TPB, 2], f32, attn)
        nw2 = sb("nw2", [P, 4, TPB], f32, attn)
        gtmp = sb("gtmp", [P, 2, TPB, C], f32, attn)
        h_cur = sb("h_cur", [P, TPB, C], f32, attn)
        hTk = sb("hTk", [P, 2, 2, T], f32r, attn)
        wvT = sb("wvT", [P, H // 2, C], f32, attn)
        wp_sb = sb("wp_sb", [P, H // 2, C], f32, attn)
        start = ExitStack()
        wqk = sb("wqk", [P, 2, H, D], f32, start)
        wqT = sb("wqT", [P, H // 2, C], f32, start)
        wkT = sb("wkT", [P, H // 2, C], f32, start)
        wmod_sb = sb("wmod_sb", [P, MODS * C], f32, start)
        modrow = sb("modrow", [B, MODS, C], f32, start)
        gsign = sb("gsign", [B, 2, C], f32, start)
        band = sb("band", [H, BAND], f32, start)
        wv = sb("wv", [P, H, D], f32, start)
        start.close()
        h_r = sb("h_r", [P, 2, 2, TPB, C], f32r, attn)
        hTq = sb("hTq", [P, 2, 2, T], f32r, attn)
        kT = sb("kT", [P, 2, 2, HG, T], f32r, attn)
        uT = sb("uT", [P, 2, HG, T], f32, attn)
        pT0 = sb("pT0", [P, 2, 2, HG, T], f32r, attn)
        pT1 = sb("pT1", [P, 2, 2, HG, P], f32r, attn)
        tabT = sb("tabT", [H, 2 * REL + 1], f32, attn)
        cT = sb("cT", [P, B], f32, attn)
        silu = sb("silu", [P, 3, B], f32, attn)
        attn.close()

        w1_sb = sb("w1_sb", [P, E, F])
        w2_sb = sb("w2_sb", [P, E, FT, C])
        y_got = sb("y_got", [P, NT, 2, C])
        lane_is = sb("lane_is", [P, 2, NT, P], bf16)
        tile_is = sb("tile_is", [P, 2, NT, SLOT_TILES])
        tile_val = sb("tile_val", [P, 2, NT, 2, SLOT_TILES], bf16)
        xe_sb = sb("xe_sb", [P, E // 2, PAIR, C])
        xeT = sb("xeT", [P, E // 2, 2 * CAP])
        gT = sb("gT", [P, 2, FT, CAP])
        y_sb = sb("y_sb", [P, E // 2, PAIR, C])
        ggb = sb("ggb", [P, B, C])
        xgb = sb("xgb", [P, NT, C])
        out_sb = sb("out_sb", [P, NT, C])
        banks = ctx.enter_context(nc.psum_tensor("banks", [P, 8, 512], f32))
        KU, SP_, TP, OB, AUX, HT0 = (0, 1), (2, 3), (4, 5), 6, 7, 2

        ld_x0 = sem("ld_x0")
        ld_x, ld_w, ld_wp, ld_c, ld_mod, ld_tab, ld_small, ld_bias, st_band = (
            sem(n) for n in ("ld_x", "ld_w", "ld_wp", "ld_c", "ld_mod", "ld_tab", "ld_small",
                             "ld_bias", "st_band"))
        ld_w1, ld_w2 = sem("ld_w1"), sem("ld_w2")
        zero_set, zero_st = sem("zero_set"), sem("zero_st")
        id_set, id_made, band_made = sem("id_set"), sem("id_made"), sem("band_made")
        const_made = sem("const_made")
        silu_exp, silu_made = sem("silu_exp"), sem("silu_made")
        mod_ready, modrow_made, st_mod, ld_mod0, ld_modr = (
            sem(n) for n in ("mod_ready", "modrow_made", "st_mod", "ld_mod0", "ld_modr"))
        wt_ready, wt_high = sem("wt_ready"), sem("wt_high")
        wT_copied, wt_low, g_copied = sem("wT_copied"), sem("wt_low"), sem("g_copied")
        stats_made, hn_chain = sem("stats_made"), sem("hn_chain")
        hr_high, hr_low, hTk_high, hTq_made = sem("hr_high"), sem("hr_low"), sem("hTk_high"), sem("hTq_made")
        k_high, t_high = sem("k_high"), sem("t_high")
        hcur_made, hT_ready, hT_copied = sem("hcur_made"), sem("hT_ready"), sem("hT_copied")
        k_ready, k_copied = sem("k_ready"), sem("k_copied")
        s_ready, biased, expd, normed = sem("s_ready"), sem("biased"), sem("expd"), sem("normed")
        t_ready, t_copied = sem("t_ready"), sem("t_copied")
        u_ready, u_copied = sem("u_ready"), sem("u_copied")
        o_ready, oT_copied = sem("o_ready"), sem("oT_copied")
        oN_ready, h2_made = sem("oN_ready"), sem("h2_made")
        h2T_ready, h2T_copied = sem("h2T_ready"), sem("h2T_copied")
        lg_ready, lg_copied = sem("lg_ready"), sem("lg_copied")
        inv_made = sem("inv_made")
        dve_chain = sem("dve_chain")
        ln2_pool, ln2_dve = sem("ln2_pool"), sem("ln2_dve")
        attn_made, x2_made, norm2_made, h2_kept = (
            sem("attn_made"), sem("x2_made"), sem("norm2_made"), sem("h2_kept"))
        top_made, e1_made = sem("top_made"), sem("e1_made")
        search_chain, compared, count_ready = sem("search_chain"), sem("compared"), sem("count_ready")
        masks_made, prefix_ready = sem("masks_made"), sem("prefix_ready")
        sel_made, pos_ready = sem("sel_made"), sem("pos_ready")
        ld_xe = [sem(f"ld_xe{e}") for e in range(E)]
        st_h2, y_sent = sem("st_h2"), sem("y_sent")
        tiles_known, val_made, lanes_made = sem("tiles_known"), sem("val_made"), sem("lanes_made")
        held_ready, token_made, row_made = sem("held_ready"), sem("token_made"), sem("row_made")
        ld_y = [sem(f"ld_y{s}") for s in range(len(CHUNKS))]
        ggb_made, gates_made, fin_gated, fin_main, fin_chain, fin_stats, fin_norm, scaled_pool, scaled_dve = (
            sem(n) for n in ("ggb_made", "gates_made", "fin_gated", "fin_main", "fin_chain", "fin_stats",
                             "fin_norm", "scaled_pool", "scaled_dve"))
        x_ready, x_copied = sem("x_ready"), sem("x_copied")
        f_ready, gelu_done = sem("f_ready"), sem("gelu_done")
        y_ready, y_copied = sem("y_ready"), sem("y_copied")
        out_made, last_made, st_out = sem("out_made"), sem("last_made"), sem("st_out")
        last_norm = sem("last_norm")

        block = ctx.enter_context(nc.Block())

        def both(ap):
            return ap.unsqueeze(1).to_broadcast([P, TPB, C])

        LAG_S, LAG_T, LAG_U, LAG_O = 2, 3, 4, 5
        TRANSPOSES, G_IN_STEP = (0, 1, 2, 3, 8, 9), ((), (8, 9), (10, 11, 12), (13,))
        CONSTS = 9 + CANDS
        W_BANK = (4, 5, 6, 7, 4, 5, 6, 7, 4, 5, 6, 4, 5, 6)
        STEPS = GROUPS + 2 * NHG + 1

        def each_slot_tile(ap):
            return ap.unsqueeze(3).to_broadcast([P, 2, NT, SLOT_TILES])

        def to_output(eng, tensor_tensor, s, normed_, scaled, made):
            lo, hi = CHUNKS[s]
            part = hn[:, lo:hi, :].rearrange("p (b t) n -> p b t n", t=TPB)
            eng.wait_ge(*normed_)
            tensor_tensor(part, part, ggb[:, lo // TPB:hi // TPB, :].unsqueeze(2)
                          .to_broadcast([P, (hi - lo) // TPB, TPB, C]), op=ALU.mult).then_inc(scaled, 1)
            eng.wait_ge(scaled, s % LAST + 1)
            tensor_tensor(out_sb[:, lo:hi, :], hn[:, lo:hi, :], xgb[:, lo:hi, :], op=ALU.add).then_inc(made, 1)

        def y_tiles(e):
            whole, mid = PAIR // 2, PAIR // 2
            if e % 2 == 0:
                return [(t, 0, P) for t in range(whole)] + [(mid, 0, HALF)]
            return [(mid, HALF, P)] + [(t, 0, P) for t in range(mid + 1, PAIR)]

        def flip(ap):
            return ap.rearrange("p (t n) -> p t n", n=P)[:, :, ::-1]

        def heads_of(q):
            k = (q - 4) if q < 8 else (q - 10)
            return slice(k % 2 + 8 * (k // 2), k % 2 + 8 * (k // 2) + 7, 2)

        class Links:

            def __init__(self, eng, chain, base=0, alone=False):
                self.eng, self.chain, self.count, self.alone = eng, chain, base, alone

            def __call__(self, ins):
                self.count = self.count + 1
                ins.then_inc(self.chain, 1)
                self.eng.wait_ge(self.chain, reached(self.eng, self.count) if self.alone else self.count)

        wait_register = {}

        def reached(eng, value):
            if isinstance(value, int):
                return value
            if eng not in wait_register:
                wait_register[eng] = eng.alloc_register("reached")
            eng.reg_mov(wait_register[eng], value)
            eng.wait_ge(id_made, 1)
            return wait_register[eng]

        def pT_part(r, a, k):
            part = pT1[:, r, a, :, :] if k == 2 else pT0[:, r, a, 2 * k:2 * k + 2, :]
            return part.rearrange("p h t -> p (h t)")

        def w_at(at):
            return at // NHG

        def has(at, lag):
            return 0 <= at - lag < GROUPS

        def attention(eng, step):
            for m in range(UNROLL):
                step(m, m, m // NHG)
            with eng.Fori(1, GROUPS // UNROLL) as i:
                for j in range(UNROLL):
                    step(UNROLL * i + j, UNROLL + j, 2 * i + j // NHG)
            for m in range(GROUPS, STEPS):
                step(m, m, m // NHG)

        @block.sync
        def _(sp):
            sp.dma_start(cT[:, :], c.rearrange("b k -> k b"), allow_slow_non_contiguous=True).then_inc(ld_c, 16)
            sp.dma_start(wmod_sb[:, :], wmod).then_inc(ld_mod, 16)
            sp.dma_start(wqk[:, 0, :, :], Wq.rearrange("h c d -> c h d")).then_inc(ld_w, 16)
            sp.dma_start(wqk[:, 1, :, :], Wk.rearrange("h c d -> c h d")).then_inc(ld_w, 16)
            x_tiles = x.rearrange("b (t p) n -> p (b t) n", p=P)
            sp.dma_start(xr[:, TPB:, :], x_tiles[:, TPB:, :]).then_inc(ld_x, 16)
            sp.wait_ge(modrow_made, 1)
            sp.dma_start(mod_dram, modrow[:, :, :].rearrange("b a n -> b (a n)")).then_inc(st_mod, 16)
            sp.wait_ge(band_made, 1)
            sp.dma_start(band_dram, band[:, :]).then_inc(st_band, 16)
            sp.wait_ge(st_mod, 16)
            sp.dma_start(mod[:, 0:2, :, :].rearrange("p b a n -> p b (a n)"), mod_dram[0:2, :].partition_broadcast(P)
                         ).then_inc(ld_mod0, 16)
            sp.wait_ge(st_band, 16)
            sp.dma_start(bias_sb[:, :, :], bass.AP(band_dram.tensor, 0, [[1, P], [BAND, H], [1, T]])
                         ).then_inc(ld_bias, 16)
            sp.dma_start(wv[:, :, :], Wv.rearrange("h c d -> c h d")).then_inc(ld_wp, 16)
            sp.dma_start(wp_sb[:, :, :], Wp.rearrange("(g p) n -> p g n", p=P)).then_inc(ld_wp, 16)
            sp.dma_start(mod[:, 2:, :, :].rearrange("p b a n -> p b (a n)"), mod_dram[2:, :].partition_broadcast(P)
                         ).then_inc(ld_modr, 16)
            for dst, src in ((gamma_bc, gamma), (beta_bc, beta), (br_bc, br)):
                sp.dma_start(dst[:, :], src.partition_broadcast(P)).then_inc(ld_small, 16)
            sp.dma_start(b2_bc[:, :, :], b2.partition_broadcast(P)).then_inc(ld_small, 16)
            sp.dma_start(wr_sb[:, :], Wr).then_inc(ld_small, 16)
            sp.dma_start(b1_sb[:, :, :], b1.rearrange("e (f p) -> p e f", p=P), allow_slow_non_contiguous=True
                         ).then_inc(ld_small, 16)
            sp.wait_ge(zero_set, 1)
            sp.dma_start(ye_dram.rearrange("(p a) n -> p a n", p=P),
                         zeros[:, :].unsqueeze(1).to_broadcast([P, 2 * NT, C])).then_inc(zero_st, 16)

            sp.wait_ge(h2_kept, B)
            sp.dma_start(h2_dram.rearrange("(t p) n -> p t n", p=P), hn[:, 0:NT, :]).then_inc(st_h2, 16)
            sp.wait_ge(lg_copied, B + 1)
            sp.dma_start(w1_sb[:, :, :], W1.rearrange("e c f -> c e f")).then_inc(ld_w1, 16)
            sp.dma_start(w2_sb[:, :, :, :], W2.rearrange("e (f p) c -> p e f c", p=P)).then_inc(ld_w2, 16)
            sp.wait_ge(y_sent, 16 * PAIR * E // 2)
            by_token = ye_dram.rearrange("(t p k) n -> p t k n", p=P, k=2)
            for s, (lo, hi) in enumerate(CHUNKS):
                sp.dma_start(y_got[:, lo:hi, :, :], by_token[:, lo:hi, :, :]).then_inc(ld_y[s], 16)
            out_tiles = out.rearrange("b (t p) n -> p (b t) n", p=P)
            for s, (lo, hi) in enumerate(CHUNKS):
                if s < LAST:
                    sp.wait_ge(out_made, s + 1)
                else:
                    sp.wait_ge(last_made, 1)
                sp.dma_start(out_tiles[:, lo:hi, :], out_sb[:, lo:hi, :]).then_inc(st_out, 16)
            sp.wait_ge(st_out, 16 * len(CHUNKS))

        @block.gpsimd
        def _(pool):
            nc.gpsimd.memset(ident[:, :], 0.0).then_inc(id_set, 1)
            nc.gpsimd.memset(ones_bf[:, :], 1.0).then_inc(const_made, 1)
            pool.wait_ge(id_set, 1)
            nc.gpsimd.affine_select(out=ident[:, :], in_=ident[:, :], compare_op=ALU.not_equal,
                                    fill=1.0, base=0, pattern=[[-1, P]], channel_multiplier=1
                                    ).then_inc(id_made, 1)
            nc.gpsimd.memset(zeros[:, :], 0.0).then_inc(zero_set, 1)
            nc.gpsimd.memset(h2_cur[:, :, :], 0.0).then_inc(h2_made, 1)
            pool.wait_ge(const_made, 1)
            nc.gpsimd.affine_select(out=before_bf[:, :], in_=ones_bf[:, :], compare_op=ALU.is_gt,
                                    fill=0.0, base=0, pattern=[[1, P]], channel_multiplier=-1
                                    ).then_inc(const_made, 1)
            nc.gpsimd.iota(slot_base[:, :, :], [[0, NT], [CAP, E]], base=-TRASH, channel_multiplier=0,
                           allow_small_or_imprecise_dtypes=True).then_inc(const_made, 1)
            nc.gpsimd.iota(rt[:, LOWFIRST, :, :], [[0, NT], [-1, E]], base=E, channel_multiplier=0,
                           allow_small_or_imprecise_dtypes=True).then_inc(const_made, 1)
            small = dict(allow_small_or_imprecise_dtypes=True)
            nc.gpsimd.iota(lane_iota[:, :], [[1, P]], base=0, channel_multiplier=0, **small).then_inc(const_made, 1)
            nc.gpsimd.iota(tile_iota[:, :], [[1, SLOT_TILES]], base=0, channel_multiplier=0, **small
                           ).then_inc(const_made, 1)
            nc.gpsimd.iota(digit[:, 0, :, :], [[0, 2], [1, NT]], base=0, channel_multiplier=0, **small
                           ).then_inc(const_made, 1)
            nc.gpsimd.iota(digit[:, 1, :, :], [[1, 2], [0, NT]], base=1, channel_multiplier=2, **small
                           ).then_inc(const_made, 1)
            for j in range(CANDS):
                nc.gpsimd.memset(incs[:, j, :], (j + 1) << (BITS - DIGIT)).then_inc(const_made, 1)
            nc.gpsimd.memset(cand[:, 0, :], 0).then_inc(const_made, 1)

            t_ = nc.gpsimd.tensor_tensor

            def input_of(b):
                links = Links(pool, hn_chain, 4 * (b - 1))
                hb, xb = hn[:, 2 * b:2 * b + TPB, :], xr[:, 2 * b:2 * b + TPB, :]

                def each(ap):
                    return ap[:, 2 * b:2 * b + TPB].unsqueeze(2).to_broadcast([P, TPB, C])
                links(t_(hb, xb, each(mv[:, :, 0]), op=ALU.subtract))
                links(t_(hb, hb, each(rstd[:, :]), op=ALU.mult))
                links(t_(hb, hb, both(mod[:, b, CA, :]), op=ALU.mult))
                links(t_(hb, hb, both(mod[:, b, SA, :]), op=ALU.add))

            def step(m, at, w):
                if at == 0:
                    pool.wait_ge(stats_made, 1)
                    pool.wait_ge(ld_mod0, 16)
                if at == 1:
                    pool.wait_ge(ld_modr, 16)
                b = w - 2
                late = 2 <= w_at(at) <= B
                links = Links(pool, ln2_pool, LN2_POOL_LINKS * b, alone=True)

                def mods(k):
                    return mod[:, bass.ds(b, 1), k, :].to_broadcast([P, TPB, C])
                if at % NHG == 2 and late:
                    xb = xr[:, bass.ds(2 * b, TPB), :]
                    pool.wait_ge(attn_made, reached(pool, b + 1))
                    links(t_(gtmp[:, 1, :, :], gtmp[:, 0, :, :], mods(GA), op=ALU.mult))
                    t_(xb, xb, gtmp[:, 1, :, :], op=ALU.add).then_inc(x2_made, 1)
                if has(at, LAG_S):
                    n, r = m - LAG_S, at % 2
                    for k, (lo, hi) in enumerate(((0, P), (P, P + T))):
                        pool.wait_ge(inv_made, reached(pool, 2 * n + k + 1))
                        part = S2[:, r, :, lo:hi]
                        t_(part, part, rowinv[:, r, HG * k:HG * k + HG].unsqueeze(2)
                           .to_broadcast([P, HG, hi - lo]), op=ALU.mult).then_inc(normed, 1)
                if at % NHG == 0 and has(at, 0):
                    pool.wait_ge(hT_copied, reached(pool, w + 1))
                    if w_at(at) >= 2:
                        pool.wait_ge(s_ready, reached(pool, 3 * (m - 5) + 3))
                    for k in (HI, LO):
                        nc.gpsimd.tensor_copy(hTq[:, w_at(at) % 2, k, :].rearrange("p (t n) -> p t n", n=P),
                                              flip(hTk[:, w_at(at) % 2, k, :].bitcast(f32))).then_inc(hTq_made, 1)
                if at < B - 1:
                    input_of(at + 1)
                if at == B - 1:
                    nc.gpsimd.memset(hn[:, NT:, :], 0.0).then_inc(hn_chain, 4)
                if at % NHG == 3 and late:
                    links.count = LN2_POOL_LINKS * b + 1
                    pool.wait_ge(h2T_ready, reached(pool, w - 1))
                    pool.wait_ge(norm2_made, reached(pool, b + 1))
                    links(t_(gtmp[:, 1, :, :], gtmp[:, 0, :, :], mods(CB), op=ALU.mult))
                    t_(h2_cur[:, :, :], gtmp[:, 1, :, :], mods(SB), op=ALU.add).then_inc(h2_made, 1)
                    pool.wait_ge(h2_made, reached(pool, b + 2))
                    nc.gpsimd.tensor_copy(hn[:, bass.ds(2 * b, TPB), :], h2_cur[:, :, :]).then_inc(h2_kept, 1)
            attention(pool, step)

            pool.wait_ge(lg_copied, B + 1)
            pool.wait_ge(ld_small, 16 * 6)

            def per_batch(ap):
                return ap.unsqueeze(1).to_broadcast([P, B, C])
            t_(ggb[:, :, :], mod[:, :, GB, :], per_batch(gamma_bc[:, :]), op=ALU.mult).then_inc(ggb_made, 1)
            t_(out_sb[:, 0:B, :], mod[:, :, GB, :], per_batch(beta_bc[:, :]), op=ALU.mult).then_inc(ggb_made, 1)
            pool.wait_ge(ggb_made, 2)
            t_(xgb[:, :, :].rearrange("p (b t) n -> p b t n", t=TPB),
               xr[:, :, :].rearrange("p (b t) n -> p b t n", t=TPB),
               out_sb[:, 0:B, :].unsqueeze(2).to_broadcast([P, B, TPB, C]), op=ALU.add).then_inc(ggb_made, 1)
            pool.wait_ge(tiles_known, 1)
            for a in range(2):
                t_(tile_val[:, :, :, a, :], tile_is[:, :, :, :], each_slot_tile(digit[:, a, :, :]), op=ALU.mult
                   ).then_inc(val_made, 1)
            pool.wait_ge(st_h2, 16)
            pool.wait_ge(token_made, 1)
            for q in range(E // 2):
                for t in range(PAIR):
                    nc.gpsimd.indirect_dma_start(
                        out=xe_sb[:, q, t, :], out_offset=None, in_=h2_dram,
                        in_offset=bass.IndirectOffsetOnAxis(ap=token_of[:, 1, PAIR * q + t:PAIR * q + t + 1], axis=0),
                        bounds_check=B * T - 1, oob_is_err=False).then_inc(ld_xe[2 * q + (t > PAIR // 2)], 16)
            pool.wait_ge(row_made, 1)
            pool.wait_ge(zero_st, 16)
            for q in range(E // 2):
                for t in range(PAIR):
                    pool.wait_ge(y_copied, 4 * q + (1, 1, 3, 4, 4)[t])
                    nc.gpsimd.indirect_dma_start(
                        out=ye_dram, out_offset=bass.IndirectOffsetOnAxis(
                            ap=row_of[:, PAIR * q + t:PAIR * q + t + 1], axis=0),
                        in_=y_sb[:, q, t, :], in_offset=None, bounds_check=NOWHERE - 1, oob_is_err=False
                    ).then_inc(y_sent, 16)
            for s in range(LAST):
                to_output(pool, t_, s, (fin_norm, CHUNKS[s][1]), scaled_pool, out_made)

        @block.scalar
        def _(act):
            act.dma_start(xr[:, 0:TPB, :], x[0].rearrange("(t p) n -> p t n", p=P)).then_inc(ld_x0, 16)
            act.dma_start(tabT[:, :], rel_table.rearrange("r h -> h r"), allow_slow_non_contiguous=True).then_inc(ld_tab, 16)
            act.dma_start(bp_bc[:, :], bp.partition_broadcast(P)).then_inc(ld_tab, 16)
            act.wait_ge(ld_c, 16)
            nc.scalar.activation(silu[:, 0, :], cT[:, :], ACT.Exp, scale=-1.0).then_inc(silu_exp, 1)
            def weights_out(q):
                act.wait_ge(wt_ready, q + 1)
                src = banks[:, W_BANK[q], :]
                if q in TRANSPOSES:
                    dst = {0: wqT, 1: wkT, 4: wvT}[q // 2][:, 4 * (q % 2):4 * (q % 2) + 4, :]
                    nc.scalar.activation(dst.rearrange("p g n -> p (g n)"), src, ACT.Copy).then_inc(wT_copied, 1)
                else:
                    dst = A_r[:, HI, heads_of(q), :] if q < 8 else G[:, heads_of(q), :]
                    nc.scalar.activation(dst, src.rearrange("p (g n) -> p g n", g=4), ACT.Copy,
                                         scale=SCALE if q < 8 else 1.0).then_inc(wt_high if q < 8 else g_copied, 1)
            for q in range(8):
                weights_out(q)

            def step(m, at, w):
                def exps(ks):
                    if not has(at, LAG_S):
                        return
                    n, r = m - LAG_S, at % 2
                    for k in ks:
                        h = k % HG
                        part = S2[:, r, h, P:P + T] if k // HG else S2[:, r, h, 0:P]
                        act.wait_ge(biased, 2 * HG * n + k + 1)
                        nc.scalar.activation(part, part, ACT.Exp, scale=-1.0,
                                             bias=rowmin[:, r, k:k + 1],
                                             accum_out=rowsum[:, r, k:k + 1]).then_inc(expd, 1)

                def t_part(k):
                    if not has(at, LAG_T):
                        return
                    n, r = m - LAG_T, (at - LAG_T) % 2
                    act.wait_ge(t_ready, 3 * n + k + 1)
                    if at - LAG_T >= 2:
                        act.wait_ge(u_ready, 2 * (m - 5) + 2)
                    nc.scalar.activation(pT_part(r, HI, k), banks[:, TP[(3 * (at - LAG_T) + k) % 2], :],
                                         ACT.Copy).then_inc(t_high, 1)

                def u_part(k):
                    if not has(at, LAG_U):
                        return
                    n = m - LAG_U
                    act.wait_ge(u_ready, 2 * n + k + 1)
                    if at - LAG_U >= 2:
                        act.wait_ge(o_ready, m - 5)
                    nc.scalar.activation(uT[:, at % 2, 2 * k:2 * k + 2, :].rearrange("p h t -> p (h t)"),
                                         banks[:, KU[k], :], ACT.Copy).then_inc(u_copied, 1)

                exps((0, 1, 2, 3))
                u_part(0)
                t_part(0)
                exps((4, 5))
                u_part(1)
                t_part(1)
                exps((6, 7))
                t_part(2)
                if has(at, 0):
                    for k in range(2):
                        act.wait_ge(k_ready, 2 * m + k + 1)
                        if at >= 2:
                            act.wait_ge(s_ready, 3 * (m - 2) + 3)
                        nc.scalar.activation(
                            kT[:, at % 2, HI, 2 * k:2 * k + 2, :].rearrange("p h t -> p (h t)"),
                            banks[:, KU[k], :], ACT.Copy).then_inc(k_high, 1)
                if at < len(G_IN_STEP):
                    for q in G_IN_STEP[at]:
                        weights_out(q)
                if at % NHG == 0 and 2 <= w_at(at) < B + 2:
                    act.wait_ge(o_ready, m - 4)
                    nc.scalar.activation(oT[:, :].rearrange("p (t n) -> p t n", n=P),
                                         flip(banks[:, OB, 0:T]), ACT.Copy).then_inc(oT_copied, 1)
            attention(act, step)

            act.wait_ge(top_made, 1)
            nc.scalar.activation(rv[:, E1, :], rv[:, SPARE, :], ACT.Exp).then_inc(e1_made, 1)
            for e in range(E):
                for f in range(FT):
                    act.wait_ge(f_ready, FT * e + f + 1)
                    if e >= 2:
                        act.wait_ge(y_ready, e - 1)
                    nc.scalar.activation(gT[:, e % 2, f, :], banks[:, 2 + f, 0:CAP], ACT.Gelu,
                                         bias=b1_sb[:, e, f:f + 1]).then_inc(gelu_done, 1)
            act.wait_ge(gates_made, 1)
            for s, (lo, hi) in enumerate(CHUNKS):
                act.wait_ge(ld_y[s], 16)
                for t in range(lo, hi):
                    nc.scalar.activation(y_got[:, t, 1, :], y_got[:, t, 1, :], ACT.Identity,
                                         scale=rv[:, G2, t:t + 1]).then_inc(fin_gated, 1)
            for s, (lo, hi) in enumerate(CHUNKS[:LAST]):
                act.wait_ge(fin_stats, s + 1)
                for t in range(lo, hi):
                    nc.scalar.activation(hn[:, t, :], hn[:, t, :], ACT.Identity, scale=rstd[:, t:t + 1],
                                         bias=rv[:, SPARE, t:t + 1]).then_inc(fin_norm, 1)

        @block.tensor
        def _(pe):
            mm, tr = nc.tensor.matmul, nc.tensor.transpose
            pe.wait_ge(const_made, CONSTS)
            pe.wait_ge(id_made, 1)
            def weights(q):
                if q in TRANSPOSES:
                    pe.wait_ge(ld_w if q < 4 else ld_wp, 32)
                    if q >= 8:
                        pe.wait_ge(wt_low, 2)
                    w_ = wqk[:, q // 2, :, :] if q < 4 else wv[:, :, :]
                elif q < 8:
                    pe.wait_ge(wT_copied, 4)
                else:
                    pe.wait_ge(wT_copied, 6)
                    pe.wait_ge(wt_low, 4)
                    if q == 13:
                        pe.wait_ge(g_copied, 1)
                for g in range(4):
                    out_ = banks[:, W_BANK[q], g * P:(g + 1) * P]
                    if q in TRANSPOSES:
                        gg = 4 * (q % 2) + g
                        last = tr(out_, w_[:, 2 * gg:2 * gg + 2, :].rearrange("p h d -> p (h d)"), ident[:, :])
                        continue
                    h = range(H)[heads_of(q)][g]
                    lo = D * (h % 2)
                    l, r = (wkT, wqT) if q < 8 else (wvT, wp_sb)
                    last = mm(out_, l[lo:lo + D, h // 2, :], r[lo:lo + D, h // 2, :], start=True, stop=True)
                last.then_inc(wt_ready, 1)
            pe.wait_ge(silu_made, 1)
            pe.wait_ge(ld_mod, 16)
            for k, (lo, hi) in enumerate(((0, 512), (512, MODS * C))):
                mm(banks[0:B, k, 0:hi - lo], silu[:, 1, :], wmod_sb[:, lo:hi],
                   start=True, stop=True).then_inc(mod_ready, 1)
            for q in range(8):
                weights(q)
            pe.wait_ge(hcur_made, 1)
            for t in range(TPB):
                last = tr(banks[:, HT0, t * P:(t + 1) * P], h_cur[:, t, :], ident[:, :])
            last.then_inc(hT_ready, 1)

            def mm3(out_, l, r, start, stop):
                mm(out_, l(HI), r(HI), start=start, stop=False)
                mm(out_, l(HI), r(LO), start=False, stop=False)
                return mm(out_, l(LO), r(HI), start=False, stop=stop)

            def step(m, at, w):
                def scores(k):
                    if not has(at, LAG_S):
                        return
                    n, r, par = m - LAG_S, at % 2, (at - LAG_S) // NHG % 2
                    if k == 0:
                        pe.wait_ge(k_copied, 2 * n + 2)
                        if (at - LAG_S) % NHG == 0:
                            pe.wait_ge(hTq_made, 2 * w + 2)
                    if at - LAG_S > 0 or k == 2:
                        pe.wait_ge(biased, 8 * n + (-2, 0, 4)[k])
                    tile = 0 if k == 0 else 1
                    mm3(banks[:, SP_[(3 * at + k) % 2], :],
                        lambda a: hTq[:, par, a, tile * P:(tile + 1) * P],
                        lambda a: kT[:, r, a, :, 0:P] if k == 0 else kT[:, r, a, 2 * k - 2:2 * k, :],
                        True, True).then_inc(s_ready, 1)

                def transposed(k):
                    if not has(at, LAG_T):
                        return
                    n, r = m - LAG_T, (at - LAG_T) % 2
                    if k == 0:
                        pe.wait_ge(normed, 2 * n + 2)
                    if at == LAG_T and k < 2:
                        pe.wait_ge(g_copied, 2 + k)
                    if at - LAG_T > 0 or k == 2:
                        pe.wait_ge(t_copied, 3 * n + k - 1)
                    for q in range(4):
                        if k < 2:
                            h, t = 2 * k + q // 2, q % 2
                            src = S2[:, r, h, 0:P] if t == 0 else S2[:, r, h, P:2 * P]
                        else:
                            src = S2[:, r, q, 2 * P:3 * P]
                        last = tr(banks[:, TP[(3 * (at - LAG_T) + k) % 2], q * P:(q + 1) * P], src, ident[:, :])
                    last.then_inc(t_ready, 1)

                def weighted(k):
                    if not has(at, LAG_U):
                        return
                    n, r, par = m - LAG_U, at % 2, (at - LAG_U) // NHG % 2
                    if k == 0:
                        if (at - LAG_U) % NHG == 0:
                            pe.wait_ge(hr_low, w)
                        pe.wait_ge(t_copied, 3 * n + 3)
                    if has(at, 1):
                        pe.wait_ge(k_copied, 2 * (m - 1) + k + 1)
                    else:
                        pe.wait_ge(u_copied, 2 * (m - 5) + k + 1)
                    mm3(banks[:, KU[k], :], lambda a: h_r[:, par, a, 0, :],
                        lambda a: pT0[:, r, a, 2 * k:2 * k + 2, :], True, False)
                    mm3(banks[:, KU[k], :].rearrange("p (h t) -> p h t", h=2)[:, :, P:T],
                        lambda a: h_r[:, par, a, 1, :],
                        lambda a: pT1[:, r, a, 2 * k:2 * k + 2, :], False, True).then_inc(u_ready, 1)

                def h2_transposed(here):
                    if not here or at % NHG or w_at(at) < 2:
                        return
                    pe.wait_ge(h2_made, w - 1)
                    if w_at(at) < B:
                        pe.wait_ge(hT_copied, w + 1)
                    for t in range(TPB):
                        last = tr(banks[:, AUX, t * P:(t + 1) * P], h2_cur[:, t, :], ident[:, :])
                    last.then_inc(h2T_ready, 1)

                if at == 2 * NHG - 1:
                    pe.wait_ge(ld_small, 16 * 6)
                scores(0)
                scores(1)
                weighted(0)
                transposed(0)
                scores(2)
                weighted(1)
                transposed(1)
                h2_transposed(at < GROUPS)
                if at % NHG == 1 and w_at(at) >= 2:
                    pe.wait_ge(oT_copied, w - 1)
                    pe.wait_ge(lg_copied, w - 1)
                    for t in range(TPB):
                        last = tr(banks[:, AUX, T + t * P:T + (t + 1) * P], oT[:, t * P:(t + 1) * P],
                                  ident[:, :])
                    last.then_inc(oN_ready, 1)
                if has(at, LAG_O):
                    n, r, g = m - LAG_O, (at - LAG_O) % 2, (at - LAG_O) % NHG
                    if at == LAG_O:
                        pe.wait_ge(g_copied, 4)
                    pe.wait_ge(u_copied, 2 * n + 2)
                    if g == 0 and w_at(at) >= 2:
                        pe.wait_ge(oT_copied, w - 1)
                    for j in range(HG):
                        last = mm(banks[:, OB, 0:T], G[:, HG * g + j, :], uT[:, r, j, :],
                                  start=g == 0 and j == 0, stop=g == NHG - 1 and j == HG - 1)
                    last.then_inc(o_ready, 1)
                transposed(2)
                h2_transposed(GROUPS <= at)
                if at % NHG == 2 and w_at(at) < B:
                    pe.wait_ge(hcur_made, w + 2)
                    pe.wait_ge(hT_copied, w + 1)
                    if w_at(at) >= 2:
                        pe.wait_ge(attn_made, w - 1)
                    for t in range(TPB):
                        last = tr(banks[:, AUX, t * P:(t + 1) * P], h_cur[:, t, :], ident[:, :])
                    last.then_inc(hT_ready, 1)
                if has(at, 0):
                    if at % NHG == 0:
                        pe.wait_ge(hT_copied, w + 1)
                    if at == 0:
                        pe.wait_ge(wt_low, 4)
                    for k in range(2):
                        if has(at, LAG_U):
                            pe.wait_ge(u_copied, 2 * (m - LAG_U) + k + 1)
                        elif at >= 1:
                            pe.wait_ge(k_copied, 2 * (m - 1) + k + 1)
                        for j in range(2):
                            last = mm3(banks[:, KU[k], j * T:(j + 1) * T],
                                       lambda a: A_r[:, a, HG * (at % NHG) + 2 * k + j, :],
                                       lambda a: hTk[:, w_at(at) % 2, a, :], True, True)
                        last.then_inc(k_ready, 1)
                if at < len(G_IN_STEP):
                    for q in G_IN_STEP[at]:
                        weights(q)
                if at % NHG == 0 and w_at(at) >= 2:
                    pe.wait_ge(h2T_copied, w - 1)
                    for t in range(TPB):
                        last = mm(banks[:, AUX, T + t * E:T + (t + 1) * E], h2T[:, t * P:(t + 1) * P],
                                  wr_sb[:, :], start=True, stop=True)
                    last.then_inc(lg_ready, 1)
            attention(pe, step)

            with pe.Fori(0, ROUNDS // ROUND_UNROLL) as i:
                for u in range(ROUND_UNROLL):
                    for t in range(NT):
                        if t in (0, SEARCH_SPLIT):
                            pe.wait_ge(compared, 2 * (ROUND_UNROLL * i + u) + 1 + (t > 0))
                        last = mm(banks[:, 0, 0:CANDS * E], ones_bf[:, :],
                                  passing[:, t, :, :].rearrange("p a e -> p (a e)"),
                                  start=t == 0, stop=t == NT - 1)
                    last.then_inc(count_ready, 1)

            def prefix(bank, mask):
                out_ = banks[:, bank, 0:NT * E].rearrange("p (t e) -> p t e", e=E)
                last = mm(out_, before_bf[:, :], mask, start=True, stop=False)
                for t in range(NT - 1):
                    last = mm(out_[:, t + 1:, :], ones_bf[:, :],
                              mask[:, t:t + 1, :].to_broadcast([P, NT - 1 - t, E]),
                              start=False, stop=t == NT - 2)
                return last

            pe.wait_ge(masks_made, 1)
            prefix(1, masks[:, 1, :, :])
            mm(banks[:, 2, 0:E], ones_bf[:, :], ngt_bf[:, :], start=True, stop=True
               ).then_inc(prefix_ready, 1)
            pe.wait_ge(sel_made, 1)
            prefix(3, masks[:, 0, :, :]).then_inc(pos_ready, 1)

            pe.wait_ge(val_made, 2)
            for c4 in range(2 * NT // 4):
                pe.wait_ge(lanes_made, c4 + 1)
                for i in range(4 * c4, 4 * c4 + 4):
                    k, t = divmod(i, NT)
                    last = mm(banks[:, 4, 0:2 * SLOT_TILES], lane_is[:, k, t, :],
                              tile_val[:, k, t, :, :].rearrange("p a s -> p (a s)"),
                              start=i == 0, stop=i == 2 * NT - 1)
            last.then_inc(held_ready, 1)

            def expert_in(e):
                q, tiles = e // 2, range(PAIR // 2 + 1) if e % 2 == 0 else range(PAIR // 2 + 1, PAIR)
                pe.wait_ge(ld_xe[e], 16 * len(tiles))
                if e >= 2:
                    pe.wait_ge(x_copied, e - 1)
                for t in tiles:
                    last = tr(banks[:, e % 2, (t - tiles[0]) * P:(t - tiles[0] + 1) * P], xe_sb[:, q, t, :], ident[:, :])
                last.then_inc(x_ready, 1)

            def first(e):
                pe.wait_ge(x_copied, e + 1)
                pe.wait_ge(ld_w1, 16)
                for f in range(FT):
                    if e >= 1:
                        pe.wait_ge(gelu_done, FT * (e - 1) + f + 1)
                    mm(banks[:, 2 + f, 0:CAP], w1_sb[:, e, f * P:(f + 1) * P],
                       xeT[:, e // 2, CAP * (e % 2):CAP * (e % 2 + 1)],
                       start=True, stop=True).then_inc(f_ready, 1)

            def second(e):
                pe.wait_ge(gelu_done, FT * (e + 1))
                pe.wait_ge(ld_w2, 16)
                if e >= 2:
                    pe.wait_ge(y_copied, 2 * (e - 2) + 2)
                for k, (tile, first_row, end_row) in enumerate(y_tiles(e)):
                    lo = tile * P + first_row - CAP * (e % 2)
                    for f in range(FT):
                        last = mm(banks[first_row:end_row, 6 + e % 2, k * C:(k + 1) * C],
                                  gT[:, e % 2, f, lo:lo + end_row - first_row], w2_sb[:, e, f, :],
                                  start=f == 0, stop=f == FT - 1)
                last.then_inc(y_ready, 1)
            for e in range(E + 1):
                if e < E:
                    expert_in(e)
                    first(e)
                if e >= 1:
                    second(e - 1)

        @block.vector
        def _(dve):
            v = nc.vector
            link = Links(dve, dve_chain)

            RSQRT_STEPS = 4 + 3 * NEWTON

            def rsqrt_step(j, out_, z, a, var, variance):
                if j == 0:
                    return v.tensor_scalar(var, variance, EPS, None, op0=ALU.add)
                if j == 1:
                    return v.tensor_scalar(a.bitcast(i32), var.bitcast(i32), 1, None, op0=ALU.logical_shift_right)
                if j == 2:
                    return v.tensor_scalar(z.bitcast(i32), a.bitcast(i32), -1.0, float(0x5f3759df),
                                           op0=ALU.mult, op1=ALU.add)
                k, part = divmod(j - 3, 3)
                if k == NEWTON:
                    return v.tensor_scalar(out_, z, (-0.5) ** NEWTON, None, op0=ALU.mult)
                if part == 0:
                    return v.scalar_tensor_tensor(a, z, 0.25 ** k, z, op0=ALU.mult, op1=ALU.mult)
                if part == 1:
                    return v.tensor_tensor(a, a, var, op=ALU.mult)
                return v.scalar_tensor_tensor(z, a, -3.0, z, op0=ALU.add, op1=ALU.mult)

            dve.wait_ge(silu_exp, 1)
            link(v.tensor_scalar(silu[:, 1, :], silu[:, 0, :], 1.0, None, op0=ALU.add))
            link(v.reciprocal(silu[:, 2, :], silu[:, 1, :]))
            v.tensor_tensor(silu[:, 1, :], cT[:, :], silu[:, 2, :], op=ALU.mult).then_inc(silu_made, 1)
            dve.wait_ge(mod_ready, 2)
            rows = modrow[:, :, :].rearrange("b a n -> b (a n)")
            v.tensor_copy(rows[:, 0:512], banks[0:B, 0, :])
            link(v.tensor_copy(rows[:, 512:MODS * C], banks[0:B, 1, 0:MODS * C - 512]))
            gates, scales = modrow[:, GA:MODS:GB - GA, :], modrow[:, CA:MODS:CB - CA, :]
            link(v.tensor_scalar(scales, scales, 1.0, None, op0=ALU.add))
            link(v.tensor_scalar(gsign[:, :, :], gates, 0.0, 2.0, op0=ALU.is_ge, op1=ALU.mult))
            link(v.scalar_tensor_tensor(gates, gates, -1.0, gates, op0=ALU.mult, op1=ALU.max))
            link(v.tensor_scalar(gates, gates, 0.25, None, op0=ALU.max))
            v.scalar_tensor_tensor(gates, gsign[:, :, :], -1.0, gates, op0=ALU.add, op1=ALU.mult
                                   ).then_inc(modrow_made, 1)
            dve.wait_ge(ld_tab, 32)
            far = T - REL - 1
            link(v.memset(band[:, far:], NEG))
            link(v.tensor_copy(band[:, 0:far], tabT[:, 0:1].to_broadcast([H, far])))
            v.tensor_copy(band[:, far:far + REL + 1], tabT[:, 0:REL + 1]).then_inc(band_made, 1)
            dve.wait_ge(ld_x0, 16)
            dve.wait_ge(ld_x, 16)
            for t in range(NT):
                last = v.bn_stats(stats[:, t, :], xr[:, t, :])
            link(last)
            for t in range(NT):
                last = v.bn_aggr(mv[:, t, :], stats[:, t, :])
            link(last)
            for j in range(RSQRT_STEPS):
                last = rsqrt_step(j, rstd[:, :], nwt[:, 1, :], nwt[:, 2, :], nwt[:, 0, :], mv[:, :, 1])
                if j < RSQRT_STEPS - 1:
                    link(last)
            last.then_inc(stats_made, 1)
            dve.wait_ge(stats_made, 1)

            def weight_low(q):
                dve.wait_ge(wt_high, q - 3)
                v.scalar_tensor_tensor(A_r[:, LO, heads_of(q), :],
                                       banks[:, W_BANK[q], :].rearrange("p (g n) -> p g n", g=4),
                                       SCALE, A_r[:, HI, heads_of(q), :].bitcast(f32),
                                       op0=ALU.mult, op1=ALU.subtract).then_inc(wt_low, 1)
            dve.wait_ge(ld_mod0, 16)
            for t in range(TPB):
                last = v.tensor_scalar(hn[:, t, :], xr[:, t, :], mv[:, t, 0:1], rstd[:, t:t + 1],
                                       op0=ALU.subtract, op1=ALU.mult)
            link(last)
            link(v.tensor_tensor(hn[:, 0:TPB, :], hn[:, 0:TPB, :], both(mod[:, 0, CA, :]), op=ALU.mult))
            v.tensor_tensor(h_cur[:, :, :], hn[:, 0:TPB, :], both(mod[:, 0, SA, :]), op=ALU.add
                            ).then_inc(hcur_made, 1)
            for q in range(4, 8):
                weight_low(q)
            dve.wait_ge(hT_ready, 1)
            v.tensor_copy(hTk[:, 0, HI, :], banks[:, HT0, 0:T]).then_inc(hTk_high, 1)
            dve.wait_ge(hTk_high, 1)
            v.tensor_tensor(hTk[:, 0, LO, :], banks[:, HT0, 0:T], hTk[:, 0, HI, :].bitcast(f32),
                            op=ALU.subtract).then_inc(hT_copied, 1)

            LN2_STEPS = 3 + RSQRT_STEPS
            PLACES = 10

            def ln2(at, w, place):
                k = PLACES * (at % NHG - 2) + place
                if at % NHG < 2 or w_at(at) < 2 or k >= LN2_STEPS:
                    return
                b = w - 2
                if k == 0:
                    dve.wait_ge(x2_made, reached(dve, b + 1))
                    for t in range(TPB):
                        last = v.bn_stats(stats2[:, t, :], xr[:, bass.ds(2 * b + t, 1), :])
                    last.then_inc(ln2_dve, 1)
                    return
                dve.wait_ge(ln2_dve, reached(dve, (LN2_STEPS - 1) * b + k))
                if k == 1:
                    for t in range(TPB):
                        last = v.bn_aggr(mv2[:, t, :], stats2[:, t, :])
                    last.then_inc(ln2_dve, 1)
                elif k < LN2_STEPS - 1:
                    rsqrt_step(k - 2, nw2[:, 1, :], nw2[:, 1, :], nw2[:, 2, :], nw2[:, 3, :], mv2[:, :, 1]
                               ).then_inc(ln2_dve, 1)
                else:
                    for t in range(TPB):
                        last = v.tensor_scalar(gtmp[:, 0, t, :], xr[:, bass.ds(2 * b + t, 1), :],
                                               mv2[:, t, 0:1], nw2[:, 1, t:t + 1], op0=ALU.subtract, op1=ALU.mult)
                    last.then_inc(norm2_made, 1)

            def step(m, at, w):
                def bias(k):
                    if not has(at, LAG_S):
                        return
                    n, r, g = m - LAG_S, at % 2, (at - LAG_S) % NHG
                    if at - LAG_S >= 2 and k == 0:
                        dve.wait_ge(t_ready, 3 * (m - 4) + 3)
                    bank = SP_[(3 * at + k) % 2]
                    dve.wait_ge(s_ready, reached(dve, 3 * n + k + 1))
                    if k == 0:
                        parts = [(banks[:, bank, h * P:(h + 1) * P], S2[:, r, h, 0:P],
                                  bias_sb[:, HG * g + h, P:T], h) for h in range(HG)]
                    else:
                        parts = [(banks[:, bank, (h % 2) * T:(h % 2 + 1) * T], S2[:, r, h, P:P + T],
                                  bias_sb[:, HG * g + h, :], HG + h) for h in (2 * k - 2, 2 * k - 1)]
                    for src, dst, row, col in parts:
                        v.tensor_tensor_reduce(out=dst, in0=src, in1=row, scale=-1.0, scalar=3e38,
                                               op0=ALU.add, op1=ALU.min,
                                               accum_out=rowmin[:, r, col:col + 1]).then_inc(biased, 1)

                def low(dst, src, high):
                    return v.tensor_tensor(dst, src, high.bitcast(f32), op=ALU.subtract)

                def t_low(k):
                    if not has(at, LAG_T):
                        return
                    n, r = m - LAG_T, (at - LAG_T) % 2
                    dve.wait_ge(t_high, 3 * n + k + 1)
                    low(pT_part(r, LO, k), banks[:, TP[(3 * (at - LAG_T) + k) % 2], :], pT_part(r, HI, k)
                        ).then_inc(t_copied, 1)

                def inverse(k):
                    if not has(at, LAG_S):
                        return
                    n, r, part = m - LAG_S, at % 2, slice(HG * k, HG * k + HG)
                    dve.wait_ge(expd, 2 * HG * n + HG * (k + 1))
                    v.reciprocal(rowinv[:, r, part], rowsum[:, r, part]).then_inc(inv_made, 1)

                new = at % NHG == 2 and w_at(at) < B
                par = (w_at(at) + 1) % 2
                if new:
                    dve.wait_ge(hn_chain, 4 * (w + 1))
                    dve.wait_ge(hT_ready, w + 1)
                    dve.wait_ge(hr_low, w + 1)
                    v.tensor_copy(h_cur[:, :, :], hn[:, bass.ds(2 * (w + 1), TPB), :]).then_inc(hcur_made, 1)
                if at == LAG_S:
                    dve.wait_ge(ld_bias, 16)
                if at == 2 * NHG - 1:
                    dve.wait_ge(ld_small, 16 * 6)
                bias(0)
                bias(1)
                ln2(at, w, 0)
                if at % NHG == 1 and has(at, 0):
                    if w_at(at) >= 2:
                        dve.wait_ge(u_ready, 2 * (m - 6) + 2)
                    v.tensor_copy(h_r[:, w_at(at) % 2, HI, :, :], h_cur[:, :, :]).then_inc(hr_high, 1)
                bias(2)
                ln2(at, w, 1)
                if at % NHG == 1 and has(at, 0):
                    dve.wait_ge(hr_high, w + 1)
                    low(h_r[:, w_at(at) % 2, LO, :, :], h_cur[:, :, :], h_r[:, w_at(at) % 2, HI, :, :]
                        ).then_inc(hr_low, 1)
                ln2(at, w, 2)
                t_low(0)
                ln2(at, w, 3)
                inverse(0)
                ln2(at, w, 4)
                t_low(1)
                if at % NHG == 0 and w_at(at) >= 2:
                    dve.wait_ge(h2T_ready, w - 1)
                    v.tensor_copy(h2T[:, :], banks[:, AUX, 0:T]).then_inc(h2T_copied, 1)
                ln2(at, w, 5)
                inverse(1)
                if at % NHG == 1 and w_at(at) >= 2:
                    dve.wait_ge(oN_ready, w - 1)
                    v.tensor_tensor(gtmp[:, 0, :, :],
                                    banks[:, AUX, T:2 * T].rearrange("p (t n) -> p t n", t=TPB),
                                    both(bp_bc[:, :]), op=ALU.add).then_inc(attn_made, 1)
                    if w_at(at) == B + 1:
                        xb = xr[:, NT - TPB:, :]
                        dve.wait_ge(attn_made, B)
                        link(v.tensor_tensor(gtmp[:, 1, :, :], gtmp[:, 0, :, :], both(mod[:, B - 1, GA, :]), op=ALU.mult))
                        v.tensor_tensor(xb, xb, gtmp[:, 1, :, :], op=ALU.add).then_inc(x2_made, 1)
                t_low(2)
                ln2(at, w, 6)
                if new:
                    dve.wait_ge(hT_ready, w + 2)
                    if w_at(at) >= 1:
                        dve.wait_ge(hTq_made, 2 * w)
                        dve.wait_ge(k_ready, 2 * (m - 3) + 2)
                    v.tensor_copy(hTk[:, par, HI, :], banks[:, AUX, 0:T]).then_inc(hTk_high, 1)
                if has(at, 0):
                    for k in range(2):
                        dve.wait_ge(k_high, 2 * m + k + 1)
                        part = [kT[:, at % 2, a, 2 * k:2 * k + 2, :].rearrange("p h t -> p (h t)")
                                for a in (HI, LO)]
                        low(part[LO], banks[:, KU[k], :], part[HI]).then_inc(k_copied, 1)
                        ln2(at, w, 7 + k)
                else:
                    ln2(at, w, 7)
                    ln2(at, w, 8)
                ln2(at, w, 9)
                if at % NHG == 3 and w_at(at) == B + 1:
                    dve.wait_ge(norm2_made, B)
                    dve.wait_ge(h2T_ready, B)
                    dve.wait_ge(h2_kept, B - 1)
                    link(v.tensor_tensor(gtmp[:, 1, :, :], gtmp[:, 0, :, :], both(mod[:, B - 1, CB, :]), op=ALU.mult))
                    v.tensor_tensor(h2_cur[:, :, :], gtmp[:, 1, :, :], both(mod[:, B - 1, SB, :]), op=ALU.add
                                    ).then_inc(h2_made, 1)
                    dve.wait_ge(h2_made, B + 1)
                    v.tensor_copy(hn[:, NT - TPB:NT, :], h2_cur[:, :, :]).then_inc(h2_kept, 1)
                if new:
                    dve.wait_ge(hTk_high, w + 2)
                    low(hTk[:, par, LO, :], banks[:, AUX, 0:T], hTk[:, par, HI, :]).then_inc(hT_copied, 1)
                if at % NHG == 0 and w_at(at) >= 2:
                    dve.wait_ge(lg_ready, w - 1)
                    v.tensor_tensor(lg[:, bass.ds(2 * (w - 2), TPB), :],
                                    banks[:, AUX, T:T + TPB * E].rearrange("p (t e) -> p t e", t=TPB),
                                    br_bc[:, :].unsqueeze(1).to_broadcast([P, TPB, E]),
                                    op=ALU.add).then_inc(lg_copied, 1)
            attention(dve, step)

            dve.wait_ge(lg_copied, B + 1)
            dve.wait_ge(h2_kept, B)
            dve.wait_ge(const_made, CONSTS)

            def r(k):
                return rt[:, k, :, :]

            def tok(k):
                return rv[:, k, :]

            def tok_e(k):
                return rv[:, k, :].unsqueeze(2).to_broadcast([P, NT, E])

            def best_expert(src, m_, oh):
                link(v.tensor_reduce(tok(m_), src, axis=X, op=ALU.max))
                link(v.tensor_tensor(r(SCORE), src, tok_e(m_), op=ALU.is_equal))
                link(v.tensor_tensor(r(TMP), r(SCORE), r(LOWFIRST), op=ALU.mult))
                link(v.tensor_reduce(tok(BEST), r(TMP), axis=X, op=ALU.max))
                link(v.tensor_tensor(r(oh), r(TMP), tok_e(BEST), op=ALU.is_equal))
            best_expert(lg[:, TPB:, :], M1, OH1)
            link(v.scalar_tensor_tensor(r(LG2), r(OH1), -3e38, lg[:, TPB:, :], op0=ALU.mult, op1=ALU.add))
            best_expert(r(LG2), M2, OH2)
            both_oh = rt[:, OH1:OH2 + 1, :, :]
            tmps = rt[:, TMP:TMP2 + 1, :, :]
            v.tensor_tensor(tok(SPARE), tok(M2), tok(M1), op=ALU.subtract).then_inc(top_made, 1)
            link(v.scalar_tensor_tensor(r(SCORE), r(OH1), -1.0, r(OH2), op0=ALU.add, op1=ALU.add))
            dve.wait_ge(e1_made, 1)
            link(v.tensor_scalar(tok(ONEP), tok(E1), 1.0, None, op0=ALU.add))
            link(v.reciprocal(tok(W0), tok(ONEP)))
            link(v.tensor_tensor(tok(W1_), tok(E1), tok(W0), op=ALU.mult))
            link(v.tensor_tensor(tmps, both_oh, rv[:, W0:W1_ + 1, :].unsqueeze(3).to_broadcast([P, 2, NT, E]),
                                 op=ALU.mult))
            link(v.tensor_tensor(r(TMP), r(TMP), r(TMP2), op=ALU.add))
            link(v.tensor_tensor(r(KEY), r(SCORE), r(TMP), op=ALU.add))
            SEARCH_LINKS = 5
            with dve.Fori(0, ROUNDS // ROUND_UNROLL) as i:
                linked = Links(dve, search_chain, SEARCH_LINKS * ROUND_UNROLL * i)
                for u in range(ROUND_UNROLL):
                    linked(v.tensor_tensor(cand[:, 1:, :], cand[:, 0:1, :].to_broadcast([P, CANDS, E]), incs[:, :, :],
                                           op=ALU.bitwise_or))
                    candf = cand[:, :, :].bitcast(f32)
                    for k in range(2):
                        part = (slice(0, SEARCH_SPLIT), slice(SEARCH_SPLIT, NT))[k]
                        tiles = part.stop - part.start
                        v.tensor_tensor(passing[:, part, :, :],
                                        r(KEY)[:, part, :].unsqueeze(2).to_broadcast([P, tiles, CANDS, E]),
                                        candf[:, 1:, :].unsqueeze(1).to_broadcast([P, tiles, CANDS, E]), op=ALU.is_ge
                                        ).then_inc(compared, 1)
                    linked(v.tensor_scalar(incs[:, :, :], incs[:, :, :], DIGIT, None, op0=ALU.logical_shift_right))
                    dve.wait_ge(count_ready, ROUND_UNROLL * i + u + 1)
                    cnt = banks[:, 0, 0:CANDS * E].rearrange("p (a e) -> p a e", a=CANDS)
                    linked(v.scalar_tensor_tensor(best[:, 1:, :], cnt, CAP - 0.5, candf[:, 1:, :],
                                                  op0=ALU.is_ge, op1=ALU.mult))
                    linked(v.tensor_reduce(best[:, 0, :], best[:, 1:, :].rearrange("p a e -> p e a"),
                                           axis=X, op=ALU.max))
                    linked(v.tensor_tensor(candf[:, 0, :], best[:, 0, :], candf[:, 0, :], op=ALU.max))
            thr = cand[:, 0, :].bitcast(f32).unsqueeze(1).to_broadcast([P, NT, E])
            link(v.tensor_tensor(r(MASKED), r(KEY), thr, op=ALU.is_gt))
            link(v.tensor_tensor(r(EQF), r(KEY), thr, op=ALU.is_equal))
            link(v.tensor_reduce(ngt[:, :], r(MASKED).rearrange("p t e -> p e t"), axis=X, op=ALU.add))
            link(v.tensor_copy(ngt_bf[:, :], ngt[:, :]))
            v.tensor_copy(masks[:, 1, :, :], r(EQF)).then_inc(masks_made, 1)
            dve.wait_ge(prefix_ready, 1)
            link(v.tensor_copy(ngt[:, :], banks[:, 2, 0:E]))
            pref = banks[:, 1, 0:NT * E].rearrange("p (t e) -> p t e", e=E)
            link(v.tensor_tensor(r(PREF), pref, ngt[:, :].unsqueeze(1).to_broadcast([P, NT, E]), op=ALU.add))
            link(v.scalar_tensor_tensor(r(TMP), r(PREF), CAP - 0.5, r(EQF), op0=ALU.is_lt, op1=ALU.mult))
            link(v.tensor_tensor(r(SEL), r(TMP), r(MASKED), op=ALU.add))
            v.tensor_copy(masks[:, 0, :, :], r(SEL)).then_inc(sel_made, 1)
            dve.wait_ge(pos_ready, 1)
            pos = banks[:, 3, 0:NT * E].rearrange("p (t e) -> p t e", e=E)
            link(v.tensor_tensor(r(SLOT), pos, slot_base[:, :, :], op=ALU.add))
            link(v.tensor_tensor(r(SLOT), r(SLOT), r(SEL), op=ALU.mult))
            def twice(k):
                return rt[:, k:k + 1, :, :].to_broadcast([P, 2, NT, E])
            link(v.tensor_tensor(tmps, both_oh, twice(SLOT), op=ALU.mult))
            link(v.tensor_reduce(rv[:, SL:SL2 + 1, :], tmps, axis=X, op=ALU.add))
            link(v.tensor_scalar(slot_i[:, 0, :, :], rv[:, SL:SL2 + 1, :], float(TRASH), None, op0=ALU.add))
            log_p = P.bit_length() - 1
            link(v.tensor_scalar(slot_i[:, 1, :, :], slot_i[:, 0, :, :], log_p, None, op0=ALU.logical_shift_right))
            link(v.tensor_scalar(slot_i[:, 2, :, :], slot_i[:, 0, :, :], P - 1, None, op0=ALU.bitwise_and))
            link(v.tensor_copy(slot_f[:, :, :, :], slot_i[:, 1:3, :, :]))
            v.tensor_tensor(tile_is[:, :, :, :], each_slot_tile(slot_f[:, 0, :, :]),
                            tile_iota[:, :].unsqueeze(1).unsqueeze(1).to_broadcast([P, 2, NT, SLOT_TILES]),
                            op=ALU.is_equal).then_inc(tiles_known, 1)
            for c4 in range(2 * NT // 4):
                k, t = divmod(4 * c4, NT)
                v.tensor_tensor(lane_is[:, k, t:t + 4, :],
                                slot_f[:, 1, k, t:t + 4].unsqueeze(2).to_broadcast([P, 4, P]),
                                lane_iota[:, :].unsqueeze(1).to_broadcast([P, 4, P]), op=ALU.is_equal
                                ).then_inc(lanes_made, 1)
            dve.wait_ge(held_ready, 1)
            high, low_ = (banks[:, 4, a * SLOT_TILES:(a + 1) * SLOT_TILES] for a in range(2))
            link(v.tensor_copy(held[:, 1, :], low_))
            link(v.scalar_tensor_tensor(held[:, 0, :], high, 2.0 * P, held[:, 1, :], op0=ALU.mult, op1=ALU.add))
            link(v.tensor_scalar(token_of[:, 0, :], held[:, 0, :], -1.0, 0.0, op0=ALU.add, op1=ALU.max))
            v.tensor_scalar(token_of[:, 1, :], token_of[:, 0, :], 1, None, op0=ALU.logical_shift_right
                            ).then_inc(token_made, 1)
            link(v.tensor_scalar(held[:, 1, :], held[:, 0, :], 0.5, NOWHERE + 1.0, op0=ALU.is_lt, op1=ALU.mult))
            v.scalar_tensor_tensor(row_of[:, :], held[:, 0, :], -1.0, held[:, 1, :], op0=ALU.add, op1=ALU.add
                                   ).then_inc(row_made, 1)
            link(v.tensor_tensor(tmps, both_oh, twice(SEL), op=ALU.mult))
            link(v.tensor_reduce(rv[:, SE:SE2 + 1, :], tmps, axis=X, op=ALU.add))
            v.tensor_tensor(rv[:, G1:G2 + 1, :], rv[:, W0:W1_ + 1, :], rv[:, SE:SE2 + 1, :], op=ALU.mult
                            ).then_inc(gates_made, 1)
            dve.wait_ge(gates_made, 1)

            for e in range(E + 1):
                if e < E:
                    lo, hi = (0, PAIR // 2 + 1) if e % 2 == 0 else (PAIR // 2 + 1, PAIR)
                    dve.wait_ge(x_ready, e + 1)
                    v.tensor_copy(xeT[:, e // 2, lo * P:hi * P], banks[:, e % 2, 0:(hi - lo) * P]).then_inc(x_copied, 1)
                if e >= 1:
                    d = e - 1
                    dve.wait_ge(y_ready, d + 1)
                    bank = banks[:, 6 + d % 2, 0:3 * C].rearrange("p (t n) -> p t n", t=3)
                    tiles = y_tiles(d)
                    for ks in ((0, 1), (2,)) if d % 2 == 0 else ((0,), (1, 2)):
                        tile, first_row, end_row = tiles[ks[0]]
                        v.tensor_tensor(y_sb[first_row:end_row, d // 2, tile:tile + len(ks), :],
                                        bank[first_row:end_row, ks[0]:ks[-1] + 1, :],
                                        b2_bc[first_row:end_row, d, :].unsqueeze(1)
                                        .to_broadcast([end_row - first_row, len(ks), C]), op=ALU.add
                                        ).then_inc(y_copied, 1)

            MAIN = 4

            def rstd_steps(s, first, end):
                part = slice(*CHUNKS[s])
                for j in range(first, end):
                    if j == 0:
                        dve.wait_ge(fin_main, MAIN * s + 4)
                    else:
                        dve.wait_ge(fin_chain, RSQRT_STEPS * s + j)
                    if j < RSQRT_STEPS:
                        rsqrt_step(j, rstd[:, part], nwt[:, 1, part], nwt[:, 2, part], nwt[:, 0, part],
                                   mv[:, part, 1]).then_inc(fin_chain, 1)
                    else:
                        v.scalar_tensor_tensor(rv[:, SPARE, part], mv[:, part, 0], -1.0, rstd[:, part],
                                               op0=ALU.mult, op1=ALU.mult).then_inc(fin_stats, 1)

            for s, (lo, hi) in enumerate(CHUNKS):
                places = 3 * (hi - lo) + 1

                def between(place):
                    if s > 0:
                        n = RSQRT_STEPS + 1
                        rstd_steps(s - 1, n * place // places, n * (place + 1) // places)
                dve.wait_ge(ld_y[s], 16)
                for i, t in enumerate(range(lo, hi)):
                    last = v.scalar_tensor_tensor(hn[:, t, :], y_got[:, t, 0, :], rv[:, G1, t:t + 1],
                                                  hn[:, t, :], op0=ALU.mult, op1=ALU.add)
                    if t == hi - 1:
                        last.then_inc(fin_main, 1)
                    between(i)
                dve.wait_ge(fin_gated, hi)
                dve.wait_ge(fin_main, MAIN * s + 1)
                v.tensor_tensor(hn[:, lo:hi, :], hn[:, lo:hi, :], y_got[:, lo:hi, 1, :], op=ALU.add).then_inc(fin_main, 1)
                between(hi - lo)
                dve.wait_ge(fin_main, MAIN * s + 2)
                for i, t in enumerate(range(lo, hi)):
                    last = v.bn_stats(stats[:, t, :], hn[:, t, :])
                    if t == hi - 1:
                        last.then_inc(fin_main, 1)
                    between(hi - lo + 1 + i)
                dve.wait_ge(fin_main, MAIN * s + 3)
                for i, t in enumerate(range(lo, hi)):
                    last = v.bn_aggr(mv[:, t, :], stats[:, t, :])
                    if t == hi - 1:
                        last.then_inc(fin_main, 1)
                    between(2 * (hi - lo) + 1 + i)
            rstd_steps(LAST, 0, RSQRT_STEPS)
            dve.wait_ge(fin_chain, RSQRT_STEPS * (LAST + 1))
            for t in range(*CHUNKS[LAST]):
                last = v.tensor_scalar(hn[:, t, :], hn[:, t, :], mv[:, t, 0:1], rstd[:, t:t + 1],
                                       op0=ALU.subtract, op1=ALU.mult)
            last.then_inc(last_norm, 1)
            dve.wait_ge(ggb_made, 3)
            to_output(dve, v.tensor_tensor, LAST, (last_norm, 1), scaled_dve, last_made)


_INS = ['L0_attn_x', 'L0_attn_Wq', 'L0_attn_Wk', 'L0_attn_Wv', 'L0_attn_Wp', 'L0_attn_bp',
        'L0_attn_rel_table', 'L0_ffn_Wr', 'L0_ffn_br', 'L0_ffn_W1', 'L0_ffn_b1', 'L0_ffn_W2',
        'L0_ffn_b2', 'L0_ffn_gamma', 'L0_ffn_beta', 'L0_c', 'L0_wmod']
_OUTS = [((8, 256, 128), 'float32')]


def kernel(**inputs):
    import numpy as _np
    import concourse.bacc as _bacc
    from concourse import mybir as _mybir
    from concourse.bass_utils import run_bass_kernel_spmd as _run

    nc = _bacc.Bacc("TRN2", target_bir_lowering=False, num_devices=1)
    arrays, args = {}, []
    for name in _INS:
        a = _np.ascontiguousarray(inputs[name])
        arrays[f"in_{name}_dram"] = a
        args.append(nc.dram_tensor(f"in_{name}_dram", a.shape, _mybir.dt.from_np(a.dtype), kind="ExternalInput").ap())
    for i, (shape, dtype) in enumerate(_OUTS):
        dt = _mybir.dt.from_np(_np.dtype(dtype))
        args.append(nc.dram_tensor(f"out_{i}_dram", shape, dt, kind="ExternalOutput").ap())
    adaln_attention_moe_kernel(nc, *args)
    r = _run(nc, [arrays], core_ids=[0])
    got = tuple(r.results[0][f"out_{i}_dram"] for i in range(len(_OUTS)))
    return got[0]
```
